# Optimizing a Trainium2 kernel written in Bass

```python
import numpy as np
import jax
import jax.numpy as jnp

def _softmax(x, axis=-1):
    return jax.nn.softmax(x, axis=axis)

def _gelu(x):
    return jax.nn.gelu(x, approximate=True)

def _silu(x):
    return jax.nn.silu(x)

def _sigmoid(x):
    return jax.nn.sigmoid(x)

def _layernorm(x, axis=-1, eps=1e-05):
    m = jnp.mean(x, axis=axis, keepdims=True)
    v = jnp.var(x, axis=axis, keepdims=True)
    return (x - m) / jnp.sqrt(v + eps)

def _scatter_add(tgt, idx, src, axis=0):
    return tgt.at[idx].add(src)

def _segment_sum(src, seg, n):
    return jax.ops.segment_sum(src, seg, n)
kernel_name = 'mk_decoder_postln_d2_seqx_r8_8f6f4b'

def setup_inputs(seed: int=0):
    np.random.seed(seed)
    _w = jnp.asarray

    def _rec_inputs():
        import jax
        import jax.numpy as jnp
        _rk = jax.random.key(seed)
        x = -0.0002928 + 1 * jax.random.normal(jax.random.fold_in(_rk, 1), (4, 256, 128), jnp.float32)
        _lenS = 256 - jax.random.randint(jax.random.fold_in(_rk, 7), (4,), 0, max(1, 256 // 4) + 1, jnp.int32)
        _lenS2 = 256 - jax.random.randint(jax.random.fold_in(_rk, 8), (4,), 0, max(1, 256 // 4) + 1, jnp.int32)
        _ctx_512P = jax.random.normal(jax.random.fold_in(_rk, 11), (4, 16, 64), jnp.float32)
        _ctx_512c = jax.random.dirichlet(jax.random.fold_in(_rk, 511), 0.3 * jnp.ones((16,), jnp.float32), (4, 256))
        _ctx_512t = jnp.einsum('bsk,bkd->bsd', _ctx_512c, _ctx_512P)
        _ctx_512t = _ctx_512t * jax.lax.rsqrt(jnp.mean(jnp.square(_ctx_512t)) + 1e-12) * 0.953939
        ctx_512 = 0.00222621 + 0.99962 * (_ctx_512t + 0.3 * jax.random.normal(jax.random.fold_in(_rk, 611), (4, 256, 64), jnp.float32))
        return (x, ctx_512)
    x, ctx_512 = _rec_inputs()

    def _L0_attn_setup():
        import jax, jax.numpy as jnp
        import numpy as np
        D_MODEL = 128
        N_HEADS = 16
        HEAD_DIM = D_MODEL // N_HEADS
        BUCKET = 64
        key = jax.random.key(seed)
        k1, k2, k3 = jax.random.split(key, 3)
        B, T = (4, 512)
        x = jax.random.normal(k1, (B, T, D_MODEL), dtype=jnp.float32)
        W_qkv = jax.random.normal(k2, (3 * D_MODEL, D_MODEL), dtype=jnp.float32) * D_MODEL ** (-0.5)
        W_out = jax.random.normal(k3, (D_MODEL, D_MODEL), dtype=jnp.float32) * D_MODEL ** (-0.5)
        return {'x': x, 'W_qkv': W_qkv, 'W_out': W_out}
    _L0_attn_all = _L0_attn_setup()
    _L0_attn_in = {k: v for k, v in _L0_attn_all.items() if k in ('W_qkv', 'W_out')}
    del _L0_attn_all

    def _L0_xattn_setup():
        import jax, jax.numpy as jnp
        import numpy as np
        H, D, C1, C2, S, M, B, W = (16, 32, 128, 64, 256, 64, 2, 4)

        def _ln(x, g, b):
            m = jnp.mean(x, -1, keepdims=True)
            v = jnp.var(x, -1, keepdims=True)
            return (x - m) * jax.lax.rsqrt(v + 1e-05) * g + b

        def _mha(x, y, wq, wk, wv, li1_w, li1_b, lnx_g, lnx_b, lny_g, lny_b, ln3_g, ln3_b, li2_w, li2_b, li3_w, li3_b, causal):
            xn = _ln(x, lnx_g, lnx_b)
            yn = _ln(y, lny_g, lny_b)
            q = jnp.einsum('bsc,hcd->bhsd', xn, wq)
            k = jnp.einsum('btc,hcd->bhtd', yn, wk)
            v = jnp.einsum('btc,hcd->bhtd', yn, wv)
            a = jax.nn.softmax(jnp.einsum('bhsd,bhtd->bhst', q, k) * D ** (-0.5), axis=-1)
            if causal:
                s, t = (a.shape[-2], a.shape[-1])
                mask = (jnp.arange(t)[None, :] > jnp.arange(s)[:, None]).astype(a.dtype)
                a = a * mask
            o = jnp.einsum('bhst,bhtd->bhsd', a, v)
            o = o.transpose(0, 2, 1, 3).reshape(x.shape[0], x.shape[1], H * D)
            x_out = x + o @ li1_w + li1_b
            h = jax.nn.gelu(_ln(x_out, ln3_g, ln3_b) @ li2_w + li2_b, approximate=False)
            return x_out + h @ li3_w + li3_b
        key = jax.random.key(seed)
        ks = iter(jax.random.split(key, 64))

        def w(shape, scale=0.02):
            return jax.random.normal(next(ks), shape, jnp.float32) * scale
        inp = {'xx': jax.random.normal(next(ks), (B, S, C1), jnp.float32), 'ee': jax.random.normal(next(ks), (B, M, C2), jnp.float32), 'ln1_g': jnp.ones(C1, jnp.float32), 'ln1_b': jnp.zeros(C1, jnp.float32), 'ln2_g': jnp.ones(C1, jnp.float32), 'ln2_b': jnp.zeros(C1, jnp.float32)}
        for pfx, cy in (('a1', C1), ('a2', C2)):
            inp[pfx + '_wq'] = w((H, C1, D))
            inp[pfx + '_wk'] = w((H, cy, D))
            inp[pfx + '_wv'] = w((H, cy, D))
            inp[pfx + '_li1_w'] = w((H * D, C1))
            inp[pfx + '_li1_b'] = jnp.zeros(C1, jnp.float32)
            inp[pfx + '_lnx_g'] = jnp.ones(C1, jnp.float32)
            inp[pfx + '_lnx_b'] = jnp.zeros(C1, jnp.float32)
            inp[pfx + '_lny_g'] = jnp.ones(cy, jnp.float32)
            inp[pfx + '_lny_b'] = jnp.zeros(cy, jnp.float32)
            inp[pfx + '_ln3_g'] = jnp.ones(C1, jnp.float32)
            inp[pfx + '_ln3_b'] = jnp.zeros(C1, jnp.float32)
            inp[pfx + '_li2_w'] = w((C1, C1 * W))
            inp[pfx + '_li2_b'] = jnp.zeros(C1 * W, jnp.float32)
            inp[pfx + '_li3_w'] = w((C1 * W, C1))
            inp[pfx + '_li3_b'] = jnp.zeros(C1, jnp.float32)
        inp['training'] = 0
        return inp
    _L0_xattn_all = _L0_xattn_setup()
    _L0_xattn_in = {k: v for k, v in _L0_xattn_all.items() if k in ('ln1_g', 'ln1_b', 'ln2_g', 'ln2_b', 'a1_wq', 'a1_wk', 'a1_wv', 'a1_li1_w', 'a1_li1_b', 'a1_lnx_g', 'a1_lnx_b', 'a1_lny_g', 'a1_lny_b', 'a1_ln3_g', 'a1_ln3_b', 'a1_li2_w', 'a1_li2_b', 'a1_li3_w', 'a1_li3_b', 'a2_wq', 'a2_wk', 'a2_wv', 'a2_li1_w', 'a2_li1_b', 'a2_lnx_g', 'a2_lnx_b', 'a2_lny_g', 'a2_lny_b', 'a2_ln3_g', 'a2_ln3_b', 'a2_li2_w', 'a2_li2_b', 'a2_li3_w', 'a2_li3_b')}
    del _L0_xattn_all

    def _L0_ffn_setup():
        import jax, jax.numpy as jnp
        import numpy as np
        E = 16
        K = 4
        B, S, H, I = (4, 128, 128, 256)
        key = jax.random.key(seed)
        k0, k1, k2, k3 = jax.random.split(key, 4)
        scale = 0.02
        return {'hidden_states': jax.random.normal(k0, (B, S, H), jnp.float32), 'router_w': jax.random.normal(k1, (H, E), jnp.float32) * scale, 'router_b': jnp.zeros((E,), jnp.float32), 'w1': jax.random.normal(k2, (E, H, I), jnp.float32) * scale, 'b1': jnp.zeros((E, I), jnp.float32), 'w2': jax.random.normal(k3, (E, I, H), jnp.float32) * scale, 'b2': jnp.zeros((E, H), jnp.float32)}
    _L0_ffn_all = _L0_ffn_setup()
    _L0_ffn_in = {k: v for k, v in _L0_ffn_all.items() if k in ('router_w', 'router_b', 'w1', 'b1', 'w2', 'b2')}
    del _L0_ffn_all

    def _L1_attn_setup():
        import jax, jax.numpy as jnp
        import numpy as np
        D_MODEL = 128
        NUM_HEADS = 16
        D_HEAD = 64
        N_CTX = 256
        BATCH = 4
        NEG_INF = -10000000000.0
        key = jax.random.key(seed)
        k1, k2, k3, k4, k5 = jax.random.split(key, 5)
        s = 1.0 / np.sqrt(D_MODEL).astype(np.float32)
        x = jax.random.normal(k1, (BATCH, N_CTX, D_MODEL), dtype=jnp.float32)
        W_K = jax.random.normal(k2, (NUM_HEADS, D_HEAD, D_MODEL), dtype=jnp.float32) * s
        W_Q = jax.random.normal(k3, (NUM_HEADS, D_HEAD, D_MODEL), dtype=jnp.float32) * s
        W_V = jax.random.normal(k4, (NUM_HEADS, D_HEAD, D_MODEL), dtype=jnp.float32) * s
        W_O = jax.random.normal(k5, (D_MODEL, NUM_HEADS * D_HEAD), dtype=jnp.float32) * s
        return {'x': x, 'W_K': W_K, 'W_Q': W_Q, 'W_V': W_V, 'W_O': W_O}
    _L1_attn_all = _L1_attn_setup()
    _L1_attn_in = {k: v for k, v in _L1_attn_all.items() if k in ('W_K', 'W_Q', 'W_V', 'W_O')}
    del _L1_attn_all

    def _L1_xattn_setup():
        import jax, jax.numpy as jnp
        import numpy as np
        HEADS = 16
        D_MODEL = 128
        IMG_MODEL = 64
        D_K = D_MODEL // HEADS
        key = jax.random.key(seed)
        ks = jax.random.split(key, 12)
        B, LQ, LKV = (8, 256, 128)
        s_dm = 1.0 / np.sqrt(D_MODEL)
        s_im = 1.0 / np.sqrt(IMG_MODEL)
        return {'q': jax.random.normal(ks[0], (B, LQ, D_MODEL), jnp.float32), 'k': jax.random.normal(ks[1], (B, LKV, IMG_MODEL), jnp.float32), 'v': jax.random.normal(ks[2], (B, LKV, IMG_MODEL), jnp.float32), 'Wq': jax.random.normal(ks[3], (D_MODEL, D_MODEL), jnp.float32) * s_dm, 'bq': jnp.zeros((D_MODEL,), jnp.float32), 'Wk': jax.random.normal(ks[4], (IMG_MODEL, D_MODEL), jnp.float32) * s_im, 'bk': jnp.zeros((D_MODEL,), jnp.float32), 'Wv': jax.random.normal(ks[5], (IMG_MODEL, D_MODEL), jnp.float32) * s_im, 'bv': jnp.zeros((D_MODEL,), jnp.float32), 'Wo': jax.random.normal(ks[6], (D_MODEL, D_MODEL), jnp.float32) * s_dm, 'bo': jnp.zeros((D_MODEL,), jnp.float32)}
    _L1_xattn_all = _L1_xattn_setup()
    _L1_xattn_in = {k: v for k, v in _L1_xattn_all.items() if k in ('Wq', 'bq', 'Wk', 'bk', 'Wv', 'bv', 'Wo', 'bo')}
    del _L1_xattn_all

    def _L1_ffn_setup():
        import jax, jax.numpy as jnp
        import numpy as np
        K = 2
        CAP_FACTOR = 1.25
        key = jax.random.key(seed)
        ks = jax.random.split(key, 6)
        B, T, C, H, E = (8, 256, 128, 512, 8)
        return {'x': jax.random.normal(ks[0], (B, T, C), dtype=jnp.float32), 'Wr': jax.random.normal(ks[1], (C, E), dtype=jnp.float32) * 0.02, 'W1': jax.random.normal(ks[2], (E, C, H), dtype=jnp.float32) * 0.02, 'b1': jax.random.normal(ks[3], (E, H), dtype=jnp.float32) * 0.02, 'W2': jax.random.normal(ks[4], (E, H, C), dtype=jnp.float32) * 0.02, 'b2': jax.random.normal(ks[5], (E, C), dtype=jnp.float32) * 0.02}
    _L1_ffn_all = _L1_ffn_setup()
    _L1_ffn_in = {k: v for k, v in _L1_ffn_all.items() if k in ('Wr', 'W1', 'b1', 'W2', 'b2')}
    del _L1_ffn_all
    return {'x': x, 'ctx_512': ctx_512, 'L0_attn_W_qkv': _L0_attn_in['W_qkv'], 'L0_attn_W_out': _L0_attn_in['W_out'], 'L0_xattn_ln1_g': _L0_xattn_in['ln1_g'], 'L0_xattn_ln1_b': _L0_xattn_in['ln1_b'], 'L0_xattn_ln2_g': _L0_xattn_in['ln2_g'], 'L0_xattn_ln2_b': _L0_xattn_in['ln2_b'], 'L0_xattn_a1_wq': _L0_xattn_in['a1_wq'], 'L0_xattn_a1_wk': _L0_xattn_in['a1_wk'], 'L0_xattn_a1_wv': _L0_xattn_in['a1_wv'], 'L0_xattn_a1_li1_w': _L0_xattn_in['a1_li1_w'], 'L0_xattn_a1_li1_b': _L0_xattn_in['a1_li1_b'], 'L0_xattn_a1_lnx_g': _L0_xattn_in['a1_lnx_g'], 'L0_xattn_a1_lnx_b': _L0_xattn_in['a1_lnx_b'], 'L0_xattn_a1_lny_g': _L0_xattn_in['a1_lny_g'], 'L0_xattn_a1_lny_b': _L0_xattn_in['a1_lny_b'], 'L0_xattn_a1_ln3_g': _L0_xattn_in['a1_ln3_g'], 'L0_xattn_a1_ln3_b': _L0_xattn_in['a1_ln3_b'], 'L0_xattn_a1_li2_w': _L0_xattn_in['a1_li2_w'], 'L0_xattn_a1_li2_b': _L0_xattn_in['a1_li2_b'], 'L0_xattn_a1_li3_w': _L0_xattn_in['a1_li3_w'], 'L0_xattn_a1_li3_b': _L0_xattn_in['a1_li3_b'], 'L0_xattn_a2_wq': _L0_xattn_in['a2_wq'], 'L0_xattn_a2_wk': _L0_xattn_in['a2_wk'], 'L0_xattn_a2_wv': _L0_xattn_in['a2_wv'], 'L0_xattn_a2_li1_w': _L0_xattn_in['a2_li1_w'], 'L0_xattn_a2_li1_b': _L0_xattn_in['a2_li1_b'], 'L0_xattn_a2_lnx_g': _L0_xattn_in['a2_lnx_g'], 'L0_xattn_a2_lnx_b': _L0_xattn_in['a2_lnx_b'], 'L0_xattn_a2_lny_g': _L0_xattn_in['a2_lny_g'], 'L0_xattn_a2_lny_b': _L0_xattn_in['a2_lny_b'], 'L0_xattn_a2_ln3_g': _L0_xattn_in['a2_ln3_g'], 'L0_xattn_a2_ln3_b': _L0_xattn_in['a2_ln3_b'], 'L0_xattn_a2_li2_w': _L0_xattn_in['a2_li2_w'], 'L0_xattn_a2_li2_b': _L0_xattn_in['a2_li2_b'], 'L0_xattn_a2_li3_w': _L0_xattn_in['a2_li3_w'], 'L0_xattn_a2_li3_b': _L0_xattn_in['a2_li3_b'], 'L0_ffn_router_w': _L0_ffn_in['router_w'], 'L0_ffn_router_b': _L0_ffn_in['router_b'], 'L0_ffn_w1': _L0_ffn_in['w1'], 'L0_ffn_b1': _L0_ffn_in['b1'], 'L0_ffn_w2': _L0_ffn_in['w2'], 'L0_ffn_b2': _L0_ffn_in['b2'], 'L1_attn_W_K': _L1_attn_in['W_K'], 'L1_attn_W_Q': _L1_attn_in['W_Q'], 'L1_attn_W_V': _L1_attn_in['W_V'], 'L1_attn_W_O': _L1_attn_in['W_O'], 'L1_xattn_Wq': _L1_xattn_in['Wq'], 'L1_xattn_bq': _L1_xattn_in['bq'], 'L1_xattn_Wk': _L1_xattn_in['Wk'], 'L1_xattn_bk': _L1_xattn_in['bk'], 'L1_xattn_Wv': _L1_xattn_in['Wv'], 'L1_xattn_bv': _L1_xattn_in['bv'], 'L1_xattn_Wo': _L1_xattn_in['Wo'], 'L1_xattn_bo': _L1_xattn_in['bo'], 'L1_ffn_Wr': _L1_ffn_in['Wr'], 'L1_ffn_W1': _L1_ffn_in['W1'], 'L1_ffn_b1': _L1_ffn_in['b1'], 'L1_ffn_W2': _L1_ffn_in['W2'], 'L1_ffn_b2': _L1_ffn_in['b2']}

def reference(x, ctx_512, L0_attn_W_qkv, L0_attn_W_out, L0_xattn_ln1_g, L0_xattn_ln1_b, L0_xattn_ln2_g, L0_xattn_ln2_b, L0_xattn_a1_wq, L0_xattn_a1_wk, L0_xattn_a1_wv, L0_xattn_a1_li1_w, L0_xattn_a1_li1_b, L0_xattn_a1_lnx_g, L0_xattn_a1_lnx_b, L0_xattn_a1_lny_g, L0_xattn_a1_lny_b, L0_xattn_a1_ln3_g, L0_xattn_a1_ln3_b, L0_xattn_a1_li2_w, L0_xattn_a1_li2_b, L0_xattn_a1_li3_w, L0_xattn_a1_li3_b, L0_xattn_a2_wq, L0_xattn_a2_wk, L0_xattn_a2_wv, L0_xattn_a2_li1_w, L0_xattn_a2_li1_b, L0_xattn_a2_lnx_g, L0_xattn_a2_lnx_b, L0_xattn_a2_lny_g, L0_xattn_a2_lny_b, L0_xattn_a2_ln3_g, L0_xattn_a2_ln3_b, L0_xattn_a2_li2_w, L0_xattn_a2_li2_b, L0_xattn_a2_li3_w, L0_xattn_a2_li3_b, L0_ffn_router_w, L0_ffn_router_b, L0_ffn_w1, L0_ffn_b1, L0_ffn_w2, L0_ffn_b2, L1_attn_W_K, L1_attn_W_Q, L1_attn_W_V, L1_attn_W_O, L1_xattn_Wq, L1_xattn_bq, L1_xattn_Wk, L1_xattn_bk, L1_xattn_Wv, L1_xattn_bv, L1_xattn_Wo, L1_xattn_bo, L1_ffn_Wr, L1_ffn_W1, L1_ffn_b1, L1_ffn_W2, L1_ffn_b2):
    import jax
    import jax.numpy as jnp

    def _L0_attn_ref(x, W_qkv, W_out):
        import jax, jax.numpy as jnp
        import numpy as np
        D_MODEL = 128
        N_HEADS = 16
        HEAD_DIM = D_MODEL // N_HEADS
        BUCKET = 64
        B, T, _ = x.shape
        qkv = x @ W_qkv.T
        qkv = qkv.reshape(B, T, 3 * N_HEADS, HEAD_DIM).transpose(0, 2, 1, 3)
        q, k, v = jnp.split(qkv, 3, axis=1)
        q = jax.nn.softmax(q, axis=-1) * HEAD_DIM ** (-0.5)
        k = jnp.exp(k)
        n = T // BUCKET
        bucket = lambda t: t.reshape(B, N_HEADS, n, BUCKET, HEAD_DIM)
        b_q, b_k, b_v = (bucket(q), bucket(k), bucket(v))
        b_k_sum = jnp.sum(b_k, axis=-2)
        b_k_cumsum = jnp.cumsum(b_k_sum, axis=-2)
        b_k_cumsum = jnp.pad(b_k_cumsum, ((0, 0), (0, 0), (1, 0), (0, 0)))[:, :, :-1]
        context = jnp.einsum('bhnsd,bhnse->bhnde', b_k, b_v)
        context = jnp.cumsum(context, axis=-3)
        context = jnp.pad(context, ((0, 0), (0, 0), (1, 0), (0, 0), (0, 0)))[:, :, :-1]
        den = jnp.einsum('bhnsd,bhnd->bhns', b_q, b_k_cumsum)
        D_inv = 1.0 / jnp.maximum(den, 1e-06)
        attn = jnp.einsum('bhnsd,bhnde,bhns->bhnse', b_q, context, D_inv)
        xo = attn.reshape(B, N_HEADS, T, HEAD_DIM)
        xo = xo.transpose(0, 2, 1, 3).reshape(B, T, D_MODEL)
        return xo @ W_out.T

    def _L0_xattn_ref(xx, ee, ln1_g, ln1_b, ln2_g, ln2_b, a1_wq, a1_wk, a1_wv, a1_li1_w, a1_li1_b, a1_lnx_g, a1_lnx_b, a1_lny_g, a1_lny_b, a1_ln3_g, a1_ln3_b, a1_li2_w, a1_li2_b, a1_li3_w, a1_li3_b, a2_wq, a2_wk, a2_wv, a2_li1_w, a2_li1_b, a2_lnx_g, a2_lnx_b, a2_lny_g, a2_lny_b, a2_ln3_g, a2_ln3_b, a2_li2_w, a2_li2_b, a2_li3_w, a2_li3_b, training):
        import jax, jax.numpy as jnp
        import numpy as np
        H, D, C1, C2, S, M, B, W = (16, 32, 128, 64, 256, 64, 2, 4)

        def _ln(x, g, b):
            m = jnp.mean(x, -1, keepdims=True)
            v = jnp.var(x, -1, keepdims=True)
            return (x - m) * jax.lax.rsqrt(v + 1e-05) * g + b

        def _mha(x, y, wq, wk, wv, li1_w, li1_b, lnx_g, lnx_b, lny_g, lny_b, ln3_g, ln3_b, li2_w, li2_b, li3_w, li3_b, causal):
            xn = _ln(x, lnx_g, lnx_b)
            yn = _ln(y, lny_g, lny_b)
            q = jnp.einsum('bsc,hcd->bhsd', xn, wq)
            k = jnp.einsum('btc,hcd->bhtd', yn, wk)
            v = jnp.einsum('btc,hcd->bhtd', yn, wv)
            a = jax.nn.softmax(jnp.einsum('bhsd,bhtd->bhst', q, k) * D ** (-0.5), axis=-1)
            if causal:
                s, t = (a.shape[-2], a.shape[-1])
                mask = (jnp.arange(t)[None, :] > jnp.arange(s)[:, None]).astype(a.dtype)
                a = a * mask
            o = jnp.einsum('bhst,bhtd->bhsd', a, v)
            o = o.transpose(0, 2, 1, 3).reshape(x.shape[0], x.shape[1], H * D)
            x_out = x + o @ li1_w + li1_b
            h = jax.nn.gelu(_ln(x_out, ln3_g, ln3_b) @ li2_w + li2_b, approximate=False)
            return x_out + h @ li3_w + li3_b
        x = _ln(xx, ln1_g, ln1_b)
        x = x + _mha(x, x, a1_wq, a1_wk, a1_wv, a1_li1_w, a1_li1_b, a1_lnx_g, a1_lnx_b, a1_lny_g, a1_lny_b, a1_ln3_g, a1_ln3_b, a1_li2_w, a1_li2_b, a1_li3_w, a1_li3_b, causal=True)
        x = _ln(x, ln2_g, ln2_b)
        return x + _mha(x, ee, a2_wq, a2_wk, a2_wv, a2_li1_w, a2_li1_b, a2_lnx_g, a2_lnx_b, a2_lny_g, a2_lny_b, a2_ln3_g, a2_ln3_b, a2_li2_w, a2_li2_b, a2_li3_w, a2_li3_b, causal=False)

    def _L0_ffn_ref(hidden_states, router_w, router_b, w1, b1, w2, b2):
        import jax, jax.numpy as jnp
        import numpy as np
        E = 16
        K = 4
        B, S, H, I = (4, 128, 128, 256)
        b, s, h = hidden_states.shape
        logits = hidden_states @ router_w + router_b
        probs = jax.nn.softmax(logits, axis=-1)
        topw, topi = jax.lax.top_k(probs, K)
        topw = topw / jnp.sum(topw, axis=-1, keepdims=True)
        combine = jnp.sum(jax.nn.one_hot(topi, E, dtype=hidden_states.dtype) * topw[..., None], axis=2)
        x = hidden_states.reshape(b * s, h)
        c = combine.reshape(b * s, E)

        def body(acc, expert):
            w1e, b1e, w2e, b2e, ce = expert
            hmid = jax.nn.gelu(x @ w1e + b1e, approximate=False)
            return (acc + (hmid @ w2e + b2e) * ce[:, None], None)
        out, _ = jax.lax.scan(body, jnp.zeros_like(x), (w1, b1, w2, b2, c.T))
        return out.reshape(b, s, h)

    def _L1_attn_ref(x, W_K, W_Q, W_V, W_O):
        import jax, jax.numpy as jnp
        import numpy as np
        D_MODEL = 128
        NUM_HEADS = 16
        D_HEAD = 64
        N_CTX = 256
        BATCH = 4
        NEG_INF = -10000000000.0
        b, q_len, d_model = x.shape
        d_head = W_K.shape[1]
        K = jnp.einsum('bpd,ihd->biph', x, W_K)
        Q = jnp.einsum('bpd,ihd->biph', x, W_Q)
        V = jnp.einsum('bpd,ihd->biph', x, W_V)
        scores = jnp.einsum('biph,biqh->biqp', K, Q)
        mask = jnp.tril(jnp.ones((q_len, q_len), dtype=bool))
        scores = jnp.where(mask[None, None, :, :], scores, NEG_INF)
        attn = jax.nn.softmax(scores / np.sqrt(d_head).astype(np.float32), axis=-1)
        z = jnp.einsum('biph,biqp->biqh', V, attn)
        z_flat = jnp.transpose(z, (0, 2, 1, 3)).reshape(b, q_len, -1)
        out = jnp.einsum('bqf,df->bqd', z_flat, W_O)
        return out

    def _L1_xattn_ref(q, k, v, Wq, bq, Wk, bk, Wv, bv, Wo, bo):
        import jax, jax.numpy as jnp
        import numpy as np
        HEADS = 16
        D_MODEL = 128
        IMG_MODEL = 64
        D_K = D_MODEL // HEADS
        B, LQ, _ = q.shape
        LKV = k.shape[1]
        qh = (q @ Wq + bq).reshape(B, LQ, HEADS, D_K).transpose(0, 2, 1, 3)
        kh = (k @ Wk + bk).reshape(B, LKV, HEADS, D_K).transpose(0, 2, 1, 3)
        vh = (v @ Wv + bv).reshape(B, LKV, HEADS, D_K).transpose(0, 2, 1, 3)
        scale = 1.0 / np.sqrt(D_K)
        scores = jnp.einsum('bhqd,bhkd->bhqk', qh, kh) * scale
        attn = jax.nn.softmax(scores, axis=-1)
        out = jnp.einsum('bhqk,bhkd->bhqd', attn, vh)
        concat = out.transpose(0, 2, 1, 3).reshape(B, LQ, D_MODEL)
        return concat @ Wo + bo

    def _L1_ffn_ref(x, Wr, W1, b1, W2, b2):
        import jax, jax.numpy as jnp
        import numpy as np
        K = 2
        CAP_FACTOR = 1.25
        B, T, C = x.shape
        E = Wr.shape[1]
        capacity = int(T / E * CAP_FACTOR)
        probs = jax.nn.softmax(x @ Wr, axis=-1)
        topk_probs, topk_experts = jax.lax.top_k(probs, K)
        S = T * K
        e_flat = topk_experts.reshape(B, S)
        p_flat = topk_probs.reshape(B, S)
        x_rep = jnp.repeat(x, K, axis=1)
        onehot = jax.nn.one_hot(e_flat, E, dtype=jnp.int32)
        pos_all = jnp.cumsum(onehot, axis=1) - onehot
        pos = jnp.take_along_axis(pos_all, e_flat[..., None], axis=-1)[..., 0]
        keep = pos < capacity
        pos_c = jnp.minimum(pos, capacity - 1)
        b_idx = jnp.broadcast_to(jnp.arange(B)[:, None], (B, S))
        buf = jnp.zeros((E, B, capacity, C), dtype=x.dtype)
        buf = buf.at[e_flat, b_idx, pos_c].add(x_rep * keep[..., None].astype(x.dtype))
        h = jax.nn.relu(jnp.einsum('ebnc,ech->ebnh', buf, W1) + b1[:, None, None, :])
        y = jnp.einsum('ebnh,ehc->ebnc', h, W2) + b2[:, None, None, :]
        y_tok = y[e_flat, b_idx, pos_c]
        y_tok = y_tok * keep[..., None].astype(x.dtype) * p_flat[..., None]
        out = y_tok.reshape(B, T, K, C).sum(axis=2)
        return out
    x = _layernorm(x + _L0_attn_ref(x, L0_attn_W_qkv, L0_attn_W_out), axis=-1)
    x = _layernorm(x + _L0_xattn_ref(x, ctx_512, L0_xattn_ln1_g, L0_xattn_ln1_b, L0_xattn_ln2_g, L0_xattn_ln2_b, L0_xattn_a1_wq, L0_xattn_a1_wk, L0_xattn_a1_wv, L0_xattn_a1_li1_w, L0_xattn_a1_li1_b, L0_xattn_a1_lnx_g, L0_xattn_a1_lnx_b, L0_xattn_a1_lny_g, L0_xattn_a1_lny_b, L0_xattn_a1_ln3_g, L0_xattn_a1_ln3_b, L0_xattn_a1_li2_w, L0_xattn_a1_li2_b, L0_xattn_a1_li3_w, L0_xattn_a1_li3_b, L0_xattn_a2_wq, L0_xattn_a2_wk, L0_xattn_a2_wv, L0_xattn_a2_li1_w, L0_xattn_a2_li1_b, L0_xattn_a2_lnx_g, L0_xattn_a2_lnx_b, L0_xattn_a2_lny_g, L0_xattn_a2_lny_b, L0_xattn_a2_ln3_g, L0_xattn_a2_ln3_b, L0_xattn_a2_li2_w, L0_xattn_a2_li2_b, L0_xattn_a2_li3_w, L0_xattn_a2_li3_b, 0), axis=-1)
    x = _layernorm(x + _L0_ffn_ref(x, L0_ffn_router_w, L0_ffn_router_b, L0_ffn_w1, L0_ffn_b1, L0_ffn_w2, L0_ffn_b2), axis=-1)
    x = _layernorm(x + _L1_attn_ref(x, L1_attn_W_K, L1_attn_W_Q, L1_attn_W_V, L1_attn_W_O), axis=-1)
    x = _layernorm(x + _L1_xattn_ref(x, ctx_512, ctx_512, L1_xattn_Wq, L1_xattn_bq, L1_xattn_Wk, L1_xattn_bk, L1_xattn_Wv, L1_xattn_bv, L1_xattn_Wo, L1_xattn_bo), axis=-1)
    x = _layernorm(x + _L1_ffn_ref(x, L1_ffn_Wr, L1_ffn_W1, L1_ffn_b1, L1_ffn_W2, L1_ffn_b2), axis=-1)
    return x

_drawn_inputs = setup_inputs


def setup_inputs(seed=0):
    import zlib

    import numpy as np

    out = dict(_drawn_inputs(seed))
    spreads = {'L0_xattn_ln1_g': (1.0, 0.2),
     'L0_xattn_ln1_b': (0.0, 0.1),
     'L0_xattn_ln2_g': (1.0, 0.2),
     'L0_xattn_ln2_b': (0.0, 0.1),
     'L0_xattn_a1_li1_b': (0.0, 0.1),
     'L0_xattn_a1_lnx_g': (1.0, 0.6),
     'L0_xattn_a1_lnx_b': (0.0, 0.8),
     'L0_xattn_a1_lny_g': (1.0, 0.6),
     'L0_xattn_a1_lny_b': (0.0, 0.8),
     'L0_xattn_a1_ln3_g': (1.0, 0.6),
     'L0_xattn_a1_ln3_b': (0.0, 0.8),
     'L0_xattn_a1_li2_b': (0.0, 0.405),
     'L0_xattn_a1_li3_b': (0.0, 0.1),
     'L0_xattn_a2_li1_b': (0.0, 0.1),
     'L0_xattn_a2_lnx_g': (1.0, 0.6),
     'L0_xattn_a2_lnx_b': (0.0, 0.8),
     'L0_xattn_a2_lny_g': (1.0, 0.6),
     'L0_xattn_a2_lny_b': (0.0, 0.8),
     'L0_xattn_a2_ln3_g': (1.0, 0.6),
     'L0_xattn_a2_ln3_b': (0.0, 0.8),
     'L0_xattn_a2_li2_b': (0.0, 0.42),
     'L0_xattn_a2_li3_b': (0.0, 0.1),
     'L0_ffn_router_b': (0.0, 0.1),
     'L0_ffn_b1': (0.0, 0.665),
     'L0_ffn_b2': (0.0, 0.1),
     'L1_xattn_bq': (0.0, 0.407),
     'L1_xattn_bk': (0.0, 0.8),
     'L1_xattn_bv': (0.0, 0.1),
     'L1_xattn_bo': (0.0, 0.1)}
    factors = {'L0_xattn_a1_wq': 8.0,
     'L0_xattn_a1_wk': 8.0,
     'L0_xattn_a1_wv': 4.599,
     'L0_xattn_a1_li1_w': 5.063,
     'L0_xattn_a1_li2_w': 2.855,
     'L0_xattn_a2_wq': 8.0,
     'L0_xattn_a2_wk': 8.0,
     'L0_xattn_a2_li2_w': 2.717,
     'L0_ffn_w1': 2.929,
     'L1_ffn_Wr': 5.134,
     'L1_ffn_W1': 5.878,
     'L1_ffn_b1': 8.0,
     'L1_ffn_W2': 4.875,
     'L1_ffn_b2': 8.0}
    for name, (base, spread) in spreads.items():
        noise = np.random.default_rng([zlib.crc32(name.encode()), seed]).standard_normal(out[name].shape)
        drawn = base * np.exp(spread * noise) if base else spread * noise
        out[name] = jnp.asarray(drawn.astype(out[name].dtype))
    for name, factor in factors.items():
        out[name] = (out[name] * factor).astype(out[name].dtype)
    return out
```

```python
import concourse.bass as bass
from concourse import mybir
from contextlib import ExitStack

import numpy as np

fp32 = mybir.dt.float32
bf16 = mybir.dt.bfloat16
u32 = mybir.dt.uint32
ALU = mybir.AluOpType
ACT = mybir.ActivationFunctionType
AX = mybir.AxisListType

P = 128
BATCHES, T, C, CC = 4, 256, 128, 64
TT = T // P
PAIR = 2
HEADS = 16
EPS = 1e-5
BUCKET = 64
HD0 = C // HEADS
E0, K0, I0 = 16, 4, 256
E1, I1 = 8, 512
CAP = int(T / E1 * 1.25)
SLOT = 64

ROWS = {}
for _n, _w in [("ln1_g", C), ("ln1_b", C), ("ln2_g", C), ("ln2_b", C), ("a1_li1_b", C), ("a1_li3_b", C),
               ("a2_li1_b", C), ("a2_li3_b", C), ("bo", C), ("router_b", E0), ("bv", HEADS * 32)]:
    ROWS[_n] = (sum(w for _, w in ROWS.values()), _w)
NROWS = sum(w for _, w in ROWS.values())
COLS = {}
for _n, _w in [("a1_lnx_g", 1), ("a1_lnx_b", 1), ("a1_lny_g", 1), ("a1_lny_b", 1), ("a1_ln3_g", 1), ("a1_ln3_b", 1),
               ("a1_li2_b", 4), ("a2_lnx_g", 1), ("a2_lnx_b", 1), ("a2_lny_g", 1), ("a2_lny_b", 1), ("a2_ln3_g", 1),
               ("a2_ln3_b", 1), ("a2_li2_b", 4), ("ffn0_b1", 2 * E0), ("ffn1_b1", 4 * E1), ("bq", 4), ("bk", 4)]:
    COLS[_n] = (sum(w for _, w in COLS.values()), _w)
NCOLS = sum(w for _, w in COLS.values())
CONSTS = {}
for _n, _w in [("ident", P), ("same_head", P), ("head_of", HEADS), ("later_key", 3 * P), ("earlier", P),
               ("masked", P), ("iota_e", E0), ("iota_slot", SLOT), ("minus_half", TT)]:
    CONSTS[_n] = (sum(w for _, w in CONSTS.values()), _w)
NCONSTS = sum(w for _, w in CONSTS.values())


def shape_constants():
    p, f = np.arange(P)[:, None], np.arange(P)[None, :]
    later = (p > f)
    parts = {
        "ident": p == f, "same_head": p // HD0 == f // HD0,
        "head_of": p // HD0 == np.arange(HEADS)[None, :],
        "later_key": np.concatenate([later, np.ones((P, P)), later], 1),
        "earlier": p < f,
        "masked": np.where(f > p, -1e10, 0.0),
        "iota_e": np.broadcast_to(np.arange(E0), (P, E0)),
        "iota_slot": np.broadcast_to(np.where(np.arange(SLOT) < CAP, np.arange(SLOT) + 1, -5), (P, SLOT)),
        "minus_half": np.full((P, TT), -0.5),
    }
    return np.concatenate([np.asarray(parts[n], np.float32) for n in CONSTS], 1)


WEIGHTS = {
    "qkv": (C, 3 * C), "wout": (C, C),
    "a1_wq": (C, 512), "a1_wk": (C, 512), "a1_wv": (C, 512), "a1_li1": (P, 512), "a1_li2": (C, 512), "a1_li3": (P, 512),
    "ctx_wk": (2 * CC, 512), "ctx_wv": (2 * CC, 512), "a2_wq": (C, 512), "a2_li1": (P, 512), "a2_li2": (C, 512), "a2_li3": (P, 512),
    "router": (C, E0), "ffn0_b2": (E0, C), "ffn0_w1": (C, E0 * I0), "ffn0_w2": (P, 2 * E0 * C),
    "l1_wq": (C, 1024), "l1_wk": (C, 1024), "l1_wv": (C, 1024), "l1_wo": (P, 1024),
    "lx_wq": (C, 512), "lx_wo": (P, 512),
    "router1": (C, E1), "ffn1_b2": (P, 4 * C), "ffn1_w1": (C, E1 * I1), "ffn1_w2": (P, 4 * E1 * C),
}

ATTENTIONS = [
    dict(name="a1", d=32, scale=32 ** -0.5, kind="keep_later", wq="a1_wq", wk="a1_wk", wv="a1_wv", wo="a1_li1"),
    dict(name="a2", d=32, scale=32 ** -0.5, kind="full", wq="a2_wq", wk="ctx_wk", wv="ctx_wv", wo="a2_li1"),
    dict(name="l1", d=64, scale=1 / 8, kind="causal", wq="l1_wq", wk="l1_wk", wv="l1_wv", wo="l1_wo"),
    dict(name="lx", d=32, scale=8 ** -0.5, kind="full", wq="lx_wq", wk="ctx_wk", wv="ctx_wv", wo="lx_wo"),
]
BLOCKS = {
    "full": [(0, 0), (0, 1), (1, 0), (1, 1)],
    "causal": [(0, 0), (0, 1), (1, 1)],
    "keep_later": [(0, 0), (1, 0), (1, 1)],
}
PARTS = {
    "full": [(True, 0, 0, 0, T), (False, 1, T, 0, T)],
    "causal": [(True, 0, 0, 0, T), (False, 1, T, P, P)],
    "keep_later": [(True, 1, P, 0, T), (False, 0, 0, 0, P)],
}
HALVES = HEADS // 2
STEPS = PAIR * HALVES


def decoder(nc, A, out):
    ctx = ExitStack()
    with ctx:
        def sb(name, shape, dt=fp32):
            return ctx.enter_context(nc.sbuf_tensor(name, shape, dt))

        W = {n: sb("w_" + n, [p, w]) for n, (p, w) in WEIGHTS.items()}
        rows, cols, consts = sb("rows", [P, NROWS]), sb("cols", [P, NCOLS]), sb("consts", [P, NCONSTS])

        def row(n):
            return rows[:, ROWS[n][0]:ROWS[n][0] + ROWS[n][1]]

        def col(n, k=0, p=P):
            return cols[0:p, COLS[n][0] + k:COLS[n][0] + k + 1]

        def const(n):
            return consts[:, CONSTS[n][0]:CONSTS[n][0] + CONSTS[n][1]]

        ident = const("ident")
        ident16, masked16 = sb("ident16", [P, P], bf16), sb("masked16", [P, P], bf16)

        def per_batch(name, shape):
            return [sb(f"{name}{b}", shape) for b in range(PAIR)]

        X, R, Z, U, BIASED = (per_batch(n, [P, TT, C]) for n in ("X", "R", "Z", "U", "BIASED"))
        XN, YN = (per_batch(n, [P, T]) for n in ("XN", "YN"))
        CTX, CTXT = per_batch("CTX", [P, TT, CC]), per_batch("CTXT", [P, T])
        stats, moments = sb("stats", [P, TT, 6]), sb("moments", [P, TT, 2])
        variance, rstd = sb("variance", [P, TT]), sb("rstd", [P, TT])

        QB, KB, OB = (sb(n, [P, 8, T]) for n in ("QB", "KB", "OB"))
        VB = per_batch("VB", [P, TT, 1024])
        PB, PT = sb("PB", [P, 3, 4, T]), sb("PT", [P, 3, 2, TT * T])
        negmax, sums, inverse = (sb(n, [P, 4, 4]) for n in ("negmax", "sums", "inverse"))

        vb = [VB[b][:, :, :].rearrange("p t n -> p (t n)") for b in range(PAIR)]

        def carve(flat, at, *shape):
            size = int(np.prod(shape))
            v = flat[:, at:at + size]
            if len(shape) == 2:
                v = v.rearrange("p (a b) -> p a b", b=shape[1])
            if len(shape) == 3:
                v = v.rearrange("p (a b c) -> p a b c", b=shape[1], c=shape[2])
            return v

        QS = [carve(vb[b], 0, TT, C) for b in range(PAIR)]
        QN = [carve(vb[b], 256, TT, C) for b in range(PAIR)]
        K0B = [carve(vb[b], 512, TT, C) for b in range(PAIR)]
        V0B = [carve(vb[b], 768, TT, C + 1) for b in range(PAIR)]
        CM = [carve(vb[b], 1040, 3, C + HEADS) for b in range(PAIR)]
        QT = [carve(vb[b], 1500, T) for b in range(PAIR)]
        OT = [carve(vb[b], 1760, T) for b in range(PAIR)]
        small0 = per_batch("small", [P, 200])
        HB = [QB[:, 4 * b:4 * b + 4, :] for b in range(PAIR)]
        HE = [KB[:, 2 * k:2 * k + 2, :] for k in range(4)]
        PM = [carve(vb[b], 0, TT, E1, SLOT) for b in range(PAIR)]
        PW = [carve(vb[b], 1024, TT, E1, SLOT) for b in range(PAIR)]
        qb, kb, ob = (x[:, :, :].rearrange("p a b -> p (a b)") for x in (QB, KB, OB))
        PWT = [carve(qb, 1024 * b, 4, T) for b in range(PAIR)]
        HX = [carve(kb, 512 * k, 8, SLOT) for k in range(4)]
        BUF = [carve(ob, 512 * b, E1 * SLOT) for b in range(PAIR)]
        YB = [carve(ob, 1024 + 512 * b, 4, C) for b in range(PAIR)]

        scratch = [ob[:, 1024 * b:1024 * b + 1024] for b in range(PAIR)]
        shifted0 = [carve(scratch[b], 0, TT, E0) for b in range(PAIR)]
        expd0 = [carve(scratch[b], 32, TT, E0) for b in range(PAIR)]
        combine0 = [carve(scratch[b], 64, TT, E0) for b in range(PAIR)]
        onehot0 = [scratch[b][:, 96:96 + TT * K0 * E0].rearrange("p (t k e) -> p t k e", k=K0, e=E0) for b in range(PAIR)]
        combT = [carve(scratch[b], 256, T) for b in range(PAIR)]
        shifted1, expd1, chosen1 = ([carve(small0[b][:, :], at, TT, E1) for b in range(PAIR)] for at in (0, 16, 32))
        onehot1 = [small0[b][:, 48:80].rearrange("p (t k e) -> p t k e", k=2, e=E1) for b in range(PAIR)]
        top8 = [carve(small0[b][:, :], 128, TT, 8) for b in range(PAIR)]
        one, two = ([small0[b][:, at:at + TT] for b in range(PAIR)] for at in (160, 162))
        index8 = [sb(f"index8_{b}", [P, TT, 8], u32) for b in range(PAIR)]

        SC = [ctx.enter_context(nc.psum_tensor(f"SC{k}", [P, 2, TT, T], fp32)) for k in range(2)]
        G = [ctx.enter_context(nc.psum_tensor(f"G{k}", [P, 512], fp32)) for k in range(4)]

        weights_in = {n: ctx.enter_context(nc.semaphore("in_" + n)) for n in WEIGHTS}
        consts_in = ctx.enter_context(nc.semaphore("consts_in"))
        masks_made = ctx.enter_context(nc.semaphore("masks_made"))
        tables_in = ctx.enter_context(nc.semaphore("tables_in"))

        per_pass = []

        def sem(name):
            per_pass.append(ctx.enter_context(nc.semaphore(name)))
            return per_pass[-1]

        x_in = [sem(f"x_in{b}") for b in range(PAIR)]
        out_stored = sem("out_stored")
        bank_filled = [sem(f"bank_filled{k}") for k in range(4)]
        bank_emptied = [sem(f"bank_emptied{k}") for k in range(4)]
        dve_chain = sem("dve_chain")
        pool_chain = sem("pool_chain")
        variance_ready, rstd_ready = sem("variance_ready"), sem("rstd_ready")
        z_ready = sem("z_ready")
        u_ready = sem("u_ready")
        bias_ready = sem("bias_ready")
        kv_drawn, q_exp, q_normal = sem("kv_drawn"), sem("q_exp"), sem("q_normal")
        scores_ready, max_ready, exp_ready = sem("scores_ready"), sem("max_ready"), sem("exp_ready")
        inverse_ready, probs_ready = sem("inverse_ready"), sem("probs_ready")
        logits_shifted, logits_exp = sem("logits_shifted"), sem("logits_exp")
        chosen_ready, dispatch_ready = sem("chosen_ready"), sem("dispatch_ready")
        hidden_ready = sem("hidden_ready")
        zeroed = sem("zeroed")
        final_ready = sem("final_ready")

        tile_number = {}

        def fill(pe, key):
            n = tile_number[key] = len(tile_number)
            if n >= 4:
                pe.wait_ge(bank_emptied[n % 4], n // 4)
            return G[n % 4]

        def filled(key):
            return bank_filled[tile_number[key] % 4], 1

        def wait_filled(eng, key):
            n = tile_number[key]
            eng.wait_ge(bank_filled[n % 4], n // 4 + 1)
            return G[n % 4]

        def emptied(key):
            return bank_emptied[tile_number[key] % 4], 1

        def wait_emptied(eng, key):
            n = tile_number[key]
            eng.wait_ge(bank_emptied[n % 4], n // 4 + 1)

        with nc.Block(no_gpsimd_drain=True) as block:
            @block.sync
            def _(sp):
                sp.dma_start(consts[:, :], A["consts"]).then_inc(consts_in, 16)
                sp.dma_start(rows[:, :], A["rows"].partition_broadcast(P)).then_inc(tables_in, 16)
                sp.dma_start(cols[:, :], A["cols"]).then_inc(tables_in, 16)
                for n in list(WEIGHTS):
                    if "ffn" not in n:
                        sp.dma_start(W[n][:, :], A[n]).then_inc(weights_in[n], 16)

            @block.scalar
            def _(act):
                for n in list(WEIGHTS):
                    if "ffn" in n:
                        act.dma_start(W[n][:, :], A[n]).then_inc(weights_in[n], 16)

            @block.vector
            def _(dve):
                dve.wait_ge(consts_in, 16)
                nc.vector.tensor_copy(ident16[:, :], ident).then_inc(masks_made, 1)
                nc.vector.tensor_copy(masked16[:, :], const("masked")).then_inc(masks_made, 1)

        with nc.Fori(0, BATCHES // PAIR) as it:
            with nc.Block() as block:

                @block.tensor
                def _(pe):
                    mm = nc.tensor.matmul

                    def transposed(key, src, width, wait):
                        wait()
                        g = fill(pe, key)
                        for t in range(TT):
                            last = nc.tensor.transpose(g[0:width, t * P:(t + 1) * P], src[:, t, :], ident)
                        last.then_inc(*filled(key))

                    def z_transposed(n, b, src=None, width=C):
                        transposed(("T", n, b), Z[b] if src is None else src, width, lambda: pe.wait_ge(z_ready, n))

                    pe.wait_ge(consts_in, 16)
                    pe.wait_ge(masks_made, 2)
                    pe.wait_ge(tables_in, 32)

                    pe.wait_ge(weights_in["qkv"], 16)
                    for b in range(PAIR):
                        pe.wait_ge(x_in[b], 64)
                        for t in range(TT):
                            g = fill(pe, ("qkv", b, t))
                            mm(g[:, 0:3 * C], XN[b][:, t * P:(t + 1) * P], W["qkv"][:, :], start=True, stop=True)\
                                .then_inc(*filled(("qkv", b, t)))
                    for b in range(PAIR):
                        for t in range(TT):
                            wait_emptied(pe, ("qkv", b, t))
                        pe.wait_ge(zeroed, b + 1)
                        g = fill(pe, ("ctx", b))
                        w = C + 1
                        half = slice(0, BUCKET)
                        mm(g[:, 0:w], K0B[b][half, 0, :], V0B[b][half, 0, :], start=True, stop=True)
                        mm(g[:, w:2 * w], K0B[b][:, 0, :], V0B[b][:, 0, :], start=True, stop=True)
                        mm(g[:, 2 * w:3 * w], K0B[b][:, 0, :], V0B[b][:, 0, :], start=True, stop=False)
                        mm(g[:, 2 * w:3 * w], K0B[b][half, 1, :], V0B[b][half, 1, :], start=False, stop=True)\
                            .then_inc(*filled(("ctx", b)))
                        transposed(("qT", b), QN[b], C, lambda: pe.wait_ge(q_normal, b + 1))
                    for b in range(PAIR):
                        wait_emptied(pe, ("qT", b))
                        wait_emptied(pe, ("ctx", b))
                        g = fill(pe, ("num", b))
                        w = C + HEADS
                        for n in (1, 2, 3):
                            r, t = BUCKET * (n % 2), n // 2
                            last = mm(g[r:r + BUCKET, t * w:(t + 1) * w], QT[b][:, n * BUCKET:(n + 1) * BUCKET],
                                      CM[b][:, n - 1, :], start=True, stop=True)
                        last.then_inc(*filled(("num", b)))
                    for b in range(PAIR):
                        transposed(("oT", b), Z[b], C, lambda: wait_emptied(pe, ("num", b)))
                    pe.wait_ge(weights_in["wout"], 16)
                    for b in range(PAIR):
                        wait_emptied(pe, ("oT", b))
                        g = fill(pe, ("wout", b))
                        for t in range(TT):
                            last = mm(g[:, t * C:(t + 1) * C], OT[b][:, t * P:(t + 1) * P], W["wout"][:, :],
                                      start=True, stop=True)
                        last.then_inc(*filled(("wout", b)))

                    def project(a, at, b):
                        name, chunks = at["name"], HEADS * at["d"] // P
                        kv = CTXT[b] if name == "lx" else XN[b] if name == "l1" else YN[b]
                        kr = slice(0, CC) if name == "a2" else slice(CC, P) if name == "lx" else slice(0, C)
                        for w in ("wq", "wk", "wv"):
                            pe.wait_ge(weights_in[at[w]], 16)
                        for side, src, kp in (("k", kv, kr), ("q", XN[b], slice(0, C))):
                            w = W[at["w" + side]]
                            for m in range(chunks // 2):
                                g = fill(pe, (side, a, b, m))
                                for k in range(2):
                                    c = 2 * m + k
                                    last = mm(g[:, k * T:(k + 1) * T], w[kp, c * P:(c + 1) * P], src[kp, :],
                                              start=True, stop=True)
                                last.then_inc(*filled((side, a, b, m)))
                        for t in range(TT):
                            for h in range(chunks // 4):
                                g = fill(pe, ("v", a, b, t, h))
                                mm(g[:, :], kv[kr, t * P:(t + 1) * P], W[at["wv"]][kr, h * 512:(h + 1) * 512],
                                   start=True, stop=True).then_inc(*filled(("v", a, b, t, h)))

                    def head(at, i, j):
                        b, h = i // HALVES, 2 * (i % HALVES) + j
                        return b, h * at["d"] // P, h * at["d"] % P

                    def scores(a, at, i):
                        n = a * STEPS + i
                        b = i // HALVES
                        if i % HALVES == 0:
                            for m in range(HEADS * at["d"] // P // 2):
                                wait_emptied(pe, ("k", a, b, m))
                                wait_emptied(pe, ("q", a, b, m))
                        if n >= 2:
                            pe.wait_ge(exp_ready, n - 1)
                        s = SC[n % 2]
                        for j in range(2):
                            _, c, r = head(at, i, j)
                            for t in range(TT):
                                causal = at["kind"] == "causal"
                                w = (t + 1) * P if causal else T
                                last = mm(s[:, j, t, 0:w], QB[r:r + at["d"], c, t * P:(t + 1) * P],
                                          KB[r:r + at["d"], c, 0:w], start=True, stop=not causal)
                                if causal:
                                    last = mm(s[:, j, t, t * P:(t + 1) * P], ident16[:, :], masked16[:, :],
                                              start=False, stop=True)
                        last.then_inc(scores_ready, 1)

                    def transpose_probs(a, at, i):
                        n = a * STEPS + i
                        pe.wait_ge(probs_ready, n + 1)
                        for j in range(2):
                            g = fill(pe, ("PT", a, i, j))
                            for k, (kt, qt) in enumerate(BLOCKS[at["kind"]]):
                                last = nc.tensor.transpose(g[:, k * P:(k + 1) * P],
                                                           PB[:, n % 3, 2 * j + qt, kt * P:(kt + 1) * P], ident)
                            last.then_inc(*filled(("PT", a, i, j)))

                    def weighted_values(a, at, u):
                        d, b = at["d"], (2 * u) // HALVES
                        for i in (2 * u, 2 * u + 1):
                            for j in range(2):
                                wait_emptied(pe, ("PT", a, i, j))
                        if u % (HALVES // 2) == 0:
                            for t in range(TT):
                                for h in range(HEADS * d // 512):
                                    wait_emptied(pe, ("v", a, b, t, h))
                        g = fill(pe, ("O", a, u))
                        sides = [(0, 1, 2, 3)] if d == 32 else [(0, 1), (2, 3)]
                        for side, (first, kt, at_col, q0, width) in [(x, y) for x in sides for y in PARTS[at["kind"]]]:
                            for k in side:
                                i, j = 2 * u + k // 2, k % 2
                                _, c, r = head(at, i, j)
                                h = 2 * (i % HALVES) + j
                                half = (k // 2) * T if d == 64 else 0
                                last = mm(g[r:r + d, half + q0:half + q0 + width], VB[b][:, kt, h * d:(h + 1) * d],
                                          PT[:, (a * STEPS + i) % 3, j, at_col:at_col + width],
                                          start=first, stop=not first)
                        last.then_inc(*filled(("O", a, u)))

                    def project_out(a, at, b):
                        chunks = HEADS * at["d"] // P
                        pe.wait_ge(weights_in[at["wo"]], 16)
                        for u in range(b * HALVES // 2, (b + 1) * HALVES // 2):
                            wait_emptied(pe, ("O", a, u))
                        g = fill(pe, ("x", a, b))
                        for t in range(TT):
                            for c in range(chunks):
                                last = mm(g[:, t * C:(t + 1) * C], OB[:, c, t * P:(t + 1) * P],
                                          W[at["wo"]][:, c * C:(c + 1) * C], start=c == 0, stop=c == chunks - 1)
                        last.then_inc(*filled(("x", a, b)))

                    def attention(a, before):
                        at = ATTENTIONS[a]
                        before(0)
                        project(a, at, 0)
                        for st in range(STEPS + 4):
                            if st == HALVES:
                                before(1)
                                project(a, at, 1)
                            if st < STEPS:
                                scores(a, at, st)
                            if 0 <= st - 2 < STEPS:
                                transpose_probs(a, at, st - 2)
                            if st >= 3 and (st - 3) % 2 == 1 and st - 3 < STEPS:
                                weighted_values(a, at, (st - 3) // 2)
                            if st == HALVES + 3:
                                project_out(a, at, 0)
                        project_out(a, at, 1)

                    def mlp(a, n):
                        name = ATTENTIONS[a]["name"]
                        pe.wait_ge(weights_in[name + "_li2"], 16)
                        pe.wait_ge(weights_in[name + "_li3"], 16)
                        for b in range(PAIR):
                            z_transposed(n + b, b)
                        for b in range(PAIR):
                            wait_emptied(pe, ("T", n + b, b))
                            for m in range(2):
                                g = fill(pe, ("li2", a, b, m))
                                for k in range(2):
                                    c = 2 * m + k
                                    last = mm(g[:, k * T:(k + 1) * T], W[name + "_li2"][:, c * P:(c + 1) * P], XN[b][:, :],
                                              start=True, stop=True)
                                last.then_inc(*filled(("li2", a, b, m)))
                        for b in range(PAIR):
                            for m in range(2):
                                wait_emptied(pe, ("li2", a, b, m))
                            g = fill(pe, ("li3", a, b))
                            for t in range(TT):
                                for c in range(4):
                                    last = mm(g[:, t * C:(t + 1) * C], HB[b][:, c, t * P:(t + 1) * P],
                                              W[name + "_li3"][:, c * C:(c + 1) * C], start=c == 0, stop=c == 3)
                            last.then_inc(*filled(("li3", a, b)))

                    for b in range(PAIR):
                        z_transposed(1 + b, b)
                    attention(0, lambda b: wait_emptied(pe, ("T", 1 + b, b)))
                    mlp(0, 3)
                    for b in range(PAIR):
                        z_transposed(5 + 2 * b, b)
                        z_transposed(6 + 2 * b, b, BIASED[b][:, :, 0:CC], CC)
                    attention(1, lambda b: (wait_emptied(pe, ("T", 5 + 2 * b, b)), wait_emptied(pe, ("T", 6 + 2 * b, b))))
                    mlp(1, 9)

                    for b in range(PAIR):
                        z_transposed(11 + b, b, X[b])
                    pe.wait_ge(weights_in["router"], 16)
                    for b in range(PAIR):
                        wait_emptied(pe, ("T", 11 + b, b))
                        g = fill(pe, ("r0", b))
                        for t in range(TT):
                            last = mm(g[:, t * E0:(t + 1) * E0], XN[b][:, t * P:(t + 1) * P], W["router"][:, :],
                                      start=True, stop=True)
                        last.then_inc(*filled(("r0", b)))

                    def up0(i):
                        e, b = i // PAIR, i % PAIR
                        g = fill(pe, ("up", e, b))
                        for f in range(2):
                            last = mm(g[:, f * T:(f + 1) * T], W["ffn0_w1"][:, e * I0 + f * P:e * I0 + (f + 1) * P],
                                      XN[b][:, :], start=True, stop=True)
                        last.then_inc(*filled(("up", e, b)))

                    def down0(i):
                        e, b = i // PAIR, i % PAIR
                        wait_emptied(pe, ("up", e, b))
                        g = fill(pe, ("down", e, b))
                        for t in range(TT):
                            for f in range(2):
                                k = (2 * e + f) * C
                                last = mm(g[:, t * C:(t + 1) * C], HE[i % 4][:, f, t * P:(t + 1) * P],
                                          W["ffn0_w2"][:, k:k + C], start=f == 0, stop=f == 1)
                        last.then_inc(*filled(("down", e, b)))

                    pe.wait_ge(weights_in["ffn0_w1"], 16)
                    pe.wait_ge(weights_in["ffn0_w2"], 16)
                    pe.wait_ge(weights_in["ffn0_b2"], 16)
                    up0(0)
                    up0(1)
                    for b in range(PAIR):
                        pe.wait_ge(chosen_ready, b + 1)
                        g = fill(pe, ("cT", b))
                        for t in range(TT):
                            last = nc.tensor.transpose(g[0:E0, t * P:(t + 1) * P], combine0[b][:, t, :], ident)
                        last.then_inc(*filled(("cT", b)))
                    for b in range(PAIR):
                        wait_emptied(pe, ("cT", b))
                        g = fill(pe, ("b2", b))
                        for t in range(TT):
                            last = mm(g[:, t * C:(t + 1) * C], combT[b][0:E0, t * P:(t + 1) * P],
                                      W["ffn0_b2"][:, :], start=True, stop=True)
                        last.then_inc(*filled(("b2", b)))
                    for i in range(PAIR * E0):
                        if i + 2 < PAIR * E0:
                            up0(i + 2)
                        down0(i)

                    for b in range(PAIR):
                        z_transposed(13 + b, b, X[b])
                    attention(2, lambda b: wait_emptied(pe, ("T", 13 + b, b)))
                    for b in range(PAIR):
                        z_transposed(15 + b, b, X[b])
                    attention(3, lambda b: wait_emptied(pe, ("T", 15 + b, b)))

                    for b in range(PAIR):
                        z_transposed(17 + b, b, X[b])
                    for n in ("router1", "ffn1_w1", "ffn1_w2"):
                        pe.wait_ge(weights_in[n], 16)
                    for b in range(PAIR):
                        wait_emptied(pe, ("T", 17 + b, b))
                        g = fill(pe, ("r1", b))
                        for t in range(TT):
                            last = mm(g[:, t * E1:(t + 1) * E1], XN[b][:, t * P:(t + 1) * P], W["router1"][:, :],
                                      start=True, stop=True)
                        last.then_inc(*filled(("r1", b)))
                    for b in range(PAIR):
                        pe.wait_ge(chosen_ready, PAIR + b + 1)
                        g = fill(pe, ("pos", b))
                        mm(g[:, 0:E1], const("earlier"), chosen1[b][:, 0, :], start=True, stop=True)
                        mm(g[:, E1:2 * E1], const("later_key")[:, P:2 * P], chosen1[b][:, 0, :], start=True, stop=False)
                        mm(g[:, E1:2 * E1], const("earlier"), chosen1[b][:, 1, :], start=False, stop=True)\
                            .then_inc(*filled(("pos", b)))
                    for b in range(PAIR):
                        pe.wait_ge(dispatch_ready, 2 * b + 1)
                        g = fill(pe, ("buf", b))
                        for t in range(TT):
                            last = mm(g[:, :], X[b][:, t, :], PM[b][:, t, :, :].rearrange("p e s -> p (e s)"),
                                      start=t == 0, stop=t == TT - 1)
                        last.then_inc(*filled(("buf", b)))
                        pe.wait_ge(dispatch_ready, 2 * b + 2)
                        for m in range(2):
                            g = fill(pe, ("PWT", b, m))
                            for k in range(2):
                                for t in range(TT):
                                    p2 = 2 * (2 * m + k)
                                    last = nc.tensor.transpose(
                                        g[:, k * T + t * P:k * T + (t + 1) * P],
                                        PW[b][:, t, p2:p2 + 2, :].rearrange("p e s -> p (e s)"), ident)
                            last.then_inc(*filled(("PWT", b, m)))

                    def up1(i):
                        b, m = i // 4, i % 4
                        if m == 0:
                            wait_emptied(pe, ("buf", b))
                        g = fill(pe, ("up1", b, m))
                        for k in range(2):
                            e = 2 * m + k
                            for f in range(4):
                                s = (4 * k + f) * SLOT
                                last = mm(g[:, s:s + SLOT], W["ffn1_w1"][:, e * I1 + f * P:e * I1 + (f + 1) * P],
                                          BUF[b][:, e * SLOT:(e + 1) * SLOT], start=True, stop=True)
                        last.then_inc(*filled(("up1", b, m)))

                    def down1(i):
                        b, m = i // 4, i % 4
                        pe.wait_ge(hidden_ready, i + 1)
                        g = fill(pe, ("y", b, m))
                        for f in range(4):
                            for k in range(2):
                                w = (4 * (2 * m + k) + f) * C
                                last = mm(g[k * SLOT:(k + 1) * SLOT, 0:C], HX[i % 4][:, 4 * k + f, :],
                                          W["ffn1_w2"][:, w:w + C], start=f == 0, stop=f == 3)
                        last.then_inc(*filled(("y", b, m)))

                    for i in range(4 * PAIR + 1):
                        if i < 4 * PAIR:
                            up1(i)
                        if i >= 1:
                            down1(i - 1)
                    for b in range(PAIR):
                        for m in range(2):
                            wait_emptied(pe, ("PWT", b, m))
                        for m in range(4):
                            wait_emptied(pe, ("y", b, m))
                        g = fill(pe, ("comb", b))
                        for t in range(TT):
                            for m in range(4):
                                last = mm(g[:, t * C:(t + 1) * C], PWT[b][:, m, t * P:(t + 1) * P], YB[b][:, m, :],
                                          start=m == 0, stop=m == 3)
                        last.then_inc(*filled(("comb", b)))

                @block.scalar
                def _(act):
                    fn = nc.scalar.activation

                    def copied(key, dst, src, scale=1.0):
                        g = wait_filled(act, key)
                        fn(dst, src(g), ACT.Copy, scale=scale).then_inc(*emptied(key))

                    def affine(n, b, dst, g_name, b_name, p=P):
                        g = wait_filled(act, ("T", n, b))
                        fn(dst[0:p, :], g[0:p, 0:T], ACT.Identity, scale=col(g_name, p=p), bias=col(b_name, p=p))\
                            .then_inc(*emptied(("T", n, b)))

                    act.wait_ge(tables_in, 32)
                    for b in range(PAIR):
                        for t in range(TT):
                            g = wait_filled(act, ("qkv", b, t))
                            fn(K0B[b][:, t, :], g[:, C:2 * C], ACT.Exp)
                            fn(V0B[b][:, t, 0:C], g[:, 2 * C:3 * C], ACT.Copy).then_inc(kv_drawn, 1)
                    for b in range(PAIR):
                        for t in range(TT):
                            wait_emptied(act, ("qkv", b, t))
                            fn(QN[b][:, t, :], QS[b][:, t, :], ACT.Exp).then_inc(q_exp, 1)
                    for b in range(PAIR):
                        copied(("qT", b), QT[b], lambda g: g[:, 0:T])
                    for b in range(PAIR):
                        copied(("oT", b), OT[b], lambda g: g[:, 0:T])

                    def project(a, at, b):
                        chunks = HEADS * at["d"] // P
                        for m in range(chunks // 2):
                            if at["name"] == "lx":
                                g = wait_filled(act, ("k", a, b, m))
                                fn(KB[:, 2 * m, :], g[:, 0:T], ACT.Identity, bias=col("bk", 2 * m))
                                fn(KB[:, 2 * m + 1, :], g[:, T:2 * T], ACT.Identity, bias=col("bk", 2 * m + 1))\
                                    .then_inc(*emptied(("k", a, b, m)))
                            else:
                                copied(("q", a, b, m), QB[:, 2 * m:2 * m + 2, :].rearrange("p a b -> p (a b)"),
                                       lambda g: g[:, :], at["scale"])
                        if at["name"] != "lx":
                            for h in range(chunks // 4):
                                copied(("v", a, b, 0, h), VB[b][:, 0, h * 512:(h + 1) * 512], lambda g: g[:, :])

                    def exponentials(a, at, i):
                        n = a * STEPS + i
                        if i >= 3:
                            wait_filled(act, ("PT", a, i - 3, 1))
                        act.wait_ge(max_ready, n + 1)
                        for k in range(4):
                            j, t = k // 2, k % 2
                            w = (t + 1) * P if at["kind"] == "causal" else T
                            last = fn(PB[:, n % 3, k, 0:w], SC[n % 2][:, j, t, 0:w], ACT.Exp,
                                      bias=negmax[:, n % 4, k:k + 1], accum_out=sums[:, n % 4, k:k + 1])
                        last.then_inc(exp_ready, 1)

                    def attention(a, before):
                        at = ATTENTIONS[a]
                        project(a, at, 0)
                        for st in range(STEPS + 4):
                            if st == HALVES:
                                project(a, at, 1)
                            if st < STEPS:
                                exponentials(a, at, st)
                            i = st - 2
                            if 0 <= i < STEPS and at["kind"] != "keep_later":
                                w = len(BLOCKS[at["kind"]]) * P
                                copied(("PT", a, i, 1), PT[:, (a * STEPS + i) % 3, 1, 0:w], lambda g: g[:, 0:w])
                            if st >= 3 and (st - 3) % 2 == 1 and st - 3 < STEPS:
                                u = (st - 3) // 2
                                ub = u % (HALVES // 2)
                                if u == HALVES // 2:
                                    wait_filled(act, ("x", a, 0))
                                if at["d"] == 64:
                                    copied(("O", a, u), OB[:, 2 * ub:2 * ub + 2, :].rearrange("p a b -> p (a b)"),
                                           lambda g: g[:, :])
                                else:
                                    copied(("O", a, u), OB[:, ub, :], lambda g: g[:, 0:T])

                    def mlp(a, n):
                        name = ATTENTIONS[a]["name"]
                        for b in range(PAIR):
                            affine(n + b, b, XN[b], name + "_ln3_g", name + "_ln3_b")
                        for b in range(PAIR):
                            for m in range(2):
                                g = wait_filled(act, ("li2", a, b, m))
                                for k in range(2):
                                    c = 2 * m + k
                                    last = fn(HB[b][:, c, :], g[:, k * T:(k + 1) * T], ACT.Gelu,
                                              bias=col(name + "_li2_b", c))
                                last.then_inc(*emptied(("li2", a, b, m)))

                    for b in range(PAIR):
                        g = wait_filled(act, ("T", 1 + b, b))
                        fn(XN[b][:, :], g[:, 0:T], ACT.Identity, scale=col("a1_lnx_g"), bias=col("a1_lnx_b"))
                        fn(YN[b][:, :], g[:, 0:T], ACT.Identity, scale=col("a1_lny_g"), bias=col("a1_lny_b"))\
                            .then_inc(*emptied(("T", 1 + b, b)))
                    attention(0, None)
                    mlp(0, 3)
                    for b in range(PAIR):
                        affine(5 + 2 * b, b, XN[b], "a2_lnx_g", "a2_lnx_b")
                        affine(6 + 2 * b, b, YN[b], "a2_lny_g", "a2_lny_b", CC)
                    attention(1, None)
                    mlp(1, 9)

                    for b in range(PAIR):
                        copied(("T", 11 + b, b), XN[b][:, :], lambda g: g[:, 0:T])
                    for b in range(PAIR):
                        act.wait_ge(logits_shifted, b + 1)
                        fn(expd0[b], shifted0[b], ACT.Exp).then_inc(logits_exp, 1)

                    def gelu_up(i):
                        e, b = i // PAIR, i % PAIR
                        g = wait_filled(act, ("up", e, b))
                        if i >= 4:
                            wait_filled(act, ("down", (i - 4) // PAIR, b))
                        for f in range(2):
                            last = fn(HE[i % 4][:, f, :], g[:, f * T:(f + 1) * T], ACT.Gelu,
                                      bias=col("ffn0_b1", 2 * e + f))
                        last.then_inc(*emptied(("up", e, b)))

                    gelu_up(0)
                    gelu_up(1)
                    for b in range(PAIR):
                        copied(("cT", b), combT[b][0:E0, :], lambda g: g[0:E0, 0:T])
                    for i in range(2, PAIR * E0):
                        gelu_up(i)

                    for b in range(PAIR):
                        copied(("T", 13 + b, b), XN[b][:, :], lambda g: g[:, 0:T])
                    attention(2, None)
                    for b in range(PAIR):
                        copied(("T", 15 + b, b), XN[b][:, :], lambda g: g[:, 0:T])
                    attention(3, None)

                    for b in range(PAIR):
                        copied(("T", 17 + b, b), XN[b][:, :], lambda g: g[:, 0:T])
                    for b in range(PAIR):
                        act.wait_ge(logits_shifted, PAIR + b + 1)
                        fn(expd1[b], shifted1[b], ACT.Exp).then_inc(logits_exp, 1)
                    for b in range(PAIR):
                        copied(("buf", b), BUF[b], lambda g: g[:, :])
                        for m in range(2):
                            copied(("PWT", b, m), PWT[b][:, 2 * m:2 * m + 2, :].rearrange("p a b -> p (a b)"),
                                   lambda g: g[:, :])
                    for i in range(4 * PAIR):
                        wait_emptied(act, ("up1", i // 4, i % 4))
                        fn(HX[i % 4], HX[i % 4], ACT.Relu).then_inc(hidden_ready, 1)

                @block.vector
                def _(dve):
                    v = nc.vector
                    links = [0]

                    def link(ins):
                        links[0] += 1
                        ins.then_inc(dve_chain, 1)
                        dve.wait_ge(dve_chain, links[0])

                    norms = [0]

                    def layernorm(src, dst, width=C):
                        norms[0] += 1
                        for t in range(TT):
                            last = v.bn_stats(stats[:, t, :], src[:, t, 0:width])
                        link(last)
                        for t in range(TT):
                            last = v.bn_aggr(moments[:, t, :], stats[:, t, :])
                        link(last)
                        v.tensor_scalar(variance[:, :], moments[:, :, 1], EPS, None, ALU.add).then_inc(variance_ready, 1)
                        dve.wait_ge(rstd_ready, norms[0])
                        for t in range(TT):
                            last = v.tensor_scalar(dst[:, t, 0:width], src[:, t, 0:width], moments[:, t, 0:1],
                                                   rstd[:, t:t + 1], ALU.subtract, ALU.mult)
                        return last

                    def over_tiles(vec):
                        return vec.unsqueeze(1).to_broadcast([P, TT, C])

                    def gain_bias(x, g_name, b_name):
                        link(v.tensor_tensor(x[:, :, :], x[:, :, :], over_tiles(row(g_name)), ALU.mult))
                        return v.tensor_tensor(x[:, :, :], x[:, :, :], over_tiles(row(b_name)), ALU.add)

                    def residual(key, dst, other):
                        g = wait_filled(dve, key)
                        v.tensor_tensor(dst[:, :, :], g[:, 0:TT * C].rearrange("p (t c) -> p t c", c=C),
                                        other[:, :, :], ALU.add).then_inc(*emptied(key))
                        wait_emptied(dve, key)

                    dve.wait_ge(consts_in, 16)
                    dve.wait_ge(tables_in, 32)
                    heads = lambda x: x.rearrange("p (h d) -> p h d", d=HD0)
                    for b in range(PAIR):
                        dve.wait_ge(x_in[b], 64)
                        for t in range(TT):
                            g = wait_filled(dve, ("qkv", b, t))
                            dve.wait_ge(kv_drawn, TT * b + t + 1)
                            m = small0[b][:, t * HEADS:(t + 1) * HEADS]
                            link(v.tensor_reduce(m, heads(g[:, 0:C]), axis=AX.X, op=ALU.max))
                            v.tensor_tensor(heads(QS[b][:, t, :]), heads(g[:, 0:C]),
                                            m.unsqueeze(2).to_broadcast([P, HEADS, HD0]), ALU.subtract)\
                                .then_inc(*emptied(("qkv", b, t)))
                    for b in range(PAIR):
                        dve.wait_ge(q_exp, TT * (b + 1))
                        flat = QN[b].rearrange("p t c -> p (t c)")
                        s, r = small0[b][:, 32:64], small0[b][:, 64:96]
                        link(v.tensor_reduce(s, heads(flat), axis=AX.X, op=ALU.add))
                        link(v.reciprocal(r, s))
                        link(v.tensor_scalar(s, r, HD0 ** -0.5, None, ALU.mult))
                        v.tensor_tensor(heads(flat), heads(flat), s.unsqueeze(2).to_broadcast([P, TT * HEADS, HD0]),
                                        ALU.mult).then_inc(q_normal, 1)
                        g = wait_filled(dve, ("ctx", b))
                        prod = g[:, 0:3 * (C + 1)].rearrange("p (n c) -> p n c", c=C + 1)
                        v.tensor_tensor(CM[b][:, :, 0:C], prod[:, :, 0:C],
                                        const("same_head").unsqueeze(1).to_broadcast([P, 3, C]), ALU.mult)
                        v.tensor_tensor(CM[b][:, :, C:C + HEADS], prod[:, :, C:C + 1].to_broadcast([P, 3, HEADS]),
                                        const("head_of").unsqueeze(1).to_broadcast([P, 3, HEADS]), ALU.mult)\
                            .then_inc(*emptied(("ctx", b)))
                    for b in range(PAIR):
                        g = wait_filled(dve, ("num", b))
                        dve.wait_ge(zeroed, PAIR + b + 1)
                        for t, r0 in ((0, BUCKET), (1, 0)):
                            tile = g[r0:P, t * (C + HEADS):(t + 1) * (C + HEADS)]
                            s, r = small0[b][r0:P, 96:112], small0[b][r0:P, 112:128]
                            link(v.tensor_scalar(s, tile[:, C:C + HEADS], 1e-6, None, ALU.max))
                            link(v.reciprocal(r, s))
                            last = v.tensor_tensor(heads(Z[b][r0:P, t, :]), heads(tile[:, 0:C]),
                                                   r.unsqueeze(2).to_broadcast([P - r0, HEADS, HD0]), ALU.mult)
                            if t == 0:
                                link(last)
                        last.then_inc(*emptied(("num", b)))
                    for b in range(PAIR):
                        residual(("wout", b), R[b], X[b])
                        link(layernorm(R[b], X[b]))
                        link(layernorm(X[b], U[b]))
                        gain_bias(U[b], "ln1_g", "ln1_b").then_inc(u_ready, 1)
                        dve.wait_ge(u_ready, b + 1)
                        layernorm(U[b], Z[b]).then_inc(z_ready, 1)

                    def project(a, at, b):
                        chunks, name = HEADS * at["d"] // P, at["name"]
                        for m in range(chunks // 2):
                            if name != "lx":
                                g = wait_filled(dve, ("k", a, b, m))
                                v.tensor_copy(KB[:, 2 * m:2 * m + 2, :].rearrange("p a b -> p (a b)"), g[:, :])\
                                    .then_inc(*emptied(("k", a, b, m)))
                        for m in range(chunks // 2):
                            if name == "lx":
                                g = wait_filled(dve, ("q", a, b, m))
                                for k in range(2):
                                    last = v.tensor_scalar(QB[:, 2 * m + k, :], g[:, k * T:(k + 1) * T],
                                                           col("bq", 2 * m + k), at["scale"], ALU.add, ALU.mult)
                                last.then_inc(*emptied(("q", a, b, m)))
                        for t in range(TT):
                            for h in range(chunks // 4):
                                if name == "lx":
                                    g = wait_filled(dve, ("v", a, b, t, h))
                                    v.tensor_tensor(VB[b][:, t, 0:512], g[:, :], row("bv"), ALU.add)\
                                        .then_inc(*emptied(("v", a, b, t, h)))
                                elif t == 1:
                                    g = wait_filled(dve, ("v", a, b, t, h))
                                    v.tensor_copy(VB[b][:, t, h * 512:(h + 1) * 512], g[:, :])\
                                        .then_inc(*emptied(("v", a, b, t, h)))

                    def maxima(a, at, i):
                        n = a * STEPS + i
                        dve.wait_ge(scores_ready, n + 1)
                        s = SC[n % 2]
                        m = negmax[:, n % 4, :]
                        if at["kind"] == "causal":
                            mv = m.rearrange("p (j t) -> p j t", t=TT)
                            for t in range(TT):
                                last = v.tensor_reduce(mv[:, :, t], s[:, :, t, 0:(t + 1) * P], axis=AX.X, op=ALU.max,
                                                       negate=True)
                        else:
                            last = v.tensor_reduce(m, s[:, :, :, :].rearrange("p j t k -> p (j t) k"), axis=AX.X,
                                                   op=ALU.max, negate=True)
                        last.then_inc(max_ready, 1)

                    def inverses(a, i):
                        n = a * STEPS + i
                        dve.wait_ge(exp_ready, n + 1)
                        v.reciprocal(inverse[:, n % 4, :], sums[:, n % 4, :]).then_inc(inverse_ready, 1)

                    def attention_sum(a, b):
                        if a != 2:
                            dve.wait_ge(bias_ready, {0: 0, 1: 2, 3: 4}[a] * PAIR + b + 1)
                        residual(("x", a, b), R[b], X[b] if a == 2 else BIASED[b])

                    def attention(a):
                        at = ATTENTIONS[a]
                        project(a, at, 0)
                        for st in range(STEPS + 4):
                            if st == HALVES:
                                project(a, at, 1)
                            if st == HALVES + 4:
                                attention_sum(a, 0)
                            if st < STEPS:
                                maxima(a, at, st)
                            if 0 <= st - 1 < STEPS:
                                inverses(a, st - 1)
                            i = st - 2
                            if 0 <= i < STEPS:
                                if i >= 3:
                                    wait_filled(dve, ("O", a, (i - 3) // 2))
                                for j in ((0, 1) if at["kind"] == "keep_later" else (0,)):
                                    g = wait_filled(dve, ("PT", a, i, j))
                                    w = len(BLOCKS[at["kind"]]) * P
                                    dst = PT[:, (a * STEPS + i) % 3, j, 0:w]
                                    if at["kind"] == "keep_later":
                                        last = v.tensor_tensor(dst, g[:, 0:w], const("later_key"), ALU.mult)
                                    else:
                                        last = v.tensor_copy(dst, g[:, 0:w])
                                    last.then_inc(*emptied(("PT", a, i, j)))
                        attention_sum(a, 1)

                    def context_norm(b):
                        layernorm(CTX[b], BIASED[b], CC).then_inc(z_ready, 1)

                    attention(0)
                    for b in range(PAIR):
                        layernorm(R[b], Z[b]).then_inc(z_ready, 1)
                    for b in range(PAIR):
                        dve.wait_ge(bias_ready, PAIR + b + 1)
                        residual(("li3", 0, b), R[b], U[b])
                        link(layernorm(R[b], U[b]))
                        gain_bias(U[b], "ln2_g", "ln2_b").then_inc(u_ready, 1)
                        dve.wait_ge(u_ready, PAIR + b + 1)
                        layernorm(U[b], Z[b]).then_inc(z_ready, 1)
                        context_norm(b)
                    attention(1)
                    for b in range(PAIR):
                        layernorm(R[b], Z[b]).then_inc(z_ready, 1)
                    for b in range(PAIR):
                        dve.wait_ge(bias_ready, 3 * PAIR + b + 1)
                        residual(("li3", 1, b), R[b], U[b])
                        layernorm(R[b], X[b]).then_inc(z_ready, 1)

                    def chosen(b, prob, E, top, idx, onehot, sel, k):
                        for t in range(TT):
                            last = v.max(top[:, t, :], prob[:, t, :])
                        link(last)
                        for t in range(TT):
                            last = v.max_index(idx[:, t, :], top[:, t, :], prob[:, t, :])
                        link(last)
                        for t in range(TT):
                            last = v.tensor_tensor(onehot[:, t, :, :], const("iota_e")[:, 0:E].unsqueeze(1)
                                                   .to_broadcast([P, k, E]),
                                                   idx[:, t, 0:k].unsqueeze(2).to_broadcast([P, k, E]), ALU.is_equal)
                        link(last)
                        for t in range(TT):
                            last = v.tensor_reduce(sel[:, t, :], onehot[:, t, :, :].rearrange("p k e -> p e k"),
                                                   axis=AX.X, op=ALU.add)
                        return last

                    def shift(b, shifted, E, one):
                        link(v.tensor_reduce(one, shifted, axis=AX.X, op=ALU.max))
                        v.tensor_tensor(shifted, shifted, one.unsqueeze(2).to_broadcast([P, TT, E]), ALU.subtract)\
                            .then_inc(logits_shifted, 1)

                    for b in range(PAIR):
                        g = wait_filled(dve, ("r0", b))
                        v.tensor_tensor(shifted0[b], g[:, 0:TT * E0].rearrange("p (t e) -> p t e", e=E0),
                                        row("router_b").unsqueeze(1).to_broadcast([P, TT, E0]), ALU.add)\
                            .then_inc(*emptied(("r0", b)))
                        wait_emptied(dve, ("r0", b))
                        shift(b, shifted0[b], E0, one[b])
                    for b in range(PAIR):
                        dve.wait_ge(logits_exp, b + 1)
                        link(chosen(b, expd0[b], E0, top8[b], index8[b], onehot0[b], combine0[b], K0))
                        link(v.tensor_tensor(shifted0[b], combine0[b], expd0[b], ALU.mult))
                        link(v.tensor_reduce(one[b], shifted0[b], axis=AX.X, op=ALU.add))
                        link(v.reciprocal(two[b], one[b]))
                        v.tensor_tensor(combine0[b], shifted0[b], two[b].unsqueeze(2).to_broadcast([P, TT, E0]),
                                        ALU.mult).then_inc(chosen_ready, 1)
                    for b in range(PAIR):
                        residual(("b2", b), R[b], X[b])
                    for i in range(PAIR * E0):
                        e, b = i // PAIR, i % PAIR
                        g = wait_filled(dve, ("down", e, b))
                        if e == 0:
                            dve.wait_ge(chosen_ready, b + 1)
                        else:
                            wait_emptied(dve, ("down", e - 1, b))
                        for t in range(TT):
                            last = v.scalar_tensor_tensor(R[b][:, t, :], g[:, t * C:(t + 1) * C],
                                                          combine0[b][:, t, e:e + 1], R[b][:, t, :],
                                                          op0=ALU.mult, op1=ALU.add)
                        last.then_inc(*emptied(("down", e, b)))
                    for b in range(PAIR):
                        wait_emptied(dve, ("down", E0 - 1, b))
                        layernorm(R[b], X[b]).then_inc(z_ready, 1)

                    attention(2)
                    for b in range(PAIR):
                        layernorm(R[b], X[b]).then_inc(z_ready, 1)
                    attention(3)
                    for b in range(PAIR):
                        layernorm(R[b], X[b]).then_inc(z_ready, 1)

                    for b in range(PAIR):
                        g = wait_filled(dve, ("r1", b))
                        v.tensor_copy(shifted1[b], g[:, 0:TT * E1].rearrange("p (t e) -> p t e", e=E1))\
                            .then_inc(*emptied(("r1", b)))
                        wait_emptied(dve, ("r1", b))
                        shift(b, shifted1[b], E1, one[b])
                    for b in range(PAIR):
                        dve.wait_ge(logits_exp, PAIR + b + 1)
                        link(v.tensor_reduce(one[b], expd1[b], axis=AX.X, op=ALU.add))
                        link(v.reciprocal(two[b], one[b]))
                        link(v.tensor_tensor(expd1[b], expd1[b], two[b].unsqueeze(2).to_broadcast([P, TT, E1]),
                                             ALU.mult))
                        chosen(b, expd1[b], E1, top8[b], index8[b], onehot1[b], chosen1[b], 2).then_inc(chosen_ready, 1)
                    for b in range(PAIR):
                        g = wait_filled(dve, ("pos", b))
                        dve.wait_ge(chosen_ready, PAIR + b + 1)
                        v.scalar_tensor_tensor(shifted1[b].rearrange("p t e -> p (t e)"), g[:, 0:TT * E1], 1.0,
                                               chosen1[b].rearrange("p t e -> p (t e)"), op0=ALU.add, op1=ALU.mult)\
                            .then_inc(*emptied(("pos", b)))
                        wait_emptied(dve, ("pos", b))
                        for t in range(TT):
                            last = v.tensor_tensor(PM[b][:, t, :, :],
                                                   const("iota_slot").unsqueeze(1).to_broadcast([P, E1, SLOT]),
                                                   shifted1[b][:, t, :].unsqueeze(2).to_broadcast([P, E1, SLOT]),
                                                   ALU.is_equal)
                        last.then_inc(dispatch_ready, 1)
                        dve.wait_ge(dispatch_ready, 2 * b + 1)
                        for t in range(TT):
                            last = v.tensor_tensor(PW[b][:, t, :, :], PM[b][:, t, :, :],
                                                   expd1[b][:, t, :].unsqueeze(2).to_broadcast([P, E1, SLOT]), ALU.mult)
                        last.then_inc(dispatch_ready, 1)
                    dve.wait_ge(weights_in["ffn1_b2"], 16)
                    for i in range(4 * PAIR + 2):
                        if i < 4 * PAIR:
                            b, m = i // 4, i % 4
                            g = wait_filled(dve, ("up1", b, m))
                            if i >= 4:
                                wait_filled(dve, ("y", 0, i - 4))
                            b1 = cols[:, COLS["ffn1_b1"][0] + 8 * m:COLS["ffn1_b1"][0] + 8 * m + 8]
                            v.tensor_tensor(HX[i % 4], g[:, :].rearrange("p (a s) -> p a s", s=SLOT),
                                            b1.unsqueeze(2).to_broadcast([P, 8, SLOT]), ALU.add)\
                                .then_inc(*emptied(("up1", b, m)))
                        if i >= 2:
                            b, m = (i - 2) // 4, (i - 2) % 4
                            g = wait_filled(dve, ("y", b, m))
                            v.tensor_tensor(YB[b][:, m, :], g[:, 0:C], W["ffn1_b2"][:, m * C:(m + 1) * C], ALU.add)\
                                .then_inc(*emptied(("y", b, m)))
                    for b in range(PAIR):
                        residual(("comb", b), R[b], X[b])
                        layernorm(R[b], Z[b]).then_inc(final_ready, 1)

                @block.gpsimd
                def _(pool):
                    v = nc.gpsimd
                    norms, links = [0], [0]

                    def link(ins):
                        links[0] += 1
                        ins.then_inc(pool_chain, 1)
                        pool.wait_ge(pool_chain, links[0])

                    def inverse_deviation(times=1):
                        for _ in range(times):
                            norms[0] += 1
                            pool.wait_ge(variance_ready, norms[0])
                            v.tensor_tensor(rstd[:, :], variance[:, :], const("minus_half"), ALU.pow)\
                                .then_inc(rstd_ready, 1)

                    def plus_row(dst, src, name):
                        return v.tensor_tensor(dst[:, :, :], src[:, :, :],
                                               row(name).unsqueeze(1).to_broadcast([P, TT, C]), ALU.add)

                    pool.wait_ge(consts_in, 16)
                    for b in range(PAIR):
                        v.memset(V0B[b][:, :, C:C + 1], 1.0).then_inc(zeroed, 1)
                    for b in range(PAIR):
                        v.memset(Z[b][0:BUCKET, 0, :], 0.0).then_inc(zeroed, 1)
                    pool.wait_ge(tables_in, 32)

                    def attention(a):
                        at = ATTENTIONS[a]
                        for i in range(STEPS):
                            n = a * STEPS + i
                            pool.wait_ge(inverse_ready, n + 1)
                            inv = inverse[:, n % 4, :]
                            if at["kind"] == "causal":
                                for t in range(TT):
                                    w = (t + 1) * P
                                    p = PB[:, n % 3, :, :].rearrange("p (j t) k -> p j t k", t=TT)[:, :, t, 0:w]
                                    m = inv.rearrange("p (j t) -> p j t", t=TT)[:, :, t:t + 1].to_broadcast([P, 2, w])
                                    last = v.tensor_tensor(p, p, m, ALU.mult)
                            else:
                                p = PB[:, n % 3, :, :]
                                last = v.tensor_tensor(p, p, inv.unsqueeze(2).to_broadcast([P, 4, T]), ALU.mult)
                            last.then_inc(probs_ready, 1)

                    def bias_sums(name, first, n):
                        pool.wait_ge(u_ready, n)
                        plus_row(BIASED[(n - 1) % PAIR], U[(n - 1) % PAIR], name).then_inc(bias_ready, 1)

                    for b in range(PAIR):
                        inverse_deviation(3)
                    for b in range(PAIR):
                        bias_sums("a1_li1_b", 0, b + 1)
                    attention(0)
                    for b in range(PAIR):
                        inverse_deviation()
                        link(plus_row(U[b], U[b], "a1_li3_b"))
                        wait_emptied(pool, ("x", 0, b))
                        v.tensor_tensor(U[b][:, :, :], U[b][:, :, :], R[b][:, :, :], ALU.add).then_inc(bias_ready, 1)
                    for b in range(PAIR):
                        inverse_deviation(3)
                    for b in range(PAIR):
                        pool.wait_ge(z_ready, 8)
                        wait_filled(pool, ("T", 6 + 2 * b, b))
                        bias_sums("a2_li1_b", 0, PAIR + b + 1)
                    attention(1)
                    for b in range(PAIR):
                        inverse_deviation()
                        link(plus_row(U[b], U[b], "a2_li3_b"))
                        link(v.tensor_tensor(U[b][:, :, :], U[b][:, :, :], X[b][:, :, :], ALU.add))
                        wait_emptied(pool, ("x", 1, b))
                        v.tensor_tensor(U[b][:, :, :], U[b][:, :, :], R[b][:, :, :], ALU.add).then_inc(bias_ready, 1)
                    for b in range(PAIR):
                        inverse_deviation()
                    for b in range(PAIR):
                        inverse_deviation()
                    attention(2)
                    for b in range(PAIR):
                        inverse_deviation()
                    for b in range(PAIR):
                        pool.wait_ge(z_ready, 15 + b)
                        plus_row(BIASED[b], X[b], "bo").then_inc(bias_ready, 1)
                    attention(3)
                    for b in range(PAIR):
                        inverse_deviation()
                    for b in range(PAIR):
                        inverse_deviation()

                @block.sync
                def _(sp):
                    for b in range(PAIR):
                        n = it * PAIR + b
                        sp.dma_start(XN[b][:, :], A["xT"][n]).then_inc(x_in[b], 16)
                        sp.dma_start(X[b][:, :, :], A["x"][n].rearrange("(t p) c -> p t c", p=P)).then_inc(x_in[b], 16)
                        sp.dma_start(CTX[b][:, :, :], A["ctx"][n].rearrange("(t p) c -> p t c", p=P))\
                            .then_inc(x_in[b], 16)
                        sp.dma_start(CTXT[b][CC:P, :], A["ctxT"][n]).then_inc(x_in[b], 16)
                    for b in range(PAIR):
                        sp.wait_ge(final_ready, b + 1)
                        sp.dma_start(out[it * PAIR + b].rearrange("(t p) c -> p t c", p=P), Z[b][:, :, :])\
                            .then_inc(out_stored, 16)
                    sp.wait_ge(out_stored, 16 * PAIR)

            numbers = sorted(s.num for s in per_pass)
            nc.sync.sem_clear(range(numbers[0], numbers[-1] + 1))
            nc.all_engine_barrier()


def arranged(x, ctx_512, **w):
    def heads_in(a):
        return a.transpose(1, 0, 2).reshape(a.shape[1], -1)

    def tiles(a):
        return a.reshape(-1, P, a.shape[-1]).transpose(1, 0, 2).reshape(P, -1)

    def padded(a):
        out = np.zeros((*a.shape[:-1], HEADS, 32), a.dtype)
        out[..., :HD0] = a.reshape(*a.shape[:-1], HEADS, HD0)
        return out.reshape(*a.shape[:-1], -1)

    x0 = "L0_xattn_"
    A = {"x": x, "xT": x.transpose(0, 2, 1), "ctx": ctx_512, "ctxT": ctx_512.transpose(0, 2, 1),
         "qkv": w["L0_attn_W_qkv"].T, "wout": w["L0_attn_W_out"].T}
    for a in ("a1", "a2"):
        for k in ("wq", "wk", "wv") if a == "a1" else ("wq",):
            A[f"{a}_{k}"] = heads_in(w[f"{x0}{a}_{k}"])
        A[a + "_li1"], A[a + "_li2"], A[a + "_li3"] = (tiles(w[x0 + a + "_li1_w"]), w[x0 + a + "_li2_w"],
                                                      tiles(w[x0 + a + "_li3_w"]))
    A["router"], A["ffn0_b2"] = w["L0_ffn_router_w"], w["L0_ffn_b2"]
    A["ffn0_w1"] = heads_in(w["L0_ffn_w1"])
    A["ffn0_w2"] = tiles(w["L0_ffn_w2"].reshape(-1, C))
    for k, n in (("wq", "W_Q"), ("wk", "W_K"), ("wv", "W_V")):
        A["l1_" + k] = w["L1_attn_" + n].reshape(-1, C).T
    A["l1_wo"] = tiles(w["L1_attn_W_O"].T)
    A["lx_wq"] = padded(w["L1_xattn_Wq"])
    for k in ("k", "v"):
        A["ctx_w" + k] = np.concatenate([heads_in(w[f"{x0}a2_w{k}"]), padded(w["L1_xattn_W" + k])])
    A["lx_wo"] = tiles(padded(w["L1_xattn_Wo"].T).T)
    A["router1"] = w["L1_ffn_Wr"]
    A["ffn1_w1"] = heads_in(w["L1_ffn_W1"])
    A["ffn1_w2"] = tiles(w["L1_ffn_W2"].reshape(-1, C))
    A["ffn1_b2"] = tiles(np.repeat(w["L1_ffn_b2"], SLOT, axis=0))
    rows = {"bo": w["L1_xattn_bo"], "router_b": w["L0_ffn_router_b"], "bv": padded(w["L1_xattn_bv"])}
    A["rows"] = np.concatenate([rows[n] if n in rows else w[x0 + n] for n in ROWS])
    columns = {"ffn0_b1": w["L0_ffn_b1"], "ffn1_b1": w["L1_ffn_b1"], "bq": padded(w["L1_xattn_bq"]),
               "bk": padded(w["L1_xattn_bk"])}
    packed = np.zeros((P, NCOLS), x.dtype)
    for n, (at, width) in COLS.items():
        v = (columns[n] if n in columns else w[x0 + n]).reshape(width, -1)
        packed[:v.shape[1], at:at + width] = v.T
    A["cols"] = packed
    A["consts"] = shape_constants()
    return {n: np.ascontiguousarray(a) for n, a in A.items()}


def kernel(**inputs):
    import concourse.bacc as _bacc
    from concourse.bass_utils import run_bass_kernel_spmd as _run

    arrays = arranged(**{n: np.asarray(a) for n, a in inputs.items()})
    nc = _bacc.Bacc("TRN2", target_bir_lowering=False, num_devices=1)
    A = {n: nc.dram_tensor("in_" + n, a.shape, mybir.dt.from_np(a.dtype), kind="ExternalInput").ap()
         for n, a in arrays.items()}
    out = nc.dram_tensor("out", (BATCHES, T, C), fp32, kind="ExternalOutput").ap()
    decoder(nc, A, out)
    r = _run(nc, [{"in_" + n: a for n, a in arrays.items()}], core_ids=[0])
    return r.results[0]["out"]
```

```python
import concourse.bass as bass
from concourse import mybir
from contextlib import ExitStack

import numpy as np

fp32 = mybir.dt.float32
bf16 = mybir.dt.bfloat16
f32r = mybir.dt.float32r
u32 = mybir.dt.uint32
ALU = mybir.AluOpType
ACT = mybir.ActivationFunctionType
AX = mybir.AxisListType

P = 128
BATCHES, T, C, CC = 4, 256, 128, 64
TT = T // P
PAIR = 2
HEADS = 16
EPS = 1e-5
BUCKET = 64
HD0 = C // HEADS
E0, K0, I0 = 16, 4, 256
E1, I1 = 8, 512
CAP = int(T / E1 * 1.25)
SLOT = 64

ROWS = {}
for _n, _w in [("ln1_g", C), ("ln1_b", C), ("ln2_g", C), ("ln2_b", C), ("a1_li1_b", C), ("a1_li3_b", C),
               ("a2_li1_b", C), ("a2_li3_b", C), ("bo", C), ("router_b", E0), ("bv", HEADS * 32)]:
    ROWS[_n] = (sum(w for _, w in ROWS.values()), _w)
NROWS = sum(w for _, w in ROWS.values())
COLS = {}
for _n, _w in [("a1_lnx_g", 1), ("a1_lnx_b", 1), ("a1_lny_g", 1), ("a1_lny_b", 1), ("a1_ln3_g", 1), ("a1_ln3_b", 1),
               ("a1_li2_b", 4), ("a2_lnx_g", 1), ("a2_lnx_b", 1), ("a2_lny_g", 1), ("a2_lny_b", 1), ("a2_ln3_g", 1),
               ("a2_ln3_b", 1), ("a2_li2_b", 4), ("ffn0_b1", 2 * E0), ("ffn1_b1", 4 * E1), ("bq", 4), ("bk", 4)]:
    COLS[_n] = (sum(w for _, w in COLS.values()), _w)
NCOLS = sum(w for _, w in COLS.values())
CONSTS = {}
for _n, _w in [("ident", P), ("same_head", P), ("head_of", HEADS), ("later_key", 3 * P), ("earlier", P),
               ("masked", P), ("iota_e", E0), ("iota_slot", SLOT), ("minus_half", TT)]:
    CONSTS[_n] = (sum(w for _, w in CONSTS.values()), _w)
NCONSTS = sum(w for _, w in CONSTS.values())


def shape_constants():
    p, f = np.arange(P)[:, None], np.arange(P)[None, :]
    later = (p > f)
    parts = {
        "ident": p == f, "same_head": p // HD0 == f // HD0,
        "head_of": p // HD0 == np.arange(HEADS)[None, :],
        "later_key": np.concatenate([later, np.ones((P, P)), later], 1),
        "earlier": p < f,
        "masked": np.where(f > p, -1e10, 0.0),
        "iota_e": np.broadcast_to(np.arange(E0), (P, E0)),
        "iota_slot": np.broadcast_to(np.where(np.arange(SLOT) < CAP, np.arange(SLOT) + 1, -5), (P, SLOT)),
        "minus_half": np.full((P, TT), -0.5),
    }
    return np.concatenate([np.asarray(parts[n], np.float32) for n in CONSTS], 1)


WEIGHTS = {
    "qkv": (C, 3 * C), "wout": (C, C),
    "a1_wq": (C, 512), "a1_wk": (C, 512), "a1_wv": (C, 512), "a1_li1": (P, 512), "a1_li2": (C, 512), "a1_li3": (P, 512),
    "ctx_wk": (2 * CC, 512), "ctx_wv": (2 * CC, 512), "a2_wq": (C, 512), "a2_li1": (P, 512), "a2_li2": (C, 512), "a2_li3": (P, 512),
    "router": (C, E0), "ffn0_b2": (E0, C),
    "l1_wq": (C, 1024), "l1_wk": (C, 1024), "l1_wv": (C, 1024), "l1_wo": (P, 1024),
    "lx_wq": (C, 512), "lx_wo": (P, 512),
    "router1": (C, E1), "ffn1_b2": (P, 4 * C),
}

EXPERT_WEIGHTS = {"ffn0_w1": (C, E0 * I0), "ffn0_w2": (P, 2 * E0 * C),
                  "ffn1_w1": (C, E1 * I1), "ffn1_w2": (P, 4 * E1 * C)}
PARTS_OF_EXPERTS = 4

ATTENTIONS = [
    dict(name="a1", d=32, scale=32 ** -0.5, kind="keep_later", wq="a1_wq", wk="a1_wk", wv="a1_wv", wo="a1_li1"),
    dict(name="a2", d=32, scale=32 ** -0.5, kind="full", wq="a2_wq", wk="ctx_wk", wv="ctx_wv", wo="a2_li1"),
    dict(name="l1", d=64, scale=1 / 8, kind="causal", wq="l1_wq", wk="l1_wk", wv="l1_wv", wo="l1_wo"),
    dict(name="lx", d=32, scale=8 ** -0.5, kind="full", wq="lx_wq", wk="ctx_wk", wv="ctx_wv", wo="lx_wo"),
]
BLOCKS = {
    "full": [(0, 0), (0, 1), (1, 0), (1, 1)],
    "causal": [(0, 0), (0, 1), (1, 1)],
    "keep_later": [(0, 0), (1, 0), (1, 1)],
}
PARTS = {
    "full": [(True, 0, 0, 0, T), (False, 1, T, 0, T)],
    "causal": [(True, 0, 0, 0, T), (False, 1, T, P, P)],
    "keep_later": [(True, 1, P, 0, T), (False, 0, 0, 0, P)],
}
HALVES = HEADS // 2
SECOND_AT = 5
LAG = 3
RING = LAG + 1
SUM_AT = HALVES + LAG + 2
STEPS = PAIR * HALVES


def decoder(nc, A, out):
    ctx = ExitStack()
    with ctx:
        def sb(name, shape, dt=fp32):
            return ctx.enter_context(nc.sbuf_tensor(name, shape, dt))

        W = {n: sb("w_" + n, [p, w]) for n, (p, w) in WEIGHTS.items()}
        rows, cols, consts = sb("rows", [P, NROWS]), sb("cols", [P, NCOLS]), sb("consts", [P, NCONSTS])

        def row(n):
            return rows[:, ROWS[n][0]:ROWS[n][0] + ROWS[n][1]]

        def col(n, k=0, p=P):
            return cols[0:p, COLS[n][0] + k:COLS[n][0] + k + 1]

        def const(n):
            return consts[:, CONSTS[n][0]:CONSTS[n][0] + CONSTS[n][1]]

        ident = const("ident")
        ident16, masked16 = sb("ident16", [P, P], bf16), sb("masked16", [P, P], bf16)

        def per_batch(name, shape):
            return [sb(f"{name}{b}", shape) for b in range(PAIR)]

        X, R, Z, U, BIASED = (per_batch(n, [P, TT, C]) for n in ("X", "R", "Z", "U", "BIASED"))
        XN, YN = (per_batch(n, [P, T]) for n in ("XN", "YN"))
        CTX, CTXT = per_batch("CTX", [P, TT, CC]), per_batch("CTXT", [P, T])
        stats, moments = sb("stats", [P, TT, 6]), sb("moments", [P, TT, 2])
        variance, rstd = sb("variance", [P, TT]), sb("rstd", [P, TT])

        OB = sb("OB", [P, 8, T])
        VB = per_batch("VB", [P, TT, 1024])
        PB, PT = sb("PB", [P, RING, 4, T]), sb("PT", [P, 3, 2, TT * T])
        negmax, sums, inverse = (sb(n, [P, 4, 4]) for n in ("negmax", "sums", "inverse"))

        arena_at = nc.sbuf_base() if callable(nc.sbuf_base) else nc.sbuf_base
        arena_at = -(-arena_at // 64) * 64
        sb("arena", [P, 16 * 1024 + 16])

        def arena(name, word, shape, dt=fp32):
            return nc.alloc_sbuf_tensor_at(name, shape, dt, offset=arena_at + 4 * word)

        SQ = [arena(f"stacked_q{b}", 4096 * b, [96, HEADS, T], f32r) for b in range(PAIR)]
        SK = [arena(f"stacked_k{b}", 8192 + 4096 * b, [96, HEADS, T], f32r) for b in range(PAIR)]
        QC = [arena(f"causal_q{b}", 2048 * b, [P, 8, T]) for b in range(PAIR)]
        KC = [arena(f"causal_k{b}", (12288, 4096)[b], [P, HEADS, T]) for b in range(PAIR)]
        for n, at in (("ffn0_w1", 0), ("ffn0_w2", 4096), ("ffn1_w1", 0), ("ffn1_w2", 4096)):
            W[n] = arena(n, at, list(EXPERT_WEIGHTS[n]))
        he = arena("expert_hidden", 8192, [P, 2048])
        router_scratch = [arena(f"router_scratch{b}", 10240 + 1024 * b, [P, 1024]) for b in range(PAIR)]
        pwt = arena("weights_by_slot", 10240, [P, 2048])
        slots = arena("slot_tokens", 12288, [P, 2048])
        k_hi = sb("k_hi", [P, 4, T])

        def values(at, b, t, lo, hi):
            w = HEADS * at["d"]
            return VB[b][:, :, :].rearrange("p t n -> p (t n)")[:, t * w + lo:t * w + hi]

        vb = [VB[b][:, :, :].rearrange("p t n -> p (t n)") for b in range(PAIR)]

        def carve(flat, at, *shape):
            size = int(np.prod(shape))
            v = flat[:, at:at + size]
            if len(shape) == 2:
                v = v.rearrange("p (a b) -> p a b", b=shape[1])
            if len(shape) == 3:
                v = v.rearrange("p (a b c) -> p a b c", b=shape[1], c=shape[2])
            return v

        QS = [carve(vb[b], 0, TT, C) for b in range(PAIR)]
        QN = [carve(vb[b], 256, TT, C) for b in range(PAIR)]
        K0B = [carve(vb[b], 512, TT, C) for b in range(PAIR)]
        V0B = [carve(vb[b], 768, TT, C + 1) for b in range(PAIR)]
        CM = [carve(vb[b], 1040, 3, C + HEADS) for b in range(PAIR)]
        QT = [carve(vb[b], 1500, T) for b in range(PAIR)]
        OT = [carve(vb[b], 1760, T) for b in range(PAIR)]
        small0 = per_batch("small", [P, 200])
        HB = [OB[:, 4 * b:4 * b + 4, :] for b in range(PAIR)]
        HE = [carve(he, 512 * k, 2, T) for k in range(4)]
        halves = {"q_hi": OB[:, 4:8, :], "q_lo": carve(vb[0], 1024, 4, T), "k_hi": k_hi, "k_lo": carve(vb[1], 1024, 4, T)}
        PM = [carve(vb[b], 0, TT, E1, SLOT) for b in range(PAIR)]
        PW = [carve(vb[b], 1024, TT, E1, SLOT) for b in range(PAIR)]
        PWT = [carve(pwt, 1024 * b, 4, T) for b in range(PAIR)]
        HX = [carve(he, 512 * k, 8, SLOT) for k in range(4)]
        BUF = [carve(slots, 512 * b, E1 * SLOT) for b in range(PAIR)]
        YB = [carve(slots, 1024 + 512 * b, 4, C) for b in range(PAIR)]

        scratch = [router_scratch[b][:, :] for b in range(PAIR)]
        shifted0 = [carve(scratch[b], 0, TT, E0) for b in range(PAIR)]
        expd0 = [carve(scratch[b], 32, TT, E0) for b in range(PAIR)]
        combine0 = [carve(scratch[b], 64, TT, E0) for b in range(PAIR)]
        onehot0 = [scratch[b][:, 96:96 + TT * K0 * E0].rearrange("p (t k e) -> p t k e", k=K0, e=E0) for b in range(PAIR)]
        combT = [carve(scratch[b], 256, T) for b in range(PAIR)]
        shifted1, expd1, chosen1 = ([carve(small0[b][:, :], at, TT, E1) for b in range(PAIR)] for at in (0, 16, 32))
        onehot1 = [small0[b][:, 48:80].rearrange("p (t k e) -> p t k e", k=2, e=E1) for b in range(PAIR)]
        top8 = [carve(small0[b][:, :], 128, TT, 8) for b in range(PAIR)]
        one, two = ([small0[b][:, at:at + TT] for b in range(PAIR)] for at in (160, 162))
        index8 = [sb(f"index8_{b}", [P, TT, 8], u32) for b in range(PAIR)]

        SC = [ctx.enter_context(nc.psum_tensor(f"SC{k}", [P, 2, TT, T], fp32)) for k in range(2)]
        G = [ctx.enter_context(nc.psum_tensor(f"G{k}", [P, 512], fp32)) for k in range(4)]

        weights_in = {n: ctx.enter_context(nc.semaphore("in_" + n)) for n in WEIGHTS}
        consts_in = ctx.enter_context(nc.semaphore("consts_in"))
        masks_made = ctx.enter_context(nc.semaphore("masks_made"))
        tables_in = ctx.enter_context(nc.semaphore("tables_in"))

        per_pass = []

        def sem(name):
            per_pass.append(ctx.enter_context(nc.semaphore(name)))
            return per_pass[-1]

        x_in = [sem(f"x_in{b}") for b in range(PAIR)]
        out_stored = sem("out_stored")
        bank_filled = [sem(f"bank_filled{k}") for k in range(4)]
        bank_emptied = [sem(f"bank_emptied{k}") for k in range(4)]
        dve_chain = sem("dve_chain")
        pool_chain = sem("pool_chain")
        variance_ready, rstd_ready = sem("variance_ready"), sem("rstd_ready")
        z_ready = sem("z_ready")
        u_ready = sem("u_ready")
        bias_ready = sem("bias_ready")
        kv_drawn, q_exp, q_normal = sem("kv_drawn"), sem("q_exp"), sem("q_normal")
        hi_ready = sem("hi_ready")
        stacked = [sem(f"stacked{u}") for u in range(4)]
        experts_in = [[sem(f"experts{f}_in{g}") for g in range(PARTS_OF_EXPERTS)] for f in range(2)]
        zero_rows = sem("zero_rows")
        scores_ready, max_ready, exp_ready = sem("scores_ready"), sem("max_ready"), sem("exp_ready")
        inverse_ready, probs_ready = sem("inverse_ready"), sem("probs_ready")
        logits_shifted, logits_exp = sem("logits_shifted"), sem("logits_exp")
        chosen_ready, dispatch_ready = sem("chosen_ready"), sem("dispatch_ready")
        hidden_ready = sem("hidden_ready")
        zeroed = sem("zeroed")
        final_ready = sem("final_ready")

        def stacking(a, b):
            return {0: 0, 1: 1, 3: 2}[a] * PAIR + b

        tile_number = {}

        def fill(pe, key):
            n = tile_number[key] = len(tile_number)
            if n >= 4:
                pe.wait_ge(bank_emptied[n % 4], n // 4)
            return G[n % 4]

        def filled(key):
            return bank_filled[tile_number[key] % 4], 1

        def wait_filled(eng, key):
            n = tile_number[key]
            eng.wait_ge(bank_filled[n % 4], n // 4 + 1)
            return G[n % 4]

        def emptied(key):
            return bank_emptied[tile_number[key] % 4], 1

        def wait_emptied(eng, key):
            n = tile_number[key]
            eng.wait_ge(bank_emptied[n % 4], n // 4 + 1)

        def load_weights(act):
            act.dma_start(consts[:, :], A["consts"]).then_inc(consts_in, 16)
            for n in WEIGHTS:
                act.dma_start(W[n][:, :], A[n]).then_inc(weights_in[n], 16)
                if n == "qkv":
                    act.dma_start(rows[:, :], A["rows"].partition_broadcast(P)).then_inc(tables_in, 16)
                    act.dma_start(cols[:, :], A["cols"]).then_inc(tables_in, 16)

        def make_masks(dve):
            dve.wait_ge(consts_in, 16)
            nc.vector.tensor_copy(ident16[:, :], ident).then_inc(masks_made, 1)
            nc.vector.tensor_copy(masked16[:, :], const("masked")).then_inc(masks_made, 1)

        load_weights(nc.scalar)
        make_masks(nc.vector)

        with nc.Fori(0, BATCHES // PAIR) as it:
            with nc.Block() as block:

                @block.tensor
                def _(pe):
                    mm = nc.tensor.matmul

                    def transposed(key, src, width, wait):
                        wait()
                        g = fill(pe, key)
                        for t in range(TT):
                            last = nc.tensor.transpose(g[0:width, t * P:(t + 1) * P], src[:, t, :], ident)
                        last.then_inc(*filled(key))

                    def z_transposed(n, b, src=None, width=C):
                        transposed(("T", n, b), Z[b] if src is None else src, width, lambda: pe.wait_ge(z_ready, n))

                    pe.wait_ge(consts_in, 16)
                    pe.wait_ge(masks_made, 2)
                    pe.wait_ge(tables_in, 32)

                    pe.wait_ge(weights_in["qkv"], 16)
                    for b in range(PAIR):
                        pe.wait_ge(x_in[b], 64)
                        for t in range(TT):
                            g = fill(pe, ("qkv", b, t))
                            mm(g[:, 0:3 * C], XN[b][:, t * P:(t + 1) * P], W["qkv"][:, :], start=True, stop=True)\
                                .then_inc(*filled(("qkv", b, t)))
                    for b in range(PAIR):
                        for t in range(TT):
                            wait_emptied(pe, ("qkv", b, t))
                        pe.wait_ge(zeroed, b + 1)
                        g = fill(pe, ("ctx", b))
                        w = C + 1
                        half = slice(0, BUCKET)
                        mm(g[:, 0:w], K0B[b][half, 0, :], V0B[b][half, 0, :], start=True, stop=True)
                        mm(g[:, w:2 * w], K0B[b][:, 0, :], V0B[b][:, 0, :], start=True, stop=True)
                        mm(g[:, 2 * w:3 * w], K0B[b][:, 0, :], V0B[b][:, 0, :], start=True, stop=False)
                        mm(g[:, 2 * w:3 * w], K0B[b][half, 1, :], V0B[b][half, 1, :], start=False, stop=True)\
                            .then_inc(*filled(("ctx", b)))
                        transposed(("qT", b), QN[b], C, lambda: pe.wait_ge(q_normal, b + 1))
                    for b in range(PAIR):
                        wait_emptied(pe, ("qT", b))
                        wait_emptied(pe, ("ctx", b))
                        g = fill(pe, ("num", b))
                        w = C + HEADS
                        for n in (1, 2, 3):
                            r, t = BUCKET * (n % 2), n // 2
                            last = mm(g[r:r + BUCKET, t * w:(t + 1) * w], QT[b][:, n * BUCKET:(n + 1) * BUCKET],
                                      CM[b][:, n - 1, :], start=True, stop=True)
                        last.then_inc(*filled(("num", b)))
                    for b in range(PAIR):
                        transposed(("oT", b), Z[b], C, lambda: wait_emptied(pe, ("num", b)))
                    pe.wait_ge(weights_in["wout"], 16)
                    for b in range(PAIR):
                        wait_emptied(pe, ("oT", b))
                        g = fill(pe, ("wout", b))
                        for t in range(TT):
                            last = mm(g[:, t * C:(t + 1) * C], OT[b][:, t * P:(t + 1) * P], W["wout"][:, :],
                                      start=True, stop=True)
                        last.then_inc(*filled(("wout", b)))

                    def project(a, at, b):
                        name, chunks = at["name"], HEADS * at["d"] // P
                        kv = CTXT[b] if name == "lx" else XN[b] if name == "l1" else YN[b]
                        for n in {0: (1 + b,), 1: (5 + 2 * b, 6 + 2 * b), 2: (13 + b,), 3: (15 + b,)}[a]:
                            wait_emptied(pe, ("T", n, b))
                        kr = slice(0, CC) if name == "a2" else slice(CC, P) if name == "lx" else slice(0, C)
                        for w in ("wq", "wk", "wv"):
                            pe.wait_ge(weights_in[at[w]], 16)
                        for side, src, kp in (("k", kv, kr), ("q", XN[b], slice(0, C))):
                            w = W[at["w" + side]]
                            for m in range(chunks // 2):
                                g = fill(pe, (side, a, b, m))
                                for k in range(2):
                                    c = 2 * m + k
                                    last = mm(g[:, k * T:(k + 1) * T], w[kp, c * P:(c + 1) * P], src[kp, :],
                                              start=True, stop=True)
                                last.then_inc(*filled((side, a, b, m)))
                        for t in range(TT):
                            for h in range(chunks // 4):
                                g = fill(pe, ("v", a, b, t, h))
                                mm(g[:, :], kv[kr, t * P:(t + 1) * P], W[at["wv"]][kr, h * 512:(h + 1) * 512],
                                   start=True, stop=True).then_inc(*filled(("v", a, b, t, h)))

                    def head(at, i, j):
                        b, h = i // HALVES, 2 * (i % HALVES) + j
                        return b, h * at["d"] // P, h * at["d"] % P

                    def scores(a, at, i):
                        n = a * STEPS + i
                        b = i // HALVES
                        if at["kind"] == "causal" and i % HALVES == 0:
                            pe.wait_ge(zero_rows, b + 1)
                            for m in range(4):
                                wait_emptied(pe, ("k", a, b, m))
                                wait_emptied(pe, ("q", a, b, m))
                        if at["kind"] != "causal" and i % 2 == 0:
                            pe.wait_ge(stacked[i % HALVES // 2], 96 * (stacking(a, b) + 1))
                        if n >= 2:
                            pe.wait_ge(exp_ready, n - 1)
                        s = SC[n % 2]
                        for j in range(2):
                            _, c, r = head(at, i, j)
                            h = 2 * (i % HALVES) + j
                            for t in range(TT):
                                qs, w = slice(t * P, (t + 1) * P), (t + 1) * P
                                if at["kind"] == "causal":
                                    mm(s[:, j, t, 0:w], QC[b][:, c, qs], KC[b][:, h, 0:w], start=True, stop=False)
                                    last = mm(s[:, j, t, qs], ident16[:, :], masked16[:, :], start=False, stop=True)
                                else:
                                    last = mm(s[:, j, t, :], SQ[b][:, h, qs], SK[b][:, h, :], start=True, stop=True)
                        last.then_inc(scores_ready, 1)

                    def transpose_probs(a, at, i):
                        n = a * STEPS + i
                        pe.wait_ge(probs_ready, n + 1)
                        for j in range(2):
                            g = fill(pe, ("PT", a, i, j))
                            for k, (kt, qt) in enumerate(BLOCKS[at["kind"]]):
                                last = nc.tensor.transpose(g[:, k * P:(k + 1) * P],
                                                           PB[:, n % RING, 2 * j + qt, kt * P:(kt + 1) * P], ident)
                            last.then_inc(*filled(("PT", a, i, j)))

                    def weighted_values(a, at, u):
                        d, b = at["d"], (2 * u) // HALVES
                        for i in (2 * u, 2 * u + 1):
                            for j in range(2):
                                wait_emptied(pe, ("PT", a, i, j))
                        if u % (HALVES // 2) == 0:
                            for t in range(TT):
                                for h in range(HEADS * d // 512):
                                    wait_emptied(pe, ("v", a, b, t, h))
                        g = fill(pe, ("O", a, u))
                        sides = [(0, 1, 2, 3)] if d == 32 else [(0, 1), (2, 3)]
                        for side, (first, kt, at_col, q0, width) in [(x, y) for x in sides for y in PARTS[at["kind"]]]:
                            for k in side:
                                i, j = 2 * u + k // 2, k % 2
                                _, c, r = head(at, i, j)
                                h = 2 * (i % HALVES) + j
                                half = (k // 2) * T if d == 64 else 0
                                last = mm(g[r:r + d, half + q0:half + q0 + width], values(at, b, kt, h * d, (h + 1) * d),
                                          PT[:, (a * STEPS + i) % 3, j, at_col:at_col + width],
                                          start=first, stop=not first)
                        last.then_inc(*filled(("O", a, u)))

                    def project_out(a, at, b):
                        chunks = HEADS * at["d"] // P
                        pe.wait_ge(weights_in[at["wo"]], 16)
                        for u in range(b * HALVES // 2, (b + 1) * HALVES // 2):
                            wait_emptied(pe, ("O", a, u))
                        g = fill(pe, ("x", a, b))
                        for t in range(TT):
                            for c in range(chunks):
                                last = mm(g[:, t * C:(t + 1) * C], OB[:, c, t * P:(t + 1) * P],
                                          W[at["wo"]][:, c * C:(c + 1) * C], start=c == 0, stop=c == chunks - 1)
                        last.then_inc(*filled(("x", a, b)))

                    def attention(a, before):
                        at = ATTENTIONS[a]
                        before(0)
                        project(a, at, 0)
                        before(1)
                        for st in range(STEPS + LAG + 1):
                            if st == SECOND_AT:
                                project(a, at, 1)
                            if st < STEPS:
                                scores(a, at, st)
                            i = st - LAG
                            if 0 <= i < STEPS:
                                transpose_probs(a, at, i)
                            if i >= 1 and i % 2 == 0:
                                weighted_values(a, at, i // 2 - 1)
                            if i == HALVES + 1:
                                project_out(a, at, 0)
                        project_out(a, at, 1)

                    def mlp(a, n):
                        name = ATTENTIONS[a]["name"]
                        pe.wait_ge(weights_in[name + "_li2"], 16)
                        pe.wait_ge(weights_in[name + "_li3"], 16)
                        for b in range(PAIR):
                            z_transposed(n + b, b)
                            wait_emptied(pe, ("T", n + b, b))
                            for m in range(2):
                                g = fill(pe, ("li2", a, b, m))
                                for k in range(2):
                                    c = 2 * m + k
                                    last = mm(g[:, k * T:(k + 1) * T], W[name + "_li2"][:, c * P:(c + 1) * P], XN[b][:, :],
                                              start=True, stop=True)
                                last.then_inc(*filled(("li2", a, b, m)))
                            for m in range(2):
                                wait_emptied(pe, ("li2", a, b, m))
                            g = fill(pe, ("li3", a, b))
                            for t in range(TT):
                                for c in range(4):
                                    last = mm(g[:, t * C:(t + 1) * C], HB[b][:, c, t * P:(t + 1) * P],
                                              W[name + "_li3"][:, c * C:(c + 1) * C], start=c == 0, stop=c == 3)
                            last.then_inc(*filled(("li3", a, b)))

                    attention(0, lambda b: z_transposed(1 + b, b))
                    mlp(0, 3)
                    attention(1, lambda b: (z_transposed(5 + 2 * b, b),
                                            z_transposed(6 + 2 * b, b, BIASED[b][:, :, 0:CC], CC)))
                    mlp(1, 9)

                    pe.wait_ge(weights_in["router"], 16)
                    for b in range(PAIR):
                        z_transposed(11 + b, b, X[b])
                        wait_emptied(pe, ("T", 11 + b, b))
                        g = fill(pe, ("r0", b))
                        for t in range(TT):
                            last = mm(g[:, t * E0:(t + 1) * E0], XN[b][:, t * P:(t + 1) * P], W["router"][:, :],
                                      start=True, stop=True)
                        last.then_inc(*filled(("r0", b)))

                    def up0(i):
                        e, b = i // PAIR, i % PAIR
                        if i % (PAIR * E0 // PARTS_OF_EXPERTS) == 0:
                            pe.wait_ge(experts_in[0][e * PARTS_OF_EXPERTS // E0], 32)
                        g = fill(pe, ("up", e, b))
                        for f in range(2):
                            last = mm(g[:, f * T:(f + 1) * T], W["ffn0_w1"][:, e * I0 + f * P:e * I0 + (f + 1) * P],
                                      XN[b][:, :], start=True, stop=True)
                        last.then_inc(*filled(("up", e, b)))

                    def down0(i):
                        e, b = i // PAIR, i % PAIR
                        wait_emptied(pe, ("up", e, b))
                        g = fill(pe, ("down", e, b))
                        for t in range(TT):
                            for f in range(2):
                                k = (2 * e + f) * C
                                last = mm(g[:, t * C:(t + 1) * C], HE[i % 4][:, f, t * P:(t + 1) * P],
                                          W["ffn0_w2"][:, k:k + C], start=f == 0, stop=f == 1)
                        last.then_inc(*filled(("down", e, b)))

                    pe.wait_ge(weights_in["ffn0_b2"], 16)
                    up0(0)
                    up0(1)
                    for b in range(PAIR):
                        pe.wait_ge(chosen_ready, b + 1)
                        g = fill(pe, ("cT", b))
                        for t in range(TT):
                            last = nc.tensor.transpose(g[0:E0, t * P:(t + 1) * P], combine0[b][:, t, :], ident)
                        last.then_inc(*filled(("cT", b)))
                    for b in range(PAIR):
                        wait_emptied(pe, ("cT", b))
                        g = fill(pe, ("b2", b))
                        for t in range(TT):
                            last = mm(g[:, t * C:(t + 1) * C], combT[b][0:E0, t * P:(t + 1) * P],
                                      W["ffn0_b2"][:, :], start=True, stop=True)
                        last.then_inc(*filled(("b2", b)))
                    for i in range(PAIR * E0):
                        if i + 2 < PAIR * E0:
                            up0(i + 2)
                        down0(i)

                    attention(2, lambda b: z_transposed(13 + b, b, X[b]))
                    attention(3, lambda b: z_transposed(15 + b, b, X[b]))

                    pe.wait_ge(weights_in["router1"], 16)
                    for b in range(PAIR):
                        z_transposed(17 + b, b, X[b])
                        wait_emptied(pe, ("T", 17 + b, b))
                        g = fill(pe, ("r1", b))
                        for t in range(TT):
                            last = mm(g[:, t * E1:(t + 1) * E1], XN[b][:, t * P:(t + 1) * P], W["router1"][:, :],
                                      start=True, stop=True)
                        last.then_inc(*filled(("r1", b)))
                    for b in range(PAIR):
                        pe.wait_ge(chosen_ready, PAIR + b + 1)
                        g = fill(pe, ("pos", b))
                        mm(g[:, 0:E1], const("earlier"), chosen1[b][:, 0, :], start=True, stop=True)
                        mm(g[:, E1:2 * E1], const("later_key")[:, P:2 * P], chosen1[b][:, 0, :], start=True, stop=False)
                        mm(g[:, E1:2 * E1], const("earlier"), chosen1[b][:, 1, :], start=False, stop=True)\
                            .then_inc(*filled(("pos", b)))
                    for b in range(PAIR):
                        pe.wait_ge(dispatch_ready, 2 * b + 1)
                        g = fill(pe, ("buf", b))
                        for t in range(TT):
                            last = mm(g[:, :], X[b][:, t, :], PM[b][:, t, :, :].rearrange("p e s -> p (e s)"),
                                      start=t == 0, stop=t == TT - 1)
                        last.then_inc(*filled(("buf", b)))
                        pe.wait_ge(dispatch_ready, 2 * b + 2)
                        for m in range(2):
                            g = fill(pe, ("PWT", b, m))
                            for k in range(2):
                                for t in range(TT):
                                    p2 = 2 * (2 * m + k)
                                    last = nc.tensor.transpose(
                                        g[:, k * T + t * P:k * T + (t + 1) * P],
                                        PW[b][:, t, p2:p2 + 2, :].rearrange("p e s -> p (e s)"), ident)
                            last.then_inc(*filled(("PWT", b, m)))

                    def up1(i):
                        b, m = i // 4, i % 4
                        if m == 0:
                            wait_emptied(pe, ("buf", b))
                        if b == 0:
                            pe.wait_ge(experts_in[1][m], 32)
                        g = fill(pe, ("up1", b, m))
                        for k in range(2):
                            e = 2 * m + k
                            for f in range(4):
                                s = (4 * k + f) * SLOT
                                last = mm(g[:, s:s + SLOT], W["ffn1_w1"][:, e * I1 + f * P:e * I1 + (f + 1) * P],
                                          BUF[b][:, e * SLOT:(e + 1) * SLOT], start=True, stop=True)
                        last.then_inc(*filled(("up1", b, m)))

                    def down1(i):
                        b, m = i // 4, i % 4
                        pe.wait_ge(hidden_ready, i + 1)
                        g = fill(pe, ("y", b, m))
                        for f in range(4):
                            for k in range(2):
                                w = (4 * (2 * m + k) + f) * C
                                last = mm(g[k * SLOT:(k + 1) * SLOT, 0:C], HX[i % 4][:, 4 * k + f, :],
                                          W["ffn1_w2"][:, w:w + C], start=f == 0, stop=f == 3)
                        last.then_inc(*filled(("y", b, m)))

                    for i in range(4 * PAIR + 1):
                        if i < 4 * PAIR:
                            up1(i)
                        if i >= 1:
                            down1(i - 1)
                    for b in range(PAIR):
                        for m in range(2):
                            wait_emptied(pe, ("PWT", b, m))
                        for m in range(4):
                            wait_emptied(pe, ("y", b, m))
                        g = fill(pe, ("comb", b))
                        for t in range(TT):
                            for m in range(4):
                                last = mm(g[:, t * C:(t + 1) * C], PWT[b][:, m, t * P:(t + 1) * P], YB[b][:, m, :],
                                          start=m == 0, stop=m == 3)
                        last.then_inc(*filled(("comb", b)))

                @block.scalar
                def _(act):
                    fn = nc.scalar.activation

                    def copied(key, dst, src, scale=1.0):
                        g = wait_filled(act, key)
                        fn(dst, src(g), ACT.Copy, scale=scale).then_inc(*emptied(key))

                    def affine(n, b, dst, g_name, b_name, p=P):
                        g = wait_filled(act, ("T", n, b))
                        fn(dst[0:p, :], g[0:p, 0:T], ACT.Identity, scale=col(g_name, p=p), bias=col(b_name, p=p))\
                            .then_inc(*emptied(("T", n, b)))

                    act.wait_ge(tables_in, 32)
                    for b in range(PAIR):
                        for t in range(TT):
                            g = wait_filled(act, ("qkv", b, t))
                            fn(K0B[b][:, t, :], g[:, C:2 * C], ACT.Exp)
                            fn(V0B[b][:, t, 0:C], g[:, 2 * C:3 * C], ACT.Copy).then_inc(kv_drawn, 1)
                    for b in range(PAIR):
                        for t in range(TT):
                            wait_emptied(act, ("qkv", b, t))
                            fn(QN[b][:, t, :], QS[b][:, t, :], ACT.Exp).then_inc(q_exp, 1)
                    for b in range(PAIR):
                        copied(("qT", b), QT[b], lambda g: g[:, 0:T])
                    for b in range(PAIR):
                        copied(("oT", b), OT[b], lambda g: g[:, 0:T])

                    def project(a, at, b):
                        chunks, stacks = HEADS * at["d"] // P, at["kind"] != "causal"
                        if stacks and stacking(a, b) >= 1:
                            for u in range(4):
                                act.wait_ge(stacked[u], 96 * stacking(a, b))
                        for side in ("k", "q") if stacks else ():
                            for m in range(2):
                                g = wait_filled(act, (side, a, b, m))
                                hi = halves[side + "_hi"]
                                if at["name"] == "lx":
                                    for k in range(2):
                                        last = fn(hi[:, 2 * m + k, :].bitcast(f32r), g[:, k * T:(k + 1) * T], ACT.Identity,
                                                  bias=col("b" + side, 2 * m + k))
                                else:
                                    last = fn(hi[:, 2 * m:2 * m + 2, :].rearrange("p a b -> p (a b)").bitcast(f32r),
                                              g[:, :], ACT.Copy, scale=at["scale"] if side == "q" else 1.0)
                                last.then_inc(hi_ready, 1)
                        if not stacks:
                            for m in range(4):
                                copied(("q", a, b, m), QC[b][:, 2 * m:2 * m + 2, :].rearrange("p a b -> p (a b)"),
                                       lambda g: g[:, :], at["scale"])
                        if at["name"] != "lx":
                            for h in range(chunks // 4):
                                copied(("v", a, b, 0, h), values(at, b, 0, h * 512, (h + 1) * 512), lambda g: g[:, :])

                    def exponentials(a, at, i):
                        n = a * STEPS + i
                        if i >= RING:
                            wait_filled(act, ("PT", a, i - RING, 1))
                        act.wait_ge(max_ready, n + 1)
                        for k in range(4):
                            j, t = k // 2, k % 2
                            w = (t + 1) * P if at["kind"] == "causal" else T
                            last = fn(PB[:, n % RING, k, 0:w], SC[n % 2][:, j, t, 0:w], ACT.Exp,
                                      scale=at["scale"] if at["name"] == "lx" else 1.0, bias=negmax[:, n % 4, k:k + 1], accum_out=sums[:, n % 4, k:k + 1])
                        last.then_inc(exp_ready, 1)

                    def attention(a, before):
                        at = ATTENTIONS[a]
                        before(0)
                        project(a, at, 0)
                        before(1)
                        for st in range(STEPS + LAG + 1):
                            if st == SECOND_AT:
                                project(a, at, 1)
                            if st < STEPS:
                                exponentials(a, at, st)
                            i = st - LAG
                            if 0 <= i < STEPS and at["kind"] != "keep_later":
                                w = len(BLOCKS[at["kind"]]) * P
                                copied(("PT", a, i, 1), PT[:, (a * STEPS + i) % 3, 1, 0:w], lambda g: g[:, 0:w])
                            if i >= 1 and i % 2 == 0:
                                u = i // 2 - 1
                                ub = u % (HALVES // 2)
                                if u == HALVES // 2:
                                    wait_filled(act, ("x", a, 0))
                                if at["d"] == 64:
                                    copied(("O", a, u), OB[:, 2 * ub:2 * ub + 2, :].rearrange("p a b -> p (a b)"),
                                           lambda g: g[:, :])
                                else:
                                    copied(("O", a, u), OB[:, ub, :], lambda g: g[:, 0:T])

                    def mlp(a, n):
                        name = ATTENTIONS[a]["name"]
                        for b in range(PAIR):
                            affine(n + b, b, XN[b], name + "_ln3_g", name + "_ln3_b")
                            for m in range(2):
                                g = wait_filled(act, ("li2", a, b, m))
                                for k in range(2):
                                    c = 2 * m + k
                                    last = fn(HB[b][:, c, :], g[:, k * T:(k + 1) * T], ACT.Gelu,
                                              bias=col(name + "_li2_b", c))
                                last.then_inc(*emptied(("li2", a, b, m)))

                    def self_operands(b):
                        g = wait_filled(act, ("T", 1 + b, b))
                        fn(XN[b][:, :], g[:, 0:T], ACT.Identity, scale=col("a1_lnx_g"), bias=col("a1_lnx_b"))
                        fn(YN[b][:, :], g[:, 0:T], ACT.Identity, scale=col("a1_lny_g"), bias=col("a1_lny_b"))\
                            .then_inc(*emptied(("T", 1 + b, b)))
                    def cross_operands(b):
                        affine(5 + 2 * b, b, XN[b], "a2_lnx_g", "a2_lnx_b")
                        affine(6 + 2 * b, b, YN[b], "a2_lny_g", "a2_lny_b", CC)

                    attention(0, self_operands)
                    mlp(0, 3)
                    attention(1, cross_operands)
                    mlp(1, 9)

                    for b in range(PAIR):
                        copied(("T", 11 + b, b), XN[b][:, :], lambda g: g[:, 0:T])
                    for b in range(PAIR):
                        act.wait_ge(logits_shifted, b + 1)
                        fn(expd0[b], shifted0[b], ACT.Exp).then_inc(logits_exp, 1)

                    def gelu_up(i):
                        e, b = i // PAIR, i % PAIR
                        g = wait_filled(act, ("up", e, b))
                        if i >= 4:
                            wait_filled(act, ("down", (i - 4) // PAIR, b))
                        for f in range(2):
                            last = fn(HE[i % 4][:, f, :], g[:, f * T:(f + 1) * T], ACT.Gelu,
                                      bias=col("ffn0_b1", 2 * e + f))
                        last.then_inc(*emptied(("up", e, b)))

                    gelu_up(0)
                    gelu_up(1)
                    for b in range(PAIR):
                        copied(("cT", b), combT[b][0:E0, :], lambda g: g[0:E0, 0:T])
                    for i in range(2, PAIR * E0):
                        gelu_up(i)

                    attention(2, lambda b: copied(("T", 13 + b, b), XN[b][:, :], lambda g: g[:, 0:T]))
                    attention(3, lambda b: copied(("T", 15 + b, b), XN[b][:, :], lambda g: g[:, 0:T]))

                    for b in range(PAIR):
                        copied(("T", 17 + b, b), XN[b][:, :], lambda g: g[:, 0:T])
                    for b in range(PAIR):
                        act.wait_ge(logits_shifted, PAIR + b + 1)
                        fn(expd1[b], shifted1[b], ACT.Exp).then_inc(logits_exp, 1)
                    for b in range(PAIR):
                        copied(("buf", b), BUF[b], lambda g: g[:, :])
                        for m in range(2):
                            copied(("PWT", b, m), PWT[b][:, 2 * m:2 * m + 2, :].rearrange("p a b -> p (a b)"),
                                   lambda g: g[:, :])
                    for i in range(4 * PAIR):
                        wait_emptied(act, ("up1", i // 4, i % 4))
                        fn(HX[i % 4], HX[i % 4], ACT.Relu).then_inc(hidden_ready, 1)

                @block.vector
                def _(dve):
                    v = nc.vector
                    links = [0]

                    def link(ins):
                        links[0] += 1
                        ins.then_inc(dve_chain, 1)
                        dve.wait_ge(dve_chain, links[0])

                    norms = [0]

                    def layernorm(src, dst, width=C):
                        norms[0] += 1
                        for t in range(TT):
                            last = v.bn_stats(stats[:, t, :], src[:, t, 0:width])
                        link(last)
                        for t in range(TT):
                            last = v.bn_aggr(moments[:, t, :], stats[:, t, :])
                        link(last)
                        v.tensor_scalar(variance[:, :], moments[:, :, 1], EPS, None, ALU.add).then_inc(variance_ready, 1)
                        dve.wait_ge(rstd_ready, norms[0])
                        for t in range(TT):
                            last = v.tensor_scalar(dst[:, t, 0:width], src[:, t, 0:width], moments[:, t, 0:1],
                                                   rstd[:, t:t + 1], ALU.subtract, ALU.mult)
                        return last

                    def over_tiles(vec):
                        return vec.unsqueeze(1).to_broadcast([P, TT, C])

                    def gain_bias(x, g_name, b_name):
                        link(v.tensor_tensor(x[:, :, :], x[:, :, :], over_tiles(row(g_name)), ALU.mult))
                        return v.tensor_tensor(x[:, :, :], x[:, :, :], over_tiles(row(b_name)), ALU.add)

                    def residual(key, dst, other):
                        g = wait_filled(dve, key)
                        v.tensor_tensor(dst[:, :, :], g[:, 0:TT * C].rearrange("p (t c) -> p t c", c=C),
                                        other[:, :, :], ALU.add).then_inc(*emptied(key))
                        wait_emptied(dve, key)

                    dve.wait_ge(consts_in, 16)
                    dve.wait_ge(tables_in, 32)
                    heads = lambda x: x.rearrange("p (h d) -> p h d", d=HD0)
                    for b in range(PAIR):
                        dve.wait_ge(x_in[b], 64)
                        for t in range(TT):
                            g = wait_filled(dve, ("qkv", b, t))
                            dve.wait_ge(kv_drawn, TT * b + t + 1)
                            m = small0[b][:, t * HEADS:(t + 1) * HEADS]
                            link(v.tensor_reduce(m, heads(g[:, 0:C]), axis=AX.X, op=ALU.max))
                            v.tensor_tensor(heads(QS[b][:, t, :]), heads(g[:, 0:C]),
                                            m.unsqueeze(2).to_broadcast([P, HEADS, HD0]), ALU.subtract)\
                                .then_inc(*emptied(("qkv", b, t)))
                    for b in range(PAIR):
                        dve.wait_ge(q_exp, TT * (b + 1))
                        flat = QN[b].rearrange("p t c -> p (t c)")
                        s, r = small0[b][:, 32:64], small0[b][:, 64:96]
                        link(v.tensor_reduce(s, heads(flat), axis=AX.X, op=ALU.add))
                        link(v.reciprocal(r, s))
                        link(v.tensor_scalar(s, r, HD0 ** -0.5, None, ALU.mult))
                        v.tensor_tensor(heads(flat), heads(flat), s.unsqueeze(2).to_broadcast([P, TT * HEADS, HD0]),
                                        ALU.mult).then_inc(q_normal, 1)
                        g = wait_filled(dve, ("ctx", b))
                        prod = g[:, 0:3 * (C + 1)].rearrange("p (n c) -> p n c", c=C + 1)
                        v.tensor_tensor(CM[b][:, :, 0:C], prod[:, :, 0:C],
                                        const("same_head").unsqueeze(1).to_broadcast([P, 3, C]), ALU.mult)
                        v.tensor_tensor(CM[b][:, :, C:C + HEADS], prod[:, :, C:C + 1].to_broadcast([P, 3, HEADS]),
                                        const("head_of").unsqueeze(1).to_broadcast([P, 3, HEADS]), ALU.mult)\
                            .then_inc(*emptied(("ctx", b)))
                    for b in range(PAIR):
                        g = wait_filled(dve, ("num", b))
                        dve.wait_ge(zeroed, PAIR + b + 1)
                        for t, r0 in ((0, BUCKET), (1, 0)):
                            tile = g[r0:P, t * (C + HEADS):(t + 1) * (C + HEADS)]
                            s, r = small0[b][r0:P, 96:112], small0[b][r0:P, 112:128]
                            link(v.tensor_scalar(s, tile[:, C:C + HEADS], 1e-6, None, ALU.max))
                            link(v.reciprocal(r, s))
                            last = v.tensor_tensor(heads(Z[b][r0:P, t, :]), heads(tile[:, 0:C]),
                                                   r.unsqueeze(2).to_broadcast([P - r0, HEADS, HD0]), ALU.mult)
                            if t == 0:
                                link(last)
                        last.then_inc(*emptied(("num", b)))
                    def before_self(b):
                        if b == 0:
                            residual(("wout", 0), R[0], X[0])
                        link(layernorm(R[b], X[b]))
                        link(layernorm(X[b], U[b]))
                        gain_bias(U[b], "ln1_g", "ln1_b").then_inc(u_ready, 1)
                        dve.wait_ge(u_ready, b + 1)
                        layernorm(U[b], Z[b]).then_inc(z_ready, 1)
                        if b == 0:
                            residual(("wout", 1), R[1], X[1])

                    def project(a, at, b):
                        chunks, name = HEADS * at["d"] // P, at["name"]
                        for m in range(4) if at["kind"] == "causal" else ():
                            g = wait_filled(dve, ("k", a, b, m))
                            for k in range(2):
                                r = slice(64 * k, 64 * k + 64)
                                last = v.tensor_copy(KC[b][r, 4 * m + k:4 * m + k + 3:2, :],
                                                     g[r, :].rearrange("p (a b) -> p a b", b=T))
                            last.then_inc(*emptied(("k", a, b, m)))
                        for n, side in enumerate(("k", "q")) if at["kind"] != "causal" else ():
                            for m in range(2):
                                g = wait_filled(dve, (side, a, b, m))
                                dve.wait_ge(hi_ready, 4 * stacking(a, b) + 2 * n + m + 1)
                                hi, lo = halves[side + "_hi"], halves[side + "_lo"]
                                for k in range(2):
                                    c = 2 * m + k
                                    if name == "lx":
                                        by, op = col("b" + side, c), ALU.add
                                    else:
                                        by, op = at["scale"] if side == "q" else 1.0, ALU.mult
                                    last = v.scalar_tensor_tensor(lo[:, c, :].bitcast(f32r), g[:, k * T:(k + 1) * T], by,
                                                                  hi[:, c, :], op0=op, op1=ALU.subtract)
                                last.then_inc(*emptied((side, a, b, m)))
                        for t in range(TT):
                            for h in range(chunks // 4):
                                if name == "lx":
                                    g = wait_filled(dve, ("v", a, b, t, h))
                                    v.tensor_tensor(values(at, b, t, 0, 512), g[:, :], row("bv"), ALU.add)\
                                        .then_inc(*emptied(("v", a, b, t, h)))
                                elif t == 1:
                                    g = wait_filled(dve, ("v", a, b, t, h))
                                    v.tensor_copy(values(at, b, t, h * 512, (h + 1) * 512), g[:, :])\
                                        .then_inc(*emptied(("v", a, b, t, h)))

                    def maxima(a, at, i):
                        n = a * STEPS + i
                        dve.wait_ge(scores_ready, n + 1)
                        s = SC[n % 2]
                        m = negmax[:, n % 4, :]
                        if at["kind"] == "causal":
                            mv = m.rearrange("p (j t) -> p j t", t=TT)
                            for t in range(TT):
                                last = v.tensor_reduce(mv[:, :, t], s[:, :, t, 0:(t + 1) * P], axis=AX.X, op=ALU.max,
                                                       negate=True)
                        else:
                            last = v.tensor_reduce(m, s[:, :, :, :].rearrange("p j t k -> p (j t) k"), axis=AX.X,
                                                   op=ALU.max, negate=True)
                        if at["name"] == "lx":
                            link(last)
                            last = v.tensor_scalar(m, m, at["scale"], None, ALU.mult)
                        last.then_inc(max_ready, 1)

                    def inverses(a, i):
                        n = a * STEPS + i
                        dve.wait_ge(exp_ready, n + 1)
                        v.reciprocal(inverse[:, n % 4, :], sums[:, n % 4, :]).then_inc(inverse_ready, 1)

                    def attention_sum(a, b):
                        if a != 2:
                            dve.wait_ge(bias_ready, {0: 0, 1: 2, 3: 4}[a] * PAIR + b + 1)
                        residual(("x", a, b), R[b], X[b] if a == 2 else BIASED[b])

                    def after_norm(a, b):
                        layernorm(R[b], Z[b] if a < 2 else X[b]).then_inc(z_ready, 1)

                    def attention(a, before):
                        at = ATTENTIONS[a]
                        before(0)
                        project(a, at, 0)
                        before(1)
                        for st in range(STEPS + LAG + 1):
                            if st == SECOND_AT:
                                project(a, at, 1)
                            if st < STEPS:
                                maxima(a, at, st)
                            i = st - LAG
                            if 0 <= i < STEPS:
                                if i >= 3:
                                    wait_filled(dve, ("O", a, (i - 3) // 2))
                                for j in ((0, 1) if at["kind"] == "keep_later" else (0,)):
                                    g = wait_filled(dve, ("PT", a, i, j))
                                    w = len(BLOCKS[at["kind"]]) * P
                                    dst = PT[:, (a * STEPS + i) % 3, j, 0:w]
                                    if at["kind"] == "keep_later":
                                        last = v.tensor_tensor(dst, g[:, 0:w], const("later_key"), ALU.mult)
                                    else:
                                        last = v.tensor_copy(dst, g[:, 0:w])
                                    last.then_inc(*emptied(("PT", a, i, j)))
                            if 0 <= st - 1 < STEPS:
                                inverses(a, st - 1)
                            if st == SUM_AT:
                                attention_sum(a, 0)
                                after_norm(a, 0)
                        attention_sum(a, 1)
                        if a != 2:
                            after_norm(a, 1)

                    def context_norm(b):
                        layernorm(CTX[b], BIASED[b], CC).then_inc(z_ready, 1)

                    def before_cross(b):
                        if b == 0:
                            dve.wait_ge(bias_ready, PAIR + 1)
                            residual(("li3", 0, 0), R[0], U[0])
                        link(layernorm(R[b], U[b]))
                        gain_bias(U[b], "ln2_g", "ln2_b").then_inc(u_ready, 1)
                        dve.wait_ge(u_ready, PAIR + b + 1)
                        layernorm(U[b], Z[b]).then_inc(z_ready, 1)
                        context_norm(b)
                        if b == 0:
                            dve.wait_ge(bias_ready, PAIR + 2)
                            residual(("li3", 0, 1), R[1], U[1])

                    attention(0, before_self)
                    attention(1, before_cross)
                    for b in range(PAIR):
                        dve.wait_ge(bias_ready, 3 * PAIR + b + 1)
                        residual(("li3", 1, b), R[b], U[b])
                        layernorm(R[b], X[b]).then_inc(z_ready, 1)

                    def chosen(b, prob, E, top, idx, onehot, sel, k):
                        for t in range(TT):
                            last = v.max(top[:, t, :], prob[:, t, :])
                        link(last)
                        for t in range(TT):
                            last = v.max_index(idx[:, t, :], top[:, t, :], prob[:, t, :])
                        link(last)
                        for t in range(TT):
                            last = v.tensor_tensor(onehot[:, t, :, :], const("iota_e")[:, 0:E].unsqueeze(1)
                                                   .to_broadcast([P, k, E]),
                                                   idx[:, t, 0:k].unsqueeze(2).to_broadcast([P, k, E]), ALU.is_equal)
                        link(last)
                        for t in range(TT):
                            last = v.tensor_reduce(sel[:, t, :], onehot[:, t, :, :].rearrange("p k e -> p e k"),
                                                   axis=AX.X, op=ALU.add)
                        return last

                    def shift(b, shifted, E, one):
                        link(v.tensor_reduce(one, shifted, axis=AX.X, op=ALU.max))
                        v.tensor_tensor(shifted, shifted, one.unsqueeze(2).to_broadcast([P, TT, E]), ALU.subtract)\
                            .then_inc(logits_shifted, 1)

                    for b in range(PAIR):
                        g = wait_filled(dve, ("r0", b))
                        v.tensor_tensor(shifted0[b], g[:, 0:TT * E0].rearrange("p (t e) -> p t e", e=E0),
                                        row("router_b").unsqueeze(1).to_broadcast([P, TT, E0]), ALU.add)\
                            .then_inc(*emptied(("r0", b)))
                        wait_emptied(dve, ("r0", b))
                        shift(b, shifted0[b], E0, one[b])
                    for b in range(PAIR):
                        dve.wait_ge(logits_exp, b + 1)
                        link(chosen(b, expd0[b], E0, top8[b], index8[b], onehot0[b], combine0[b], K0))
                        link(v.tensor_tensor(shifted0[b], combine0[b], expd0[b], ALU.mult))
                        link(v.tensor_reduce(one[b], shifted0[b], axis=AX.X, op=ALU.add))
                        link(v.reciprocal(two[b], one[b]))
                        v.tensor_tensor(combine0[b], shifted0[b], two[b].unsqueeze(2).to_broadcast([P, TT, E0]),
                                        ALU.mult).then_inc(chosen_ready, 1)
                    for b in range(PAIR):
                        residual(("b2", b), R[b], X[b])
                    for i in range(PAIR * E0):
                        e, b = i // PAIR, i % PAIR
                        g = wait_filled(dve, ("down", e, b))
                        if e == 0:
                            dve.wait_ge(chosen_ready, b + 1)
                        else:
                            wait_emptied(dve, ("down", e - 1, b))
                        for t in range(TT):
                            last = v.scalar_tensor_tensor(R[b][:, t, :], g[:, t * C:(t + 1) * C],
                                                          combine0[b][:, t, e:e + 1], R[b][:, t, :],
                                                          op0=ALU.mult, op1=ALU.add)
                        last.then_inc(*emptied(("down", e, b)))

                    def before_causal(b):
                        wait_emptied(dve, ("down", E0 - 1, b))
                        layernorm(R[b], X[b]).then_inc(z_ready, 1)

                    attention(2, before_causal)
                    attention(3, lambda b: after_norm(2, 1) if b == 1 else None)

                    for b in range(PAIR):
                        g = wait_filled(dve, ("r1", b))
                        v.tensor_copy(shifted1[b], g[:, 0:TT * E1].rearrange("p (t e) -> p t e", e=E1))\
                            .then_inc(*emptied(("r1", b)))
                        wait_emptied(dve, ("r1", b))
                        shift(b, shifted1[b], E1, one[b])
                    for b in range(PAIR):
                        dve.wait_ge(logits_exp, PAIR + b + 1)
                        link(v.tensor_reduce(one[b], expd1[b], axis=AX.X, op=ALU.add))
                        link(v.reciprocal(two[b], one[b]))
                        link(v.tensor_tensor(expd1[b], expd1[b], two[b].unsqueeze(2).to_broadcast([P, TT, E1]),
                                             ALU.mult))
                        chosen(b, expd1[b], E1, top8[b], index8[b], onehot1[b], chosen1[b], 2).then_inc(chosen_ready, 1)
                    for b in range(PAIR):
                        g = wait_filled(dve, ("pos", b))
                        dve.wait_ge(chosen_ready, PAIR + b + 1)
                        v.scalar_tensor_tensor(shifted1[b].rearrange("p t e -> p (t e)"), g[:, 0:TT * E1], 1.0,
                                               chosen1[b].rearrange("p t e -> p (t e)"), op0=ALU.add, op1=ALU.mult)\
                            .then_inc(*emptied(("pos", b)))
                        wait_emptied(dve, ("pos", b))
                        for t in range(TT):
                            last = v.tensor_tensor(PM[b][:, t, :, :],
                                                   const("iota_slot").unsqueeze(1).to_broadcast([P, E1, SLOT]),
                                                   shifted1[b][:, t, :].unsqueeze(2).to_broadcast([P, E1, SLOT]),
                                                   ALU.is_equal)
                        last.then_inc(dispatch_ready, 1)
                        dve.wait_ge(dispatch_ready, 2 * b + 1)
                        for t in range(TT):
                            last = v.tensor_tensor(PW[b][:, t, :, :], PM[b][:, t, :, :],
                                                   expd1[b][:, t, :].unsqueeze(2).to_broadcast([P, E1, SLOT]), ALU.mult)
                        last.then_inc(dispatch_ready, 1)
                    dve.wait_ge(weights_in["ffn1_b2"], 16)
                    for i in range(4 * PAIR + 2):
                        if i < 4 * PAIR:
                            b, m = i // 4, i % 4
                            g = wait_filled(dve, ("up1", b, m))
                            if i >= 4:
                                wait_filled(dve, ("y", 0, i - 4))
                            b1 = cols[:, COLS["ffn1_b1"][0] + 8 * m:COLS["ffn1_b1"][0] + 8 * m + 8]
                            v.tensor_tensor(HX[i % 4], g[:, :].rearrange("p (a s) -> p a s", s=SLOT),
                                            b1.unsqueeze(2).to_broadcast([P, 8, SLOT]), ALU.add)\
                                .then_inc(*emptied(("up1", b, m)))
                        if i >= 2:
                            b, m = (i - 2) // 4, (i - 2) % 4
                            g = wait_filled(dve, ("y", b, m))
                            v.tensor_tensor(YB[b][:, m, :], g[:, 0:C], W["ffn1_b2"][:, m * C:(m + 1) * C], ALU.add)\
                                .then_inc(*emptied(("y", b, m)))
                    for b in range(PAIR):
                        residual(("comb", b), R[b], X[b])
                        layernorm(R[b], Z[b]).then_inc(final_ready, 1)

                @block.gpsimd
                def _(pool):
                    v = nc.gpsimd
                    norms, links = [0], [0]

                    def link(ins):
                        links[0] += 1
                        ins.then_inc(pool_chain, 1)
                        pool.wait_ge(pool_chain, links[0])

                    def inverse_deviation(times=1):
                        for _ in range(times):
                            norms[0] += 1
                            pool.wait_ge(variance_ready, norms[0])
                            v.tensor_tensor(rstd[:, :], variance[:, :], const("minus_half"), ALU.pow)\
                                .then_inc(rstd_ready, 1)

                    def plus_row(dst, src, name):
                        return v.tensor_tensor(dst[:, :, :], src[:, :, :],
                                               row(name).unsqueeze(1).to_broadcast([P, TT, C]), ALU.add)

                    pool.wait_ge(consts_in, 16)
                    for b in range(PAIR):
                        v.memset(V0B[b][:, :, C:C + 1], 1.0).then_inc(zeroed, 1)
                    for b in range(PAIR):
                        v.memset(Z[b][0:BUCKET, 0, :], 0.0).then_inc(zeroed, 1)
                    pool.wait_ge(tables_in, 32)

                    def attention(a):
                        at = ATTENTIONS[a]
                        for i in range(STEPS):
                            n = a * STEPS + i
                            if i == SUM_AT:
                                inverse_deviation()
                            pool.wait_ge(inverse_ready, n + 1)
                            inv = inverse[:, n % 4, :]
                            if at["kind"] == "causal":
                                for t in range(TT):
                                    w = (t + 1) * P
                                    p = PB[:, n % RING, :, :].rearrange("p (j t) k -> p j t k", t=TT)[:, :, t, 0:w]
                                    m = inv.rearrange("p (j t) -> p j t", t=TT)[:, :, t:t + 1].to_broadcast([P, 2, w])
                                    last = v.tensor_tensor(p, p, m, ALU.mult)
                            else:
                                p = PB[:, n % RING, :, :]
                                last = v.tensor_tensor(p, p, inv.unsqueeze(2).to_broadcast([P, 4, T]), ALU.mult)
                            last.then_inc(probs_ready, 1)

                    def bias_sums(name, n):
                        pool.wait_ge(u_ready, n)
                        plus_row(BIASED[(n - 1) % PAIR], U[(n - 1) % PAIR], name).then_inc(bias_ready, 1)

                    def mlp_residual(a, b):
                        link(plus_row(U[b], U[b], ("a1_li3_b", "a2_li3_b")[a]))
                        if a == 1:
                            link(v.tensor_tensor(U[b][:, :, :], U[b][:, :, :], X[b][:, :, :], ALU.add))
                        wait_emptied(pool, ("x", a, b))
                        v.tensor_tensor(U[b][:, :, :], U[b][:, :, :], R[b][:, :, :], ALU.add).then_inc(bias_ready, 1)

                    for b in range(PAIR):
                        inverse_deviation(3)
                        bias_sums("a1_li1_b", b + 1)
                    attention(0)
                    mlp_residual(0, 0)
                    inverse_deviation()
                    mlp_residual(0, 1)
                    for b in range(PAIR):
                        inverse_deviation(3)
                        wait_filled(pool, ("T", 6 + 2 * b, b))
                        bias_sums("a2_li1_b", PAIR + b + 1)
                    attention(1)
                    mlp_residual(1, 0)
                    inverse_deviation()
                    mlp_residual(1, 1)
                    for b in range(PAIR):
                        inverse_deviation()

                    def zero_other_rows(b):
                        pool.wait_ge(rstd_ready, norms[0])
                        link(v.memset(KC[b][64:P, 0:HEADS:2, :], 0.0))
                        v.memset(KC[b][0:64, 1:HEADS:2, :], 0.0).then_inc(zero_rows, 1)
                        pool.wait_ge(zero_rows, b + 1)

                    zero_other_rows(0)
                    for b in range(PAIR):
                        inverse_deviation()
                    pool.wait_ge(z_ready, 14)
                    zero_other_rows(1)
                    attention(2)
                    pool.wait_ge(z_ready, 15)
                    plus_row(BIASED[0], X[0], "bo").then_inc(bias_ready, 1)
                    inverse_deviation()
                    pool.wait_ge(z_ready, 16)
                    plus_row(BIASED[1], X[1], "bo").then_inc(bias_ready, 1)
                    attention(3)
                    inverse_deviation()
                    for b in range(PAIR):
                        inverse_deviation()

                @block.sync
                def _(sp):
                    for b in range(PAIR):
                        n = it * PAIR + b
                        sp.dma_start(XN[b][:, :], A["xT"][n]).then_inc(x_in[b], 16)
                        sp.dma_start(X[b][:, :, :], A["x"][n].rearrange("(t p) c -> p t c", p=P)).then_inc(x_in[b], 16)
                        sp.dma_start(CTX[b][:, :, :], A["ctx"][n].rearrange("(t p) c -> p t c", p=P))\
                            .then_inc(x_in[b], 16)
                        sp.dma_start(CTXT[b][CC:P, :], A["ctxT"][n]).then_inc(x_in[b], 16)

                    def stack_halves(a):
                        for b in range(PAIR):
                            for side in ("k", "q"):
                                for m in range(2):
                                    wait_emptied(sp, (side, a, b, m))
                            for u in range(4):
                                for to, parts in ((SQ[b], ("q_hi", "q_hi", "q_lo")), (SK[b], ("k_hi", "k_lo", "k_hi"))):
                                    for n, part in enumerate(parts):
                                        sp.dma_start(to[32 * n:32 * n + 32, 4 * u:4 * u + 4, :].bitcast(fp32),
                                                     halves[part][32 * u:32 * u + 32, :, :])\
                                            .then_inc(stacked[u], 16)

                    def load_experts(f, scores):
                        sp.wait_ge(scores_ready, scores)
                        for g in range(PARTS_OF_EXPERTS):
                            for n in (f"ffn{f}_w1", f"ffn{f}_w2"):
                                w = EXPERT_WEIGHTS[n][1] // PARTS_OF_EXPERTS
                                sp.dma_start(W[n][:, g * w:(g + 1) * w], A[n][:, g * w:(g + 1) * w])\
                                    .then_inc(experts_in[f][g], 16)

                    stack_halves(0)
                    stack_halves(1)
                    load_experts(0, 2 * STEPS)
                    stack_halves(3)
                    load_experts(1, 4 * STEPS)
                    for b in range(PAIR):
                        sp.wait_ge(final_ready, b + 1)
                        sp.dma_start(out[it * PAIR + b].rearrange("(t p) c -> p t c", p=P), Z[b][:, :, :])\
                            .then_inc(out_stored, 16)
                    sp.wait_ge(out_stored, 16 * PAIR)

            numbers = sorted(s.num for s in per_pass)
            nc.sync.sem_clear(range(numbers[0], numbers[-1] + 1))
            nc.all_engine_barrier()


def arranged(x, ctx_512, **w):
    def heads_in(a):
        return a.transpose(1, 0, 2).reshape(a.shape[1], -1)

    def tiles(a):
        return a.reshape(-1, P, a.shape[-1]).transpose(1, 0, 2).reshape(P, -1)

    def padded(a):
        out = np.zeros((*a.shape[:-1], HEADS, 32), a.dtype)
        out[..., :HD0] = a.reshape(*a.shape[:-1], HEADS, HD0)
        return out.reshape(*a.shape[:-1], -1)

    def by_unit(a):
        return a.reshape(*a.shape[:-1], 4, 4, 32).swapaxes(-3, -2).reshape(a.shape)

    x0 = "L0_xattn_"
    A = {"x": x, "xT": x.transpose(0, 2, 1), "ctx": ctx_512, "ctxT": ctx_512.transpose(0, 2, 1),
         "qkv": w["L0_attn_W_qkv"].T, "wout": w["L0_attn_W_out"].T}
    for a in ("a1", "a2"):
        for k in ("wq", "wk", "wv") if a == "a1" else ("wq",):
            A[f"{a}_{k}"] = heads_in(w[f"{x0}{a}_{k}"])
            if k != "wv":
                A[f"{a}_{k}"] = by_unit(A[f"{a}_{k}"])
        A[a + "_li1"], A[a + "_li2"], A[a + "_li3"] = (tiles(w[x0 + a + "_li1_w"]), w[x0 + a + "_li2_w"],
                                                      tiles(w[x0 + a + "_li3_w"]))
    A["router"], A["ffn0_b2"] = w["L0_ffn_router_w"], w["L0_ffn_b2"]
    A["ffn0_w1"] = heads_in(w["L0_ffn_w1"])
    A["ffn0_w2"] = tiles(w["L0_ffn_w2"].reshape(-1, C))
    for k, n in (("wq", "W_Q"), ("wk", "W_K"), ("wv", "W_V")):
        A["l1_" + k] = w["L1_attn_" + n].reshape(-1, C).T
    A["l1_wo"] = tiles(w["L1_attn_W_O"].T)
    A["lx_wq"] = by_unit(padded(w["L1_xattn_Wq"]))
    for k in ("k", "v"):
        A["ctx_w" + k] = np.concatenate([heads_in(w[f"{x0}a2_w{k}"]), padded(w["L1_xattn_W" + k])])
    A["ctx_wk"] = by_unit(A["ctx_wk"])
    A["lx_wo"] = tiles(padded(w["L1_xattn_Wo"].T).T)
    A["router1"] = w["L1_ffn_Wr"]
    A["ffn1_w1"] = heads_in(w["L1_ffn_W1"])
    A["ffn1_w2"] = tiles(w["L1_ffn_W2"].reshape(-1, C))
    A["ffn1_b2"] = tiles(np.repeat(w["L1_ffn_b2"], SLOT, axis=0))
    rows = {"bo": w["L1_xattn_bo"], "router_b": w["L0_ffn_router_b"], "bv": padded(w["L1_xattn_bv"])}
    A["rows"] = np.concatenate([rows[n] if n in rows else w[x0 + n] for n in ROWS])
    columns = {"ffn0_b1": w["L0_ffn_b1"], "ffn1_b1": w["L1_ffn_b1"], "bq": by_unit(padded(w["L1_xattn_bq"])),
               "bk": by_unit(padded(w["L1_xattn_bk"]))}
    packed = np.zeros((P, NCOLS), x.dtype)
    for n, (at, width) in COLS.items():
        v = (columns[n] if n in columns else w[x0 + n]).reshape(width, -1)
        packed[:v.shape[1], at:at + width] = v.T
    A["cols"] = packed
    A["consts"] = shape_constants()
    return {n: np.ascontiguousarray(a) for n, a in A.items()}


def kernel(**inputs):
    import concourse.bacc as _bacc
    from concourse.bass_utils import run_bass_kernel_spmd as _run

    arrays = arranged(**{n: np.asarray(a) for n, a in inputs.items()})
    nc = _bacc.Bacc("TRN2", target_bir_lowering=False, num_devices=1)
    A = {n: nc.dram_tensor("in_" + n, a.shape, mybir.dt.from_np(a.dtype), kind="ExternalInput").ap()
         for n, a in arrays.items()}
    out = nc.dram_tensor("out", (BATCHES, T, C), fp32, kind="ExternalOutput").ap()
    decoder(nc, A, out)
    r = _run(nc, [{"in_" + n: a for n, a in arrays.items()}], core_ids=[0])
    return r.results[0]["out"]
```

```python
import concourse.bass as bass
from concourse import mybir
from contextlib import ExitStack

import numpy as np

fp32 = mybir.dt.float32
bf16 = mybir.dt.bfloat16
f32r = mybir.dt.float32r
u32 = mybir.dt.uint32
ALU = mybir.AluOpType
ACT = mybir.ActivationFunctionType
AX = mybir.AxisListType

P = 128
BATCHES, T, C, CC = 4, 256, 128, 64
TT = T // P
PAIR = 2
HEADS = 16
EPS = 1e-5
BUCKET = 64
HD0 = C // HEADS
E0, K0, I0 = 16, 4, 256
E1, I1 = 8, 512
CAP = int(T / E1 * 1.25)
SLOT = 64

ROWS = {}
for _n, _w in [("ln1_g", C), ("ln1_b", C), ("ln2_g", C), ("ln2_b", C), ("a1_li1_b", C), ("a1_li3_b", C),
               ("a2_li1_b", C), ("a2_li3_b", C), ("bo", C), ("router_b", E0), ("bv", HEADS * 32)]:
    ROWS[_n] = (sum(w for _, w in ROWS.values()), _w)
NROWS = sum(w for _, w in ROWS.values())
COLS = {}
for _n, _w in [("a1_lnx_g", 1), ("a1_lnx_b", 1), ("a1_lny_g", 1), ("a1_lny_b", 1), ("a1_ln3_g", 1), ("a1_ln3_b", 1),
               ("a1_li2_b", 4), ("a2_lnx_g", 1), ("a2_lnx_b", 1), ("a2_lny_g", 1), ("a2_lny_b", 1), ("a2_ln3_g", 1),
               ("a2_ln3_b", 1), ("a2_li2_b", 4), ("ffn0_b1", 2 * E0), ("ffn1_b1", 4 * E1), ("bq", 4), ("bk", 4)]:
    COLS[_n] = (sum(w for _, w in COLS.values()), _w)
NCOLS = sum(w for _, w in COLS.values())
CONSTS = {}
for _n, _w in [("ident", P), ("same_head", P), ("head_of", HEADS), ("later_key", 3 * P), ("earlier", P),
               ("masked", P), ("iota_e", E0), ("iota_slot", SLOT), ("minus_half", TT)]:
    CONSTS[_n] = (sum(w for _, w in CONSTS.values()), _w)
NCONSTS = sum(w for _, w in CONSTS.values())


def shape_constants():
    p, f = np.arange(P)[:, None], np.arange(P)[None, :]
    later = (p > f)
    parts = {
        "ident": p == f, "same_head": p // HD0 == f // HD0,
        "head_of": p // HD0 == np.arange(HEADS)[None, :],
        "later_key": np.concatenate([later, np.ones((P, P)), later], 1),
        "earlier": p < f,
        "masked": np.where(f > p, -1e10, 0.0),
        "iota_e": np.broadcast_to(np.arange(E0), (P, E0)),
        "iota_slot": np.broadcast_to(np.where(np.arange(SLOT) < CAP, np.arange(SLOT) + 1, -5), (P, SLOT)),
        "minus_half": np.full((P, TT), -0.5),
    }
    return np.concatenate([np.asarray(parts[n], np.float32) for n in CONSTS], 1)


WEIGHTS = {
    "qkv": (C, 3 * C), "wout": (C, C),
    "a1_wq": (C, 512), "a1_wk": (C, 512), "a1_wv": (C, 512), "a1_li1": (P, 512), "a1_li2": (C, 512), "a1_li3": (P, 512),
    "ctx_wk": (2 * CC, 512), "ctx_wv": (2 * CC, 512), "a2_wq": (C, 512), "a2_li1": (P, 512), "a2_li2": (C, 512), "a2_li3": (P, 512),
    "router": (C, E0), "ffn0_b2": (E0, C),
    "l1_wq": (C, 1024), "l1_wk": (C, 1024), "l1_wv": (C, 1024), "l1_wo": (P, 1024),
    "lx_wq": (C, 512), "lx_wo": (P, 512),
    "router1": (C, E1), "ffn1_b2": (P, 4 * C),
}

EXPERT_WEIGHTS = {"ffn0_w1": (C, E0 * I0), "ffn0_w2": (P, 2 * E0 * C),
                  "ffn1_w1": (C, E1 * I1), "ffn1_w2": (P, 4 * E1 * C)}
PARTS_OF_EXPERTS = 4

ATTENTIONS = [
    dict(name="a1", d=32, scale=32 ** -0.5, kind="keep_later", wq="a1_wq", wk="a1_wk", wv="a1_wv", wo="a1_li1"),
    dict(name="a2", d=32, scale=32 ** -0.5, kind="full", wq="a2_wq", wk="ctx_wk", wv="ctx_wv", wo="a2_li1"),
    dict(name="l1", d=64, scale=1 / 8, kind="causal", wq="l1_wq", wk="l1_wk", wv="l1_wv", wo="l1_wo"),
    dict(name="lx", d=32, scale=8 ** -0.5, kind="full", wq="lx_wq", wk="ctx_wk", wv="ctx_wv", wo="lx_wo"),
]
BLOCKS = {
    "causal": [(0, 0), (0, 1), (1, 1)],
}
PARTS = {
    "causal": [(True, 0, 0, 0, T), (False, 1, T, P, P)],
}
HALVES = HEADS // 2
SECOND_AT = 2
LAG = 3
TURNED = 4
RING = LAG + 1
SUM_AT = HALVES + LAG + 3
STEPS = PAIR * HALVES
SHEADS = PAIR * HEADS
UNIT = 4
SHIFT_LAG = 9
HD = 32
SECOND_HEAD = 7
SUMS_AT, INVERT_AT, CHECK_AT, VALUES_AT, REFINE_AT, DIVIDE_AT = 5, 7, 7, 7, 8, 9
OUT_AT = HEADS - UNIT + DIVIDE_AT + 2
NORM_AT = OUT_AT + 2
HEAD_STEPS = SHEADS + SHIFT_LAG + DIVIDE_AT - UNIT + 1
EXP_AND_LN = "natural_log_exp_and_others"
EXPS = 8


def decoder(nc, A, out):
    ctx = ExitStack()
    with ctx:
        def sb(name, shape, dt=fp32):
            return ctx.enter_context(nc.sbuf_tensor(name, shape, dt))

        W = {n: sb("w_" + n, [p, w]) for n, (p, w) in WEIGHTS.items()}
        rows, cols, consts = sb("rows", [P, NROWS]), sb("cols", [P, NCOLS]), sb("consts", [P, NCONSTS])

        def row(n):
            return rows[:, ROWS[n][0]:ROWS[n][0] + ROWS[n][1]]

        def col(n, k=0, p=P):
            return cols[0:p, COLS[n][0] + k:COLS[n][0] + k + 1]

        def const(n):
            return consts[:, CONSTS[n][0]:CONSTS[n][0] + CONSTS[n][1]]

        ident = const("ident")
        ident16, masked16 = sb("ident16", [P, P], bf16), sb("masked16", [P, P], bf16)

        def per_batch(name, shape):
            return [sb(f"{name}{b}", shape) for b in range(PAIR)]

        X, R, Z, U, BIASED = (per_batch(n, [P, TT, C]) for n in ("X", "R", "Z", "U", "BIASED"))
        XN, YN = (per_batch(n, [P, T]) for n in ("XN", "YN"))
        CTX, CTXT = per_batch("CTX", [P, TT, CC]), per_batch("CTXT", [P, T])
        stats, moments = sb("stats", [P, 2, TT, 6]), sb("moments", [P, 2, TT, 2])
        variance, rstd = sb("variance", [P, 2, TT]), sb("rstd", [P, 2, TT])

        OB = sb("OB", [P, 8, T])
        VB = per_batch("VB", [P, TT, 1024])
        probs = sb("probs", [P, (RING * 4 + TURNED * 4) * T])
        PB = probs[:, 0:RING * 4 * T].rearrange("p (r k q) -> p r k q", k=4, q=T)
        PT = probs[:, RING * 4 * T:].rearrange("p (r j q) -> p r j q", r=TURNED, j=2)
        exps = probs[:, 4 * 4 * T:].rearrange("p (h t q) -> p h t q", t=TT, q=T)
        shift_cols = sb("shift_cols", [P, 4, TT, UNIT])
        shift_rows = sb("shift_rows", [P, 4, T], f32r)
        choice = shift_rows[3 * HD:3 * HD + UNIT, :, :]
        unit_sums = sb("unit_sums", [P, 2, T])
        unit_inverse = sb("unit_inverse", [P, 2, T])
        negmax, sums, inverse = (sb(n, [P, 4, 4]) for n in ("negmax", "sums", "inverse"))

        arena_at = nc.sbuf_base() if callable(nc.sbuf_base) else nc.sbuf_base
        arena_at = -(-arena_at // 64) * 64
        sb("arena", [P, 16 * 1024 + 16])

        def arena(name, word, shape, dt=fp32):
            return nc.alloc_sbuf_tensor_at(name, shape, dt, offset=arena_at + 4 * word)

        SQ = [arena(f"stacked_q{b}", 4096 * b, [3 * HD + UNIT, HEADS, T], f32r) for b in range(PAIR)]
        SK = [arena(f"stacked_k{b}", 8192 + 4096 * b, [3 * HD + UNIT, HEADS, T], f32r) for b in range(PAIR)]
        QC = [arena(f"causal_q{b}", 2048 * b, [P, 8, T]) for b in range(PAIR)]
        KC = [arena(f"causal_k{b}", (12288, 4096)[b], [P, HEADS, T]) for b in range(PAIR)]
        for n, at in (("ffn0_w1", 0), ("ffn0_w2", 4096), ("ffn1_w1", 0), ("ffn1_w2", 4096)):
            W[n] = arena(n, at, list(EXPERT_WEIGHTS[n]))
        he = arena("expert_hidden", 8192, [P, 2048])
        router_scratch = [arena(f"router_scratch{b}", 10240 + 1024 * b, [P, 1024]) for b in range(PAIR)]
        pwt = arena("weights_by_slot", 10240, [P, 2048])
        slots = arena("slot_tokens", 12288, [P, 2048])

        def values(at, b, t, lo, hi):
            w = HEADS * at["d"]
            return VB[b][:, :, :].rearrange("p t n -> p (t n)")[:, t * w + lo:t * w + hi]

        vb = [VB[b][:, :, :].rearrange("p t n -> p (t n)") for b in range(PAIR)]

        def carve(flat, at, *shape):
            size = int(np.prod(shape))
            v = flat[:, at:at + size]
            if len(shape) == 2:
                v = v.rearrange("p (a b) -> p a b", b=shape[1])
            if len(shape) == 3:
                v = v.rearrange("p (a b c) -> p a b c", b=shape[1], c=shape[2])
            return v

        QS = [carve(vb[b], 0, TT, C) for b in range(PAIR)]
        QN = [carve(vb[b], 256, TT, C) for b in range(PAIR)]
        K0B = [carve(vb[b], 512, TT, C) for b in range(PAIR)]
        V0B = [carve(vb[b], 768, TT, C + 1) for b in range(PAIR)]
        CM = [carve(vb[b], 1040, 3, C + HEADS) for b in range(PAIR)]
        QT = [carve(vb[b], 1500, T) for b in range(PAIR)]
        OT = [carve(vb[b], 1760, T) for b in range(PAIR)]
        small0 = per_batch("small", [P, 200])
        HB = [OB[:, 4 * b:4 * b + 4, :] for b in range(PAIR)]
        HE = [carve(he, 512 * k, 2, T) for k in range(4)]
        halves = {"q_hi": PB[:, 0, :, :], "q_lo": PB[:, 1, :, :], "k_hi": PB[:, 3, :, :], "k_lo": PB[:, 2, :, :]}
        kept = [carve(vb[k // 4], 1024 + 256 * (k % 4), TT, P) for k in range(EXPS)]
        PM = [carve(vb[b], 0, TT, E1, SLOT) for b in range(PAIR)]
        PW = [carve(vb[b], 1024, TT, E1, SLOT) for b in range(PAIR)]
        PWT = [carve(pwt, 1024 * b, 4, T) for b in range(PAIR)]
        HX = [carve(he, 512 * k, 8, SLOT) for k in range(4)]
        BUF = [carve(slots, 512 * b, E1 * SLOT) for b in range(PAIR)]
        YB = [carve(slots, 1024 + 512 * b, 4, C) for b in range(PAIR)]

        scratch = [router_scratch[b][:, :] for b in range(PAIR)]
        shifted0 = [carve(scratch[b], 0, TT, E0) for b in range(PAIR)]
        expd0 = [carve(scratch[b], 32, TT, E0) for b in range(PAIR)]
        combine0 = [carve(scratch[b], 64, TT, E0) for b in range(PAIR)]
        onehot0 = [scratch[b][:, 96:96 + TT * K0 * E0].rearrange("p (t k e) -> p t k e", k=K0, e=E0) for b in range(PAIR)]
        combT = [carve(scratch[b], 256, T) for b in range(PAIR)]
        shifted1, expd1, chosen1 = ([carve(small0[b][:, :], at, TT, E1) for b in range(PAIR)] for at in (0, 16, 32))
        onehot1 = [small0[b][:, 48:80].rearrange("p (t k e) -> p t k e", k=2, e=E1) for b in range(PAIR)]
        top8 = [carve(small0[b][:, :], 128, TT, 8) for b in range(PAIR)]
        one, two = ([small0[b][:, at:at + TT] for b in range(PAIR)] for at in (160, 162))
        index8 = [sb(f"index8_{b}", [P, TT, 8], u32) for b in range(PAIR)]

        SC = [ctx.enter_context(nc.psum_tensor(f"SC{k}", [P, 2, TT, T], fp32)) for k in range(2)]
        G = [ctx.enter_context(nc.psum_tensor(f"G{k}", [P, 512], fp32)) for k in range(4)]

        weights_in = {n: ctx.enter_context(nc.semaphore("in_" + n)) for n in WEIGHTS}
        consts_in = ctx.enter_context(nc.semaphore("consts_in"))
        masks_made = ctx.enter_context(nc.semaphore("masks_made"))
        tables_in = ctx.enter_context(nc.semaphore("tables_in"))

        per_pass = []

        def sem(name):
            per_pass.append(ctx.enter_context(nc.semaphore(name)))
            return per_pass[-1]

        x_in = [sem(f"x_in{b}") for b in range(PAIR)]
        out_stored = sem("out_stored")
        bank_filled = [sem(f"bank_filled{k}") for k in range(4)]
        bank_emptied = [sem(f"bank_emptied{k}") for k in range(4)]
        dve_chain = sem("dve_chain")
        pool_chain = sem("pool_chain")
        context_ready = sem("context_ready")
        variance_ready, rstd_ready = sem("variance_ready"), sem("rstd_ready")
        z_ready = sem("z_ready")
        u_ready = sem("u_ready")
        bias_ready = sem("bias_ready")
        kv_drawn, q_exp, q_normal = sem("kv_drawn"), sem("q_exp"), sem("q_normal")
        hi_ready = sem("hi_ready")
        stacked = [[sem(f"stacked{b}_{u}") for u in range(HEADS // UNIT)] for b in range(PAIR)]
        experts_in = [[sem(f"experts{f}_in{g}") for g in range(PARTS_OF_EXPERTS)] for f in range(2)]
        zero_rows = sem("zero_rows")
        choice_in = [sem(f"choice_in{b}") for b in range(PAIR)]
        shift_scores = sem("shift_scores")
        head_max = sem("head_max")
        shifts_in = [sem(f"shifts_in{k}") for k in range(4)]
        head_scores = sem("head_scores")
        head_exp = sem("head_exp")
        first_kept, second_kept = sem("first_kept"), sem("second_kept")
        first_inverse = sem("first_inverse")
        inverse_checked = sem("inverse_checked")
        sums_inverse = sem("sums_inverse")
        scores_ready, max_ready, exp_ready = sem("scores_ready"), sem("max_ready"), sem("exp_ready")
        inverse_ready, probs_ready = sem("inverse_ready"), sem("probs_ready")
        logits_shifted, logits_exp = sem("logits_shifted"), sem("logits_exp")
        chosen_ready, dispatch_ready = sem("chosen_ready"), sem("dispatch_ready")
        hidden_ready = sem("hidden_ready")
        zeroed = sem("zeroed")
        final_ready = sem("final_ready")

        def stacking(a, b):
            return {0: 0, 1: 1, 3: 2}[a] * PAIR + b

        def head_number(a, g):
            return stacking(a, 0) // PAIR * SHEADS + g

        def unit_at(h, at):
            u, k = divmod(h - at, UNIT)
            return u if k == 0 and 0 <= u < SHEADS // UNIT else None

        ALL_TILES = range(12)

        def tile_of(at, side, m):
            chunks = HEADS * at["d"] // P
            return {"k": 0, "q": chunks // 2, "v": chunks}[side] + m

        def second_tiles(at, g):
            first, each = (SECOND_AT, 2) if at["kind"] == "causal" else (SECOND_HEAD, 3)
            return range(max(0, each * (g - first)), max(0, min(3 * HEADS * at["d"] // P // 2, each * (g - first + 1))))

        tile_number = {}

        def fill(pe, key):
            n = tile_number[key] = len(tile_number)
            if n >= 4:
                pe.wait_ge(bank_emptied[n % 4], n // 4)
            return G[n % 4]

        def filled(key):
            return bank_filled[tile_number[key] % 4], 1

        def wait_filled(eng, key):
            n = tile_number[key]
            eng.wait_ge(bank_filled[n % 4], n // 4 + 1)
            return G[n % 4]

        def emptied(key):
            return bank_emptied[tile_number[key] % 4], 1

        def wait_emptied(eng, key):
            n = tile_number[key]
            eng.wait_ge(bank_emptied[n % 4], n // 4 + 1)

        def load_weights(act):
            act.dma_start(consts[:, :], A["consts"]).then_inc(consts_in, 16)
            for n in WEIGHTS:
                act.dma_start(W[n][:, :], A[n]).then_inc(weights_in[n], 16)
                if n == "qkv":
                    act.dma_start(rows[:, :], A["rows"].partition_broadcast(P)).then_inc(tables_in, 16)
                    act.dma_start(cols[:, :], A["cols"]).then_inc(tables_in, 16)

        def make_masks(dve):
            dve.wait_ge(consts_in, 16)
            nc.vector.tensor_copy(ident16[:, :], ident).then_inc(masks_made, 1)
            nc.vector.tensor_copy(masked16[:, :], const("masked")).then_inc(masks_made, 1)
            nc.vector.tensor_copy(choice, consts[3 * HD:3 * HD + UNIT, CONSTS["ident"][0] + 3 * HD:CONSTS["ident"][0] + 3 * HD + UNIT].unsqueeze(2).to_broadcast([UNIT, UNIT, T]))\
                .then_inc(masks_made, 1)

        load_weights(nc.scalar)
        make_masks(nc.vector)

        with nc.Fori(0, BATCHES // PAIR) as it:
            with nc.Block() as block:

                @block.tensor
                def _(pe):
                    mm = nc.tensor.matmul

                    def transposed(key, src, width, wait):
                        wait()
                        g = fill(pe, key)
                        for t in range(TT):
                            last = nc.tensor.transpose(g[0:width, t * P:(t + 1) * P], src[:, t, :], ident)
                        last.then_inc(*filled(key))

                    def cross_transposed(b):
                        z_transposed(5 + b, b)
                        transposed(("CT", b), CTX[b], CC, lambda: pe.wait_ge(context_ready, b + 1))

                    def z_transposed(n, b, src=None, width=C):
                        transposed(("T", n, b), Z[b] if src is None else src, width, lambda: pe.wait_ge(z_ready, n))

                    pe.wait_ge(consts_in, 16)
                    pe.wait_ge(masks_made, 2)
                    pe.wait_ge(tables_in, 32)

                    pe.wait_ge(weights_in["qkv"], 16)
                    for b in range(PAIR):
                        pe.wait_ge(x_in[b], 64)
                        for t in range(TT):
                            g = fill(pe, ("qkv", b, t))
                            mm(g[:, 0:3 * C], XN[b][:, t * P:(t + 1) * P], W["qkv"][:, :], start=True, stop=True)\
                                .then_inc(*filled(("qkv", b, t)))
                    for b in range(PAIR):
                        for t in range(TT):
                            wait_emptied(pe, ("qkv", b, t))
                        pe.wait_ge(zeroed, b + 1)
                        g = fill(pe, ("ctx", b))
                        w = C + 1
                        half = slice(0, BUCKET)
                        mm(g[:, 0:w], K0B[b][half, 0, :], V0B[b][half, 0, :], start=True, stop=True)
                        mm(g[:, w:2 * w], K0B[b][:, 0, :], V0B[b][:, 0, :], start=True, stop=True)
                        mm(g[:, 2 * w:3 * w], K0B[b][:, 0, :], V0B[b][:, 0, :], start=True, stop=False)
                        mm(g[:, 2 * w:3 * w], K0B[b][half, 1, :], V0B[b][half, 1, :], start=False, stop=True)\
                            .then_inc(*filled(("ctx", b)))
                        transposed(("qT", b), QN[b], C, lambda: pe.wait_ge(q_normal, b + 1))
                    for b in range(PAIR):
                        wait_emptied(pe, ("qT", b))
                        wait_emptied(pe, ("ctx", b))
                        g = fill(pe, ("num", b))
                        w = C + HEADS
                        for n in (1, 2, 3):
                            r, t = BUCKET * (n % 2), n // 2
                            last = mm(g[r:r + BUCKET, t * w:(t + 1) * w], QT[b][:, n * BUCKET:(n + 1) * BUCKET],
                                      CM[b][:, n - 1, :], start=True, stop=True)
                        last.then_inc(*filled(("num", b)))
                    for b in range(PAIR):
                        transposed(("oT", b), Z[b], C, lambda: wait_emptied(pe, ("num", b)))
                    pe.wait_ge(weights_in["wout"], 16)
                    for b in range(PAIR):
                        wait_emptied(pe, ("oT", b))
                        g = fill(pe, ("wout", b))
                        for t in range(TT):
                            last = mm(g[:, t * C:(t + 1) * C], OT[b][:, t * P:(t + 1) * P], W["wout"][:, :],
                                      start=True, stop=True)
                        last.then_inc(*filled(("wout", b)))

                    def project(a, at, b, tiles=ALL_TILES):
                        name, chunks = at["name"], HEADS * at["d"] // P
                        kv = CTXT[b] if name == "lx" else XN[b] if name == "l1" else YN[b]
                        if 0 in tiles:
                            wait_emptied(pe, ("T", {0: 1, 1: 5, 2: 11, 3: 13}[a] + b, b))
                            if a == 1:
                                wait_emptied(pe, ("CT", b))
                            for w in ("wq", "wk", "wv"):
                                pe.wait_ge(weights_in[at[w]], 16)
                        kr = slice(0, CC) if name == "a2" else slice(CC, P) if name == "lx" else slice(0, C)
                        for side, src, kp in (("k", kv, kr), ("q", XN[b], slice(0, C))):
                            w = W[at["w" + side]]
                            for m in range(chunks // 2):
                                if tile_of(at, side, m) not in tiles:
                                    continue
                                g = fill(pe, (side, a, b, m))
                                for k in range(2):
                                    c = 2 * m + k
                                    last = mm(g[:, k * T:(k + 1) * T], w[kp, c * P:(c + 1) * P], src[kp, :],
                                              start=True, stop=True)
                                last.then_inc(*filled((side, a, b, m)))
                        for t in range(TT):
                            for h in range(chunks // 4):
                                if tile_of(at, "v", t * chunks // 4 + h) not in tiles:
                                    continue
                                g = fill(pe, ("v", a, b, t, h))
                                mm(g[:, :], kv[kr, t * P:(t + 1) * P], W[at["wv"]][kr, h * 512:(h + 1) * 512],
                                   start=True, stop=True).then_inc(*filled(("v", a, b, t, h)))

                    def head(at, i, j):
                        b, h = i // HALVES, 2 * (i % HALVES) + j
                        return b, h * at["d"] // P, h * at["d"] % P

                    def scores(a, at, i):
                        n = i
                        b = i // HALVES
                        if i % HALVES == 0:
                            pe.wait_ge(zero_rows, b + 1)
                            for m in range(4):
                                wait_emptied(pe, ("k", a, b, m))
                                wait_emptied(pe, ("q", a, b, m))
                        if n >= 2:
                            pe.wait_ge(exp_ready, n - 1)
                        s = SC[n % 2]
                        for j in range(2):
                            _, c, r = head(at, i, j)
                            h = 2 * (i % HALVES) + j
                            for t in range(TT):
                                qs, w = slice(t * P, (t + 1) * P), (t + 1) * P
                                mm(s[:, j, t, 0:w], QC[b][:, c, qs], KC[b][:, h, 0:w], start=True, stop=False)
                                last = mm(s[:, j, t, qs], ident16[:, :], masked16[:, :], start=False, stop=True)
                        last.then_inc(scores_ready, 1)

                    def transpose_probs(a, at, i):
                        n = i
                        pe.wait_ge(probs_ready, n + 1)
                        for j in range(2):
                            g = fill(pe, ("PT", a, i, j))
                            for k, (kt, qt) in enumerate(BLOCKS[at["kind"]]):
                                last = nc.tensor.transpose(g[:, k * P:(k + 1) * P],
                                                           PB[:, n % RING, 2 * j + qt, kt * P:(kt + 1) * P], ident)
                            last.then_inc(*filled(("PT", a, i, j)))

                    def weighted_values(a, at, u):
                        d, b = at["d"], (2 * u) // HALVES
                        for i in (2 * u, 2 * u + 1):
                            for j in range(2):
                                wait_emptied(pe, ("PT", a, i, j))
                        if u % (HALVES // 2) == 0:
                            for t in range(TT):
                                for h in range(HEADS * d // 512):
                                    wait_emptied(pe, ("v", a, b, t, h))
                        g = fill(pe, ("O", a, u))
                        sides = [(0, 1, 2, 3)] if d == 32 else [(0, 1), (2, 3)]
                        for side, (first, kt, at_col, q0, width) in [(x, y) for x in sides for y in PARTS[at["kind"]]]:
                            for k in side:
                                i, j = 2 * u + k // 2, k % 2
                                _, c, r = head(at, i, j)
                                h = 2 * (i % HALVES) + j
                                half = (k // 2) * T if d == 64 else 0
                                last = mm(g[r:r + d, half + q0:half + q0 + width], values(at, b, kt, h * d, (h + 1) * d),
                                          PT[:, i % TURNED, j, at_col:at_col + width],
                                          start=first, stop=not first)
                        last.then_inc(*filled(("O", a, u)))

                    def project_out(a, at, b):
                        chunks = HEADS * at["d"] // P
                        pe.wait_ge(weights_in[at["wo"]], 16)
                        for u in range(b * HALVES // 2, (b + 1) * HALVES // 2):
                            wait_emptied(pe, ("O", a, u))
                        c0 = 4 * b if at["d"] == HD else 0
                        g = fill(pe, ("x", a, b))
                        for t in range(TT):
                            for c in range(chunks):
                                last = mm(g[:, t * C:(t + 1) * C], OB[:, c0 + c, t * P:(t + 1) * P],
                                          W[at["wo"]][:, c * C:(c + 1) * C], start=c == 0, stop=c == chunks - 1)
                        last.then_inc(*filled(("x", a, b)))

                    def attention(a, before):
                        at = ATTENTIONS[a]
                        before(0)
                        project(a, at, 0)
                        before(1)
                        for st in range(STEPS + LAG + 2):
                            if second_tiles(at, st):
                                project(a, at, 1, second_tiles(at, st))
                            if st < STEPS:
                                scores(a, at, st)
                            i = st - LAG
                            if 0 <= i < STEPS:
                                transpose_probs(a, at, i)
                            if i >= 3 and i % 2 == 1:
                                weighted_values(a, at, i // 2 - 1)
                            if i == HALVES + 2:
                                project_out(a, at, 0)
                        project_out(a, at, 1)

                    def head_products(a, at, g):
                        n, (b, h) = head_number(a, g), divmod(g, HEADS)
                        if h % UNIT == 0:
                            pe.wait_ge(stacked[b][h // UNIT], 96 * (stacking(a, b) // PAIR + 1))
                        if n >= 2:
                            pe.wait_ge(head_max, n - 1)
                        for t in range(TT):
                            last = mm(SC[0][:, n % 2, t, :], SQ[b][0:3 * HD, h, t * P:(t + 1) * P],
                                      SK[b][0:3 * HD, h, :], start=True, stop=True)
                        last.then_inc(shift_scores, 1)

                    def turn_shifts(a, u):
                        pe.wait_ge(head_max, head_number(a, UNIT * u + UNIT))
                        g = fill(pe, ("M", a, u))
                        for t in range(TT):
                            last = nc.tensor.transpose(g[0:UNIT, t * P:(t + 1) * P],
                                                       shift_cols[:, u % 4, t, :], ident)
                        last.then_inc(*filled(("M", a, u)))

                    def transposed_products(a, at, g):
                        n, (b, h) = head_number(a, g), divmod(g, HEADS)
                        if h == 0:
                            pe.wait_ge(choice_in[b], 16 * (a // 3 + 1))
                        if h % UNIT == 0:
                            unit = n // UNIT
                            pe.wait_ge(shifts_in[unit % 4], 16 * (unit // 4 + 1))
                        if n >= 2:
                            pe.wait_ge(head_exp, n - 1)
                        for t in range(TT):
                            last = mm(SC[1][:, n % 2, t, :], SK[b][:, h, t * P:(t + 1) * P], SQ[b][:, h, :],
                                      start=True, stop=True)
                        last.then_inc(head_scores, 1)

                    ones = const("later_key")[:, P:P + HD]

                    def unit_sum(a, u, kt):
                        n, key = head_number(a, UNIT * u), ("S", a, u)
                        pe.wait_ge(head_exp, n + UNIT)
                        g = fill(pe, key) if kt == 0 else G[tile_number[key] % 4]
                        for k in range(UNIT):
                            last = mm(g[HD * k:HD * k + HD, 0:T], ones, exps[:, (n + k) % EXPS, kt, :],
                                      start=kt == 0, stop=kt == TT - 1)
                        if kt == TT - 1:
                            last.then_inc(*filled(key))

                    def unit_values(a, at, u, half):
                        n, b, h0 = head_number(a, UNIT * u), u // 4, u % 4 * UNIT
                        if u % 4 == 0:
                            for t in range(TT):
                                wait_emptied(pe, ("v", a, b, t, 0))
                        if at["kind"] == "keep_later":
                            pe.wait_ge(first_kept, n + UNIT)
                            pe.wait_ge(second_kept, n + UNIT)
                        g = fill(pe, ("O", a, u)) if half == 0 else G[tile_number["O", a, u] % 4]
                        if at["kind"] == "keep_later":
                            parts = [(True, False, 1, 0, P, False), (False, True, 0, 0, P, True), (True, True, 1, P, P, True)]
                        else:
                            parts = [(True, False, 0, 0, T, False), (False, True, 1, 0, T, False)]
                        cut = len(parts) - 1
                        for first, end, kt, q0, w, masked in (parts[cut:] if half else parts[:cut]):
                            for k in range(UNIT):
                                slot, h = (n + k) % EXPS, h0 + k
                                src = kept[slot][:, kt, :] if masked else exps[:, slot, kt, q0:q0 + w]
                                last = mm(g[HD * k:HD * k + HD, q0:q0 + w], values(at, b, kt, h * HD, (h + 1) * HD), src,
                                          start=first, stop=end)
                        if half:
                            last.then_inc(*filled(("O", a, u)))

                    def stacked_attention(a, before):
                        at = ATTENTIONS[a]
                        before(0)
                        project(a, at, 0)
                        before(1)
                        for g in range(HEAD_STEPS):
                            if second_tiles(at, g):
                                project(a, at, 1, second_tiles(at, g))
                            if g < SHEADS:
                                head_products(a, at, g)
                            if g % UNIT == 1 and 1 <= g // UNIT <= SHEADS // UNIT:
                                turn_shifts(a, g // UNIT - 1)
                            h = g - SHIFT_LAG
                            for part in range(2):
                                if unit_at(h, SUMS_AT + part) is not None:
                                    unit_sum(a, unit_at(h, SUMS_AT + part), part)
                                if unit_at(h, VALUES_AT + part) is not None:
                                    unit_values(a, at, unit_at(h, VALUES_AT + part), part)
                            if 0 <= h < SHEADS:
                                transposed_products(a, at, h)
                            if h == OUT_AT:
                                project_out(a, at, 0)
                        project_out(a, at, 1)

                    def mlp(a, n):
                        name = ATTENTIONS[a]["name"]
                        pe.wait_ge(weights_in[name + "_li2"], 16)
                        pe.wait_ge(weights_in[name + "_li3"], 16)
                        for b in range(PAIR):
                            z_transposed(n + b, b)
                            wait_emptied(pe, ("T", n + b, b))
                            for m in range(2):
                                g = fill(pe, ("li2", a, b, m))
                                for k in range(2):
                                    c = 2 * m + k
                                    last = mm(g[:, k * T:(k + 1) * T], W[name + "_li2"][:, c * P:(c + 1) * P], XN[b][:, :],
                                              start=True, stop=True)
                                last.then_inc(*filled(("li2", a, b, m)))
                            for m in range(2):
                                wait_emptied(pe, ("li2", a, b, m))
                            g = fill(pe, ("li3", a, b))
                            for t in range(TT):
                                for c in range(4):
                                    last = mm(g[:, t * C:(t + 1) * C], HB[b][:, c, t * P:(t + 1) * P],
                                              W[name + "_li3"][:, c * C:(c + 1) * C], start=c == 0, stop=c == 3)
                            last.then_inc(*filled(("li3", a, b)))

                    stacked_attention(0, lambda b: z_transposed(1 + b, b))
                    mlp(0, 3)
                    stacked_attention(1, cross_transposed)
                    mlp(1, 7)

                    pe.wait_ge(weights_in["router"], 16)
                    for b in range(PAIR):
                        z_transposed(9 + b, b, X[b])
                        wait_emptied(pe, ("T", 9 + b, b))
                        g = fill(pe, ("r0", b))
                        for t in range(TT):
                            last = mm(g[:, t * E0:(t + 1) * E0], XN[b][:, t * P:(t + 1) * P], W["router"][:, :],
                                      start=True, stop=True)
                        last.then_inc(*filled(("r0", b)))

                    def up0(i):
                        e, b = i // PAIR, i % PAIR
                        if i % (PAIR * E0 // PARTS_OF_EXPERTS) == 0:
                            pe.wait_ge(experts_in[0][e * PARTS_OF_EXPERTS // E0], 32)
                        g = fill(pe, ("up", e, b))
                        for f in range(2):
                            last = mm(g[:, f * T:(f + 1) * T], W["ffn0_w1"][:, e * I0 + f * P:e * I0 + (f + 1) * P],
                                      XN[b][:, :], start=True, stop=True)
                        last.then_inc(*filled(("up", e, b)))

                    def down0(i):
                        e, b = i // PAIR, i % PAIR
                        wait_emptied(pe, ("up", e, b))
                        g = fill(pe, ("down", e, b))
                        for t in range(TT):
                            for f in range(2):
                                k = (2 * e + f) * C
                                last = mm(g[:, t * C:(t + 1) * C], HE[i % 4][:, f, t * P:(t + 1) * P],
                                          W["ffn0_w2"][:, k:k + C], start=f == 0, stop=f == 1)
                        last.then_inc(*filled(("down", e, b)))

                    pe.wait_ge(weights_in["ffn0_b2"], 16)
                    up0(0)
                    up0(1)
                    for b in range(PAIR):
                        pe.wait_ge(chosen_ready, b + 1)
                        g = fill(pe, ("cT", b))
                        for t in range(TT):
                            last = nc.tensor.transpose(g[0:E0, t * P:(t + 1) * P], combine0[b][:, t, :], ident)
                        last.then_inc(*filled(("cT", b)))
                    for b in range(PAIR):
                        wait_emptied(pe, ("cT", b))
                        g = fill(pe, ("b2", b))
                        for t in range(TT):
                            last = mm(g[:, t * C:(t + 1) * C], combT[b][0:E0, t * P:(t + 1) * P],
                                      W["ffn0_b2"][:, :], start=True, stop=True)
                        last.then_inc(*filled(("b2", b)))
                    for i in range(PAIR * E0):
                        if i + 2 < PAIR * E0:
                            up0(i + 2)
                        down0(i)

                    attention(2, lambda b: z_transposed(11 + b, b, X[b]))
                    stacked_attention(3, lambda b: z_transposed(13 + b, b, X[b]))

                    pe.wait_ge(weights_in["router1"], 16)
                    for b in range(PAIR):
                        z_transposed(15 + b, b, X[b])
                        wait_emptied(pe, ("T", 15 + b, b))
                        g = fill(pe, ("r1", b))
                        for t in range(TT):
                            last = mm(g[:, t * E1:(t + 1) * E1], XN[b][:, t * P:(t + 1) * P], W["router1"][:, :],
                                      start=True, stop=True)
                        last.then_inc(*filled(("r1", b)))
                    for b in range(PAIR):
                        pe.wait_ge(chosen_ready, PAIR + b + 1)
                        g = fill(pe, ("pos", b))
                        mm(g[:, 0:E1], const("earlier"), chosen1[b][:, 0, :], start=True, stop=True)
                        mm(g[:, E1:2 * E1], const("later_key")[:, P:2 * P], chosen1[b][:, 0, :], start=True, stop=False)
                        mm(g[:, E1:2 * E1], const("earlier"), chosen1[b][:, 1, :], start=False, stop=True)\
                            .then_inc(*filled(("pos", b)))
                    for b in range(PAIR):
                        pe.wait_ge(dispatch_ready, 2 * b + 1)
                        g = fill(pe, ("buf", b))
                        for t in range(TT):
                            last = mm(g[:, :], X[b][:, t, :], PM[b][:, t, :, :].rearrange("p e s -> p (e s)"),
                                      start=t == 0, stop=t == TT - 1)
                        last.then_inc(*filled(("buf", b)))

                    def turn_weights(i):
                        b, m = i // 2, i % 2
                        pe.wait_ge(dispatch_ready, 2 * b + 2)
                        g = fill(pe, ("PWT", b, m))
                        for k in range(2):
                            for t in range(TT):
                                p2 = 2 * (2 * m + k)
                                last = nc.tensor.transpose(
                                    g[:, k * T + t * P:k * T + (t + 1) * P],
                                    PW[b][:, t, p2:p2 + 2, :].rearrange("p e s -> p (e s)"), ident)
                        last.then_inc(*filled(("PWT", b, m)))

                    def up1(i):
                        b, m = i // 4, i % 4
                        if m == 0:
                            wait_emptied(pe, ("buf", b))
                        if b == 0:
                            pe.wait_ge(experts_in[1][m], 32)
                        g = fill(pe, ("up1", b, m))
                        for k in range(2):
                            e = 2 * m + k
                            for f in range(4):
                                s = (4 * k + f) * SLOT
                                last = mm(g[:, s:s + SLOT], W["ffn1_w1"][:, e * I1 + f * P:e * I1 + (f + 1) * P],
                                          BUF[b][:, e * SLOT:(e + 1) * SLOT], start=True, stop=True)
                        last.then_inc(*filled(("up1", b, m)))

                    def down1(i):
                        b, m = i // 4, i % 4
                        pe.wait_ge(hidden_ready, i + 1)
                        g = fill(pe, ("y", b, m))
                        for f in range(4):
                            for k in range(2):
                                w = (4 * (2 * m + k) + f) * C
                                last = mm(g[k * SLOT:(k + 1) * SLOT, 0:C], HX[i % 4][:, 4 * k + f, :],
                                          W["ffn1_w2"][:, w:w + C], start=f == 0, stop=f == 3)
                        last.then_inc(*filled(("y", b, m)))

                    for i in range(4 * PAIR + 1):
                        if i < 4 * PAIR:
                            up1(i)
                        if i < 2 * PAIR:
                            turn_weights(i)
                        if i >= 1:
                            down1(i - 1)
                    for b in range(PAIR):
                        for m in range(2):
                            wait_emptied(pe, ("PWT", b, m))
                        for m in range(4):
                            wait_emptied(pe, ("y", b, m))
                        g = fill(pe, ("comb", b))
                        for t in range(TT):
                            for m in range(4):
                                last = mm(g[:, t * C:(t + 1) * C], PWT[b][:, m, t * P:(t + 1) * P], YB[b][:, m, :],
                                          start=m == 0, stop=m == 3)
                        last.then_inc(*filled(("comb", b)))

                @block.scalar
                def _(act):
                    fn = nc.scalar.activation

                    def copied(key, dst, src, scale=1.0):
                        g = wait_filled(act, key)
                        fn(dst, src(g), ACT.Copy, scale=scale).then_inc(*emptied(key))

                    def affine(key, dst, g_name, b_name, p=P):
                        g = wait_filled(act, key)
                        fn(dst[0:p, :], g[0:p, 0:T], ACT.Identity, scale=col(g_name, p=p), bias=col(b_name, p=p))\
                            .then_inc(*emptied(key))

                    act.wait_ge(tables_in, 32)
                    for b in range(PAIR):
                        for t in range(TT):
                            g = wait_filled(act, ("qkv", b, t))
                            fn(K0B[b][:, t, :], g[:, C:2 * C], ACT.Exp)
                            fn(V0B[b][:, t, 0:C], g[:, 2 * C:3 * C], ACT.Copy).then_inc(kv_drawn, 1)
                    for b in range(PAIR):
                        for t in range(TT):
                            wait_emptied(act, ("qkv", b, t))
                            fn(QN[b][:, t, :], QS[b][:, t, :], ACT.Exp).then_inc(q_exp, 1)
                    for b in range(PAIR):
                        copied(("qT", b), QT[b], lambda g: g[:, 0:T])
                    for b in range(PAIR):
                        copied(("oT", b), OT[b], lambda g: g[:, 0:T])

                    def project(a, at, b, tiles=ALL_TILES):
                        chunks, stacks = HEADS * at["d"] // P, at["kind"] != "causal"
                        if stacks and stacking(a, b) >= 1 and 0 in tiles:
                            for u in range(4):
                                m, other = stacking(a, b) - 1, 1 - b
                                act.wait_ge(stacked[other][u], 96 * (m // PAIR + 1))
                        for side in ("k", "q") if stacks else ():
                            for m in range(2):
                                if tile_of(at, side, m) not in tiles:
                                    continue
                                g = wait_filled(act, (side, a, b, m))
                                hi = halves[side + "_hi"]
                                if at["name"] == "lx":
                                    for k in range(2):
                                        last = fn(hi[:, 2 * m + k, :].bitcast(f32r), g[:, k * T:(k + 1) * T], ACT.Identity,
                                                  bias=col("b" + side, 2 * m + k))
                                else:
                                    last = fn(hi[:, 2 * m:2 * m + 2, :].rearrange("p a b -> p (a b)").bitcast(f32r),
                                              g[:, :], ACT.Copy, scale=at["scale"] if side == "q" else 1.0)
                                last.then_inc(hi_ready, 1)
                        if not stacks:
                            for m in range(4):
                                if tile_of(at, "q", m) not in tiles:
                                    continue
                                copied(("q", a, b, m), QC[b][:, 2 * m:2 * m + 2, :].rearrange("p a b -> p (a b)"),
                                       lambda g: g[:, :], at["scale"])
                        if at["name"] in ("a1", "a2") and tile_of(at, "v", 0) in tiles:
                            copied(("v", a, b, 0, 0), values(at, b, 0, 0, 512), lambda g: g[:, :])
                        if at["name"] == "l1":
                            for h in range(chunks // 4):
                                if tile_of(at, "v", h) not in tiles:
                                    continue
                                copied(("v", a, b, 0, h), values(at, b, 0, h * 512, (h + 1) * 512), lambda g: g[:, :])

                    def exponentials(a, at, i):
                        n = i
                        if i >= RING:
                            wait_filled(act, ("PT", a, i - RING, 1))
                        act.wait_ge(max_ready, n + 1)
                        for k in range(4):
                            j, t = k // 2, k % 2
                            w = (t + 1) * P
                            last = fn(PB[:, n % RING, k, 0:w], SC[n % 2][:, j, t, 0:w], ACT.Exp,
                                      bias=negmax[:, n % 4, k:k + 1], accum_out=sums[:, n % 4, k:k + 1])
                        last.then_inc(exp_ready, 1)

                    def attention(a, before):
                        at = ATTENTIONS[a]
                        before(0)
                        project(a, at, 0)
                        before(1)
                        for st in range(STEPS + LAG + 2):
                            if second_tiles(at, st):
                                project(a, at, 1, second_tiles(at, st))
                            if st < STEPS:
                                exponentials(a, at, st)
                            i = st - LAG
                            if 0 <= i < STEPS:
                                w = len(BLOCKS[at["kind"]]) * P
                                copied(("PT", a, i, 1), PT[:, i % TURNED, 1, 0:w], lambda g: g[:, 0:w])
                            if i >= 3 and i % 2 == 1:
                                u = i // 2 - 1
                                ub = u % (HALVES // 2)
                                if u == HALVES // 2:
                                    wait_filled(act, ("x", a, 0))
                                if at["d"] == 64:
                                    copied(("O", a, u), OB[:, 2 * ub:2 * ub + 2, :].rearrange("p a b -> p (a b)"),
                                           lambda g: g[:, :])
                                else:
                                    copied(("O", a, u), OB[:, ub, :], lambda g: g[:, 0:T])

                    def stacked_attention(a, before):
                        at = ATTENTIONS[a]
                        nc.scalar.preload_act_table_set(EXP_AND_LN)
                        before(0)
                        project(a, at, 0)
                        before(1)
                        for g in range(HEAD_STEPS):
                            if second_tiles(at, g):
                                project(a, at, 1, second_tiles(at, g))
                            if g % UNIT == 1 and 1 <= g // UNIT <= SHEADS // UNIT:
                                u = g // UNIT - 1
                                m = wait_filled(act, ("M", a, u))
                                fn(shift_rows[0:UNIT, u % 4, :], m[0:UNIT, 0:T], ACT.Copy)\
                                    .then_inc(*emptied(("M", a, u)))
                            h = g - SHIFT_LAG
                            if unit_at(h, INVERT_AT) is not None:
                                u = unit_at(h, INVERT_AT)
                                if u >= 2:
                                    wait_emptied(act, ("O", a, u - 2))
                                s = wait_filled(act, ("S", a, u))
                                fn(unit_sums[:, u % 2, :], s[:, 0:T], ACT.Copy)
                                fn(unit_inverse[:, u % 2, :], s[:, 0:T], ACT.Ln).then_inc(*emptied(("S", a, u)))
                            if 0 <= h < SHEADS:
                                n = head_number(a, h)
                                if h >= EXPS:
                                    wait_filled(act, ("O", a, (h - EXPS) // UNIT))
                                act.wait_ge(head_scores, n + 1)
                                fn(exps[:, n % EXPS, :, :].rearrange("p t q -> p (t q)"),
                                   SC[1][:, n % 2, :, :].rearrange("p t q -> p (t q)"), ACT.Exp,
                                   scale=at["scale"] if at["name"] == "lx" else 1.0).then_inc(head_exp, 1)
                            if unit_at(h, INVERT_AT) is not None:
                                u = unit_at(h, INVERT_AT)
                                wait_emptied(act, ("S", a, u))
                                fn(unit_inverse[:, u % 2, :], unit_inverse[:, u % 2, :], ACT.Exp, scale=-1.0)\
                                    .then_inc(first_inverse, 1)

                    def mlp(a, n):
                        name = ATTENTIONS[a]["name"]
                        for b in range(PAIR):
                            affine(("T", n + b, b), XN[b], name + "_ln3_g", name + "_ln3_b")
                            for m in range(2):
                                g = wait_filled(act, ("li2", a, b, m))
                                for k in range(2):
                                    c = 2 * m + k
                                    last = fn(HB[b][:, c, :], g[:, k * T:(k + 1) * T], ACT.Gelu,
                                              bias=col(name + "_li2_b", c))
                                last.then_inc(*emptied(("li2", a, b, m)))

                    def self_operands(b):
                        g = wait_filled(act, ("T", 1 + b, b))
                        fn(XN[b][:, :], g[:, 0:T], ACT.Identity, scale=col("a1_lnx_g"), bias=col("a1_lnx_b"))
                        fn(YN[b][:, :], g[:, 0:T], ACT.Identity, scale=col("a1_lny_g"), bias=col("a1_lny_b"))\
                            .then_inc(*emptied(("T", 1 + b, b)))
                    def cross_operands(b):
                        affine(("T", 5 + b, b), XN[b], "a2_lnx_g", "a2_lnx_b")
                        affine(("CT", b), YN[b], "a2_lny_g", "a2_lny_b", CC)

                    stacked_attention(0, self_operands)
                    mlp(0, 3)
                    stacked_attention(1, cross_operands)
                    mlp(1, 7)

                    for b in range(PAIR):
                        copied(("T", 9 + b, b), XN[b][:, :], lambda g: g[:, 0:T])
                    for b in range(PAIR):
                        act.wait_ge(logits_shifted, b + 1)
                        fn(expd0[b], shifted0[b], ACT.Exp).then_inc(logits_exp, 1)

                    def gelu_up(i):
                        e, b = i // PAIR, i % PAIR
                        g = wait_filled(act, ("up", e, b))
                        if i >= 4:
                            wait_filled(act, ("down", (i - 4) // PAIR, b))
                        for f in range(2):
                            last = fn(HE[i % 4][:, f, :], g[:, f * T:(f + 1) * T], ACT.Gelu,
                                      bias=col("ffn0_b1", 2 * e + f))
                        last.then_inc(*emptied(("up", e, b)))

                    gelu_up(0)
                    gelu_up(1)
                    for b in range(PAIR):
                        copied(("cT", b), combT[b][0:E0, :], lambda g: g[0:E0, 0:T])
                    for i in range(2, PAIR * E0):
                        gelu_up(i)

                    attention(2, lambda b: copied(("T", 11 + b, b), XN[b][:, :], lambda g: g[:, 0:T]))
                    stacked_attention(3, lambda b: copied(("T", 13 + b, b), XN[b][:, :], lambda g: g[:, 0:T]))

                    for b in range(PAIR):
                        copied(("T", 15 + b, b), XN[b][:, :], lambda g: g[:, 0:T])
                        act.wait_ge(logits_shifted, PAIR + b + 1)
                        fn(expd1[b], shifted1[b], ACT.Exp).then_inc(logits_exp, 1)
                    for b in range(PAIR):
                        copied(("buf", b), BUF[b], lambda g: g[:, :])
                    for i in range(4 * PAIR):
                        wait_emptied(act, ("up1", i // 4, i % 4))
                        fn(HX[i % 4], HX[i % 4], ACT.Relu).then_inc(hidden_ready, 1)
                        if i < 2 * PAIR:
                            b, m = i // 2, i % 2
                            copied(("PWT", b, m), PWT[b][:, 2 * m:2 * m + 2, :].rearrange("p a b -> p (a b)"),
                                   lambda g: g[:, :])

                @block.vector
                def _(dve):
                    v = nc.vector
                    links = [0]

                    def link(ins):
                        links[0] += 1
                        ins.then_inc(dve_chain, 1)
                        dve.wait_ge(dve_chain, links[0])

                    norms = [0]

                    def measure(src, width=C):
                        norms[0] += 1
                        k = norms[0] % 2
                        for t in range(TT):
                            last = v.bn_stats(stats[:, k, t, :], src[:, t, 0:width])
                        link(last)
                        for t in range(TT):
                            last = v.bn_aggr(moments[:, k, t, :], stats[:, k, t, :])
                        link(last)
                        v.tensor_scalar(variance[:, k, :], moments[:, k, :, 1], EPS, None, ALU.add)\
                            .then_inc(variance_ready, 1)
                        return norms[0], src, width

                    def normalise(measured, dst):
                        n, src, width = measured
                        dve.wait_ge(rstd_ready, n)
                        for t in range(TT):
                            last = v.tensor_scalar(dst[:, t, 0:width], src[:, t, 0:width], moments[:, n % 2, t, 0:1],
                                                   rstd[:, n % 2, t:t + 1], ALU.subtract, ALU.mult)
                        return last

                    def layernorm(src, dst, width=C):
                        return normalise(measure(src, width), dst)

                    def both_layernorms(srcs, dsts, width=C):
                        measured = [measure(srcs[b], width) for b in range(PAIR)]
                        return [normalise(measured[b], dsts[b]) for b in range(PAIR)]

                    def over_tiles(vec):
                        return vec.unsqueeze(1).to_broadcast([P, TT, C])

                    def gain_bias(x, g_name, b_name):
                        link(v.tensor_tensor(x[:, :, :], x[:, :, :], over_tiles(row(g_name)), ALU.mult))
                        return v.tensor_tensor(x[:, :, :], x[:, :, :], over_tiles(row(b_name)), ALU.add)

                    def residual(key, dst, other):
                        g = wait_filled(dve, key)
                        v.tensor_tensor(dst[:, :, :], g[:, 0:TT * C].rearrange("p (t c) -> p t c", c=C),
                                        other[:, :, :], ALU.add).then_inc(*emptied(key))
                        wait_emptied(dve, key)

                    dve.wait_ge(consts_in, 16)
                    dve.wait_ge(tables_in, 32)
                    heads = lambda x: x.rearrange("p (h d) -> p h d", d=HD0)
                    for b in range(PAIR):
                        dve.wait_ge(x_in[b], 64)
                        for t in range(TT):
                            g = wait_filled(dve, ("qkv", b, t))
                            dve.wait_ge(kv_drawn, TT * b + t + 1)
                            m = small0[b][:, t * HEADS:(t + 1) * HEADS]
                            link(v.tensor_reduce(m, heads(g[:, 0:C]), axis=AX.X, op=ALU.max))
                            v.tensor_tensor(heads(QS[b][:, t, :]), heads(g[:, 0:C]),
                                            m.unsqueeze(2).to_broadcast([P, HEADS, HD0]), ALU.subtract)\
                                .then_inc(*emptied(("qkv", b, t)))
                    for b in range(PAIR):
                        dve.wait_ge(q_exp, TT * (b + 1))
                        flat = QN[b].rearrange("p t c -> p (t c)")
                        s, r = small0[b][:, 32:64], small0[b][:, 64:96]
                        link(v.tensor_reduce(s, heads(flat), axis=AX.X, op=ALU.add))
                        link(v.reciprocal(r, s))
                        link(v.tensor_scalar(s, r, HD0 ** -0.5, None, ALU.mult))
                        v.tensor_tensor(heads(flat), heads(flat), s.unsqueeze(2).to_broadcast([P, TT * HEADS, HD0]),
                                        ALU.mult).then_inc(q_normal, 1)
                        g = wait_filled(dve, ("ctx", b))
                        prod = g[:, 0:3 * (C + 1)].rearrange("p (n c) -> p n c", c=C + 1)
                        v.tensor_tensor(CM[b][:, :, 0:C], prod[:, :, 0:C],
                                        const("same_head").unsqueeze(1).to_broadcast([P, 3, C]), ALU.mult)
                        v.tensor_tensor(CM[b][:, :, C:C + HEADS], prod[:, :, C:C + 1].to_broadcast([P, 3, HEADS]),
                                        const("head_of").unsqueeze(1).to_broadcast([P, 3, HEADS]), ALU.mult)\
                            .then_inc(*emptied(("ctx", b)))
                    for last in both_layernorms(CTX, CTX, CC):
                        last.then_inc(context_ready, 1)
                    for b in range(PAIR):
                        g = wait_filled(dve, ("num", b))
                        dve.wait_ge(zeroed, PAIR + b + 1)
                        for t, r0 in ((0, BUCKET), (1, 0)):
                            tile = g[r0:P, t * (C + HEADS):(t + 1) * (C + HEADS)]
                            s, r = small0[b][r0:P, 96:112], small0[b][r0:P, 112:128]
                            link(v.tensor_scalar(s, tile[:, C:C + HEADS], 1e-6, None, ALU.max))
                            link(v.reciprocal(r, s))
                            last = v.tensor_tensor(heads(Z[b][r0:P, t, :]), heads(tile[:, 0:C]),
                                                   r.unsqueeze(2).to_broadcast([P - r0, HEADS, HD0]), ALU.mult)
                            if t == 0:
                                link(last)
                        last.then_inc(*emptied(("num", b)))
                    under_way = {}

                    def before_self(b):
                        if b == 0:
                            residual(("wout", 0), R[0], X[0])
                            m = measure(R[0])
                            residual(("wout", 1), R[1], X[1])
                            link(normalise(m, X[0]))
                            m0, m1 = measure(X[0]), measure(R[1])
                            link(normalise(m0, U[0]))
                            gain_bias(U[0], "ln1_g", "ln1_b").then_inc(u_ready, 1)
                            link(normalise(m1, X[1]))
                            dve.wait_ge(u_ready, 1)
                            m0, m1 = measure(U[0]), measure(X[1])
                            normalise(m0, Z[0]).then_inc(z_ready, 1)
                            under_way[0] = m1
                        else:
                            link(normalise(under_way[0], U[1]))
                            gain_bias(U[1], "ln1_g", "ln1_b").then_inc(u_ready, 1)
                            dve.wait_ge(u_ready, 2)
                            layernorm(U[1], Z[1]).then_inc(z_ready, 1)

                    def project(a, at, b, tiles=ALL_TILES):
                        chunks, name = HEADS * at["d"] // P, at["name"]
                        for m in range(4) if at["kind"] == "causal" else ():
                            if tile_of(at, "k", m) not in tiles:
                                continue
                            g = wait_filled(dve, ("k", a, b, m))
                            for k in range(2):
                                r = slice(64 * k, 64 * k + 64)
                                last = v.tensor_copy(KC[b][r, 4 * m + k:4 * m + k + 3:2, :],
                                                     g[r, :].rearrange("p (a b) -> p a b", b=T))
                            last.then_inc(*emptied(("k", a, b, m)))
                        for n, side in enumerate(("k", "q")) if at["kind"] != "causal" else ():
                            for m in range(2):
                                if tile_of(at, side, m) not in tiles:
                                    continue
                                g = wait_filled(dve, (side, a, b, m))
                                dve.wait_ge(hi_ready, 4 * stacking(a, b) + 2 * n + m + 1)
                                hi, lo = halves[side + "_hi"], halves[side + "_lo"]
                                for k in range(2):
                                    c = 2 * m + k
                                    if name == "lx":
                                        by, op = col("b" + side, c), ALU.add
                                    else:
                                        by, op = at["scale"] if side == "q" else 1.0, ALU.mult
                                    last = v.scalar_tensor_tensor(lo[:, c, :].bitcast(f32r), g[:, k * T:(k + 1) * T], by,
                                                                  hi[:, c, :], op0=op, op1=ALU.subtract)
                                last.then_inc(*emptied((side, a, b, m)))
                        for t in range(TT):
                            for h in range(chunks // 4):
                                if tile_of(at, "v", t * chunks // 4 + h) not in tiles:
                                    continue
                                if name == "lx":
                                    g = wait_filled(dve, ("v", a, b, t, h))
                                    v.tensor_tensor(values(at, b, t, 0, 512), g[:, :], row("bv"), ALU.add)\
                                        .then_inc(*emptied(("v", a, b, t, h)))
                                elif t == 1:
                                    g = wait_filled(dve, ("v", a, b, t, h))
                                    v.tensor_copy(values(at, b, t, h * 512, (h + 1) * 512), g[:, :])\
                                        .then_inc(*emptied(("v", a, b, t, h)))

                    def maxima(a, at, i):
                        n = i
                        dve.wait_ge(scores_ready, n + 1)
                        s = SC[n % 2]
                        m = negmax[:, n % 4, :]
                        mv = m.rearrange("p (j t) -> p j t", t=TT)
                        for t in range(TT):
                            last = v.tensor_reduce(mv[:, :, t], s[:, :, t, 0:(t + 1) * P], axis=AX.X, op=ALU.max,
                                                   negate=True)
                        last.then_inc(max_ready, 1)

                    def inverses(a, i):
                        n = i
                        dve.wait_ge(exp_ready, n + 1)
                        v.reciprocal(inverse[:, n % 4, :], sums[:, n % 4, :]).then_inc(inverse_ready, 1)

                    def attention_sum(a, b):
                        if a != 2:
                            dve.wait_ge(bias_ready, {0: 0, 1: 2, 3: 4}[a] * PAIR + b + 1)
                        residual(("x", a, b), R[b], X[b] if a == 2 else BIASED[b])

                    def after_norm(a, b):
                        layernorm(R[b], Z[b] if a < 2 else X[b]).then_inc(z_ready, 1)

                    def attention(a, before):
                        at = ATTENTIONS[a]
                        before(0)
                        project(a, at, 0)
                        before(1)
                        for st in range(STEPS + LAG + 2):
                            if second_tiles(at, st):
                                project(a, at, 1, second_tiles(at, st))
                            if st < STEPS:
                                maxima(a, at, st)
                            i = st - LAG
                            if 0 <= i < STEPS:
                                if i >= TURNED:
                                    wait_filled(dve, ("O", a, (i - TURNED) // 2))
                                g = wait_filled(dve, ("PT", a, i, 0))
                                w = len(BLOCKS[at["kind"]]) * P
                                v.tensor_copy(PT[:, i % TURNED, 0, 0:w], g[:, 0:w]).then_inc(*emptied(("PT", a, i, 0)))
                            if 0 <= st - 1 < STEPS:
                                inverses(a, st - 1)
                            if st == SUM_AT:
                                attention_sum(a, 0)
                                after_norm(a, 0)
                        attention_sum(a, 1)

                    def stacked_attention(a, before):
                        at = ATTENTIONS[a]
                        before(0)
                        project(a, at, 0)
                        before(1)
                        for g in range(HEAD_STEPS):
                            if second_tiles(at, g):
                                project(a, at, 1, second_tiles(at, g))
                            if g < SHEADS:
                                n = head_number(a, g)
                                dve.wait_ge(shift_scores, n + 1)
                                v.tensor_reduce(shift_cols[:, g // UNIT % 4, :, g % UNIT], SC[0][:, n % 2, :, :],
                                                axis=AX.X, op=ALU.max, negate=True).then_inc(head_max, 1)
                            h = g - SHIFT_LAG
                            if at["kind"] == "keep_later" and 0 <= h - 1 < SHEADS:
                                n = head_number(a, h - 1)
                                dve.wait_ge(head_exp, n + 1)
                                if h - 1 >= EXPS:
                                    wait_filled(dve, ("O", a, (h - 1 - EXPS) // UNIT))
                                v.tensor_tensor(kept[n % EXPS][:, 1, :], exps[:, n % EXPS, 1, P:T],
                                                const("later_key")[:, 0:P], ALU.mult).then_inc(second_kept, 1)
                            if unit_at(h, REFINE_AT) is not None:
                                u = unit_at(h, REFINE_AT)
                                dve.wait_ge(inverse_checked, head_number(a, 0) // UNIT + u + 1)
                                v.scalar_tensor_tensor(unit_inverse[:, u % 2, :], unit_sums[:, u % 2, :], -2.0,
                                                       unit_inverse[:, u % 2, :], op0=ALU.add, op1=ALU.mult)\
                                    .then_inc(sums_inverse, 1)
                            if unit_at(h, DIVIDE_AT) is not None:
                                u = unit_at(h, DIVIDE_AT)
                                o = wait_filled(dve, ("O", a, u))
                                dve.wait_ge(sums_inverse, head_number(a, 0) // UNIT + u + 1)
                                v.scalar_tensor_tensor(OB[:, u, :], o[:, 0:T], -1.0, unit_inverse[:, u % 2, :],
                                                       op0=ALU.mult, op1=ALU.mult)\
                                    .then_inc(*emptied(("O", a, u)))
                            if h == NORM_AT:
                                attention_sum(a, 0)
                                after_norm(a, 0)
                        attention_sum(a, 1)
                        after_norm(a, 1)

                    def before_cross(b):
                        def finish(m):
                            link(normalise(m, U[b]))
                            gain_bias(U[b], "ln2_g", "ln2_b").then_inc(u_ready, 1)
                            dve.wait_ge(u_ready, PAIR + b + 1)
                            return measure(U[b])

                        def residual_of(b):
                            dve.wait_ge(bias_ready, PAIR + 1 + b)
                            residual(("li3", 0, b), R[b], U[b])
                            return measure(R[b])

                        if b == 0:
                            m = finish(residual_of(0))
                            normalise(m, Z[0]).then_inc(z_ready, 1)
                            under_way[1] = residual_of(1)
                        else:
                            normalise(finish(under_way[1]), Z[1]).then_inc(z_ready, 1)

                    stacked_attention(0, before_self)
                    stacked_attention(1, before_cross)
                    for b in range(PAIR):
                        dve.wait_ge(bias_ready, 3 * PAIR + b + 1)
                        residual(("li3", 1, b), R[b], U[b])
                        layernorm(R[b], X[b]).then_inc(z_ready, 1)

                    def chosen(b, prob, E, top, idx, onehot, sel, k):
                        for t in range(TT):
                            last = v.max(top[:, t, :], prob[:, t, :])
                        link(last)
                        for t in range(TT):
                            last = v.max_index(idx[:, t, :], top[:, t, :], prob[:, t, :])
                        link(last)
                        for t in range(TT):
                            last = v.tensor_tensor(onehot[:, t, :, :], const("iota_e")[:, 0:E].unsqueeze(1)
                                                   .to_broadcast([P, k, E]),
                                                   idx[:, t, 0:k].unsqueeze(2).to_broadcast([P, k, E]), ALU.is_equal)
                        link(last)
                        for t in range(TT):
                            last = v.tensor_reduce(sel[:, t, :], onehot[:, t, :, :].rearrange("p k e -> p e k"),
                                                   axis=AX.X, op=ALU.add)
                        return last

                    def shift(b, shifted, E, one):
                        link(v.tensor_reduce(one, shifted, axis=AX.X, op=ALU.max))
                        v.tensor_tensor(shifted, shifted, one.unsqueeze(2).to_broadcast([P, TT, E]), ALU.subtract)\
                            .then_inc(logits_shifted, 1)

                    for b in range(PAIR):
                        g = wait_filled(dve, ("r0", b))
                        v.tensor_tensor(shifted0[b], g[:, 0:TT * E0].rearrange("p (t e) -> p t e", e=E0),
                                        row("router_b").unsqueeze(1).to_broadcast([P, TT, E0]), ALU.add)\
                            .then_inc(*emptied(("r0", b)))
                        wait_emptied(dve, ("r0", b))
                        shift(b, shifted0[b], E0, one[b])
                    for b in range(PAIR):
                        dve.wait_ge(logits_exp, b + 1)
                        link(chosen(b, expd0[b], E0, top8[b], index8[b], onehot0[b], combine0[b], K0))
                        link(v.tensor_tensor(shifted0[b], combine0[b], expd0[b], ALU.mult))
                        link(v.tensor_reduce(one[b], shifted0[b], axis=AX.X, op=ALU.add))
                        link(v.reciprocal(two[b], one[b]))
                        v.tensor_tensor(combine0[b], shifted0[b], two[b].unsqueeze(2).to_broadcast([P, TT, E0]),
                                        ALU.mult).then_inc(chosen_ready, 1)
                    for b in range(PAIR):
                        residual(("b2", b), R[b], X[b])
                    for i in range(PAIR * E0):
                        e, b = i // PAIR, i % PAIR
                        g = wait_filled(dve, ("down", e, b))
                        if e == 0:
                            dve.wait_ge(chosen_ready, b + 1)
                        else:
                            wait_emptied(dve, ("down", e - 1, b))
                        for t in range(TT):
                            last = v.scalar_tensor_tensor(R[b][:, t, :], g[:, t * C:(t + 1) * C],
                                                          combine0[b][:, t, e:e + 1], R[b][:, t, :],
                                                          op0=ALU.mult, op1=ALU.add)
                        last.then_inc(*emptied(("down", e, b)))

                    def before_causal(b):
                        if b == 0:
                            for k in range(PAIR):
                                wait_emptied(dve, ("down", E0 - 1, k))
                            m0, under_way[2] = measure(R[0]), measure(R[1])
                            normalise(m0, X[0]).then_inc(z_ready, 1)
                            normalise(under_way[2], X[1]).then_inc(z_ready, 1)

                    attention(2, before_causal)
                    stacked_attention(3, lambda b: after_norm(2, 1) if b == 0 else None)

                    for b in range(PAIR):
                        g = wait_filled(dve, ("r1", b))
                        v.tensor_copy(shifted1[b], g[:, 0:TT * E1].rearrange("p (t e) -> p t e", e=E1))\
                            .then_inc(*emptied(("r1", b)))
                        wait_emptied(dve, ("r1", b))
                        shift(b, shifted1[b], E1, one[b])
                        dve.wait_ge(logits_exp, PAIR + b + 1)
                        link(v.tensor_reduce(one[b], expd1[b], axis=AX.X, op=ALU.add))
                        link(v.reciprocal(two[b], one[b]))
                        link(v.tensor_tensor(expd1[b], expd1[b], two[b].unsqueeze(2).to_broadcast([P, TT, E1]),
                                             ALU.mult))
                        chosen(b, expd1[b], E1, top8[b], index8[b], onehot1[b], chosen1[b], 2).then_inc(chosen_ready, 1)
                    for b in range(PAIR):
                        g = wait_filled(dve, ("pos", b))
                        dve.wait_ge(chosen_ready, PAIR + b + 1)
                        v.scalar_tensor_tensor(shifted1[b].rearrange("p t e -> p (t e)"), g[:, 0:TT * E1], 1.0,
                                               chosen1[b].rearrange("p t e -> p (t e)"), op0=ALU.add, op1=ALU.mult)\
                            .then_inc(*emptied(("pos", b)))
                        wait_emptied(dve, ("pos", b))
                        for t in range(TT):
                            last = v.tensor_tensor(PM[b][:, t, :, :],
                                                   const("iota_slot").unsqueeze(1).to_broadcast([P, E1, SLOT]),
                                                   shifted1[b][:, t, :].unsqueeze(2).to_broadcast([P, E1, SLOT]),
                                                   ALU.is_equal)
                        last.then_inc(dispatch_ready, 1)
                        dve.wait_ge(dispatch_ready, 2 * b + 1)
                        for t in range(TT):
                            last = v.tensor_tensor(PW[b][:, t, :, :], PM[b][:, t, :, :],
                                                   expd1[b][:, t, :].unsqueeze(2).to_broadcast([P, E1, SLOT]), ALU.mult)
                        last.then_inc(dispatch_ready, 1)
                    dve.wait_ge(weights_in["ffn1_b2"], 16)
                    for i in range(4 * PAIR + 2):
                        if i < 4 * PAIR:
                            b, m = i // 4, i % 4
                            g = wait_filled(dve, ("up1", b, m))
                            if i >= 4:
                                wait_filled(dve, ("y", 0, i - 4))
                            b1 = cols[:, COLS["ffn1_b1"][0] + 8 * m:COLS["ffn1_b1"][0] + 8 * m + 8]
                            v.tensor_tensor(HX[i % 4], g[:, :].rearrange("p (a s) -> p a s", s=SLOT),
                                            b1.unsqueeze(2).to_broadcast([P, 8, SLOT]), ALU.add)\
                                .then_inc(*emptied(("up1", b, m)))
                        if i >= 2:
                            b, m = (i - 2) // 4, (i - 2) % 4
                            g = wait_filled(dve, ("y", b, m))
                            v.tensor_tensor(YB[b][:, m, :], g[:, 0:C], W["ffn1_b2"][:, m * C:(m + 1) * C], ALU.add)\
                                .then_inc(*emptied(("y", b, m)))
                    measured = []
                    for b in range(PAIR):
                        residual(("comb", b), R[b], X[b])
                        measured.append(measure(R[b]))
                    for b in range(PAIR):
                        normalise(measured[b], Z[b]).then_inc(final_ready, 1)

                @block.gpsimd
                def _(pool):
                    v = nc.gpsimd
                    norms, links = [0], [0]

                    def link(ins):
                        links[0] += 1
                        ins.then_inc(pool_chain, 1)
                        pool.wait_ge(pool_chain, links[0])

                    def inverse_deviation(times=1):
                        for _ in range(times):
                            norms[0] += 1
                            pool.wait_ge(variance_ready, norms[0])
                            k = norms[0] % 2
                            v.tensor_tensor(rstd[:, k, :], variance[:, k, :], const("minus_half"), ALU.pow)\
                                .then_inc(rstd_ready, 1)

                    def plus_row(dst, src, name):
                        return v.tensor_tensor(dst[:, :, :], src[:, :, :],
                                               row(name).unsqueeze(1).to_broadcast([P, TT, C]), ALU.add)

                    pool.wait_ge(consts_in, 16)
                    for b in range(PAIR):
                        v.memset(V0B[b][:, :, C:C + 1], 1.0).then_inc(zeroed, 1)
                    for b in range(PAIR):
                        v.memset(Z[b][0:BUCKET, 0, :], 0.0).then_inc(zeroed, 1)
                    pool.wait_ge(tables_in, 32)

                    def attention(a):
                        at = ATTENTIONS[a]
                        for i in range(STEPS):
                            n = i
                            if i == SUM_AT:
                                inverse_deviation()
                            pool.wait_ge(inverse_ready, n + 1)
                            inv = inverse[:, n % 4, :]
                            for t in range(TT):
                                w = (t + 1) * P
                                p = PB[:, n % RING, :, :].rearrange("p (j t) k -> p j t k", t=TT)[:, :, t, 0:w]
                                m = inv.rearrange("p (j t) -> p j t", t=TT)[:, :, t:t + 1].to_broadcast([P, 2, w])
                                last = v.tensor_tensor(p, p, m, ALU.mult)
                            last.then_inc(probs_ready, 1)

                    def stacked_attention(a):
                        at = ATTENTIONS[a]
                        for g in range(HEAD_STEPS):
                            h = g - SHIFT_LAG
                            if at["kind"] == "keep_later" and 0 <= h < SHEADS:
                                n = head_number(a, h)
                                pool.wait_ge(head_exp, n + 1)
                                if h >= EXPS:
                                    wait_filled(pool, ("O", a, (h - EXPS) // UNIT))
                                v.tensor_tensor(kept[n % EXPS][:, 0, :], exps[:, n % EXPS, 0, 0:P],
                                                const("later_key")[:, 0:P], ALU.mult).then_inc(first_kept, 1)
                            if unit_at(h, CHECK_AT) is not None:
                                u = unit_at(h, CHECK_AT)
                                unit, total, inv = (head_number(a, 0) // UNIT + u, unit_sums[:, u % 2, :],
                                                    unit_inverse[:, u % 2, :])
                                pool.wait_ge(first_inverse, unit + 1)
                                v.tensor_tensor(total, total, inv, ALU.mult).then_inc(inverse_checked, 1)
                            if h == NORM_AT:
                                inverse_deviation()

                    def bias_sums(name, n):
                        pool.wait_ge(u_ready, n)
                        plus_row(BIASED[(n - 1) % PAIR], U[(n - 1) % PAIR], name).then_inc(bias_ready, 1)

                    def mlp_residual(a, b):
                        link(plus_row(U[b], U[b], ("a1_li3_b", "a2_li3_b")[a]))
                        if a == 1:
                            link(v.tensor_tensor(U[b][:, :, :], U[b][:, :, :], X[b][:, :, :], ALU.add))
                        wait_emptied(pool, ("x", a, b))
                        v.tensor_tensor(U[b][:, :, :], U[b][:, :, :], R[b][:, :, :], ALU.add).then_inc(bias_ready, 1)

                    inverse_deviation(2)
                    inverse_deviation(3 * PAIR)
                    for b in range(PAIR):
                        bias_sums("a1_li1_b", b + 1)
                    stacked_attention(0)
                    mlp_residual(0, 0)
                    inverse_deviation()
                    mlp_residual(0, 1)
                    for b in range(PAIR):
                        inverse_deviation(2)
                        bias_sums("a2_li1_b", PAIR + b + 1)
                    stacked_attention(1)
                    mlp_residual(1, 0)
                    inverse_deviation()
                    mlp_residual(1, 1)
                    for b in range(PAIR):
                        inverse_deviation()

                    def zero_other_rows(b):
                        pool.wait_ge(rstd_ready, norms[0])
                        link(v.memset(KC[b][64:P, 0:HEADS:2, :], 0.0))
                        v.memset(KC[b][0:64, 1:HEADS:2, :], 0.0).then_inc(zero_rows, 1)
                        pool.wait_ge(zero_rows, b + 1)

                    zero_other_rows(0)
                    for b in range(PAIR):
                        inverse_deviation()
                    pool.wait_ge(z_ready, 12)
                    zero_other_rows(1)
                    attention(2)
                    pool.wait_ge(z_ready, 13)
                    plus_row(BIASED[0], X[0], "bo").then_inc(bias_ready, 1)
                    inverse_deviation()
                    pool.wait_ge(z_ready, 14)
                    plus_row(BIASED[1], X[1], "bo").then_inc(bias_ready, 1)
                    stacked_attention(3)
                    inverse_deviation()
                    for b in range(PAIR):
                        inverse_deviation()

                @block.sync
                def _(sp):
                    for b in range(PAIR):
                        n = it * PAIR + b
                        sp.dma_start(XN[b][:, :], A["xT"][n]).then_inc(x_in[b], 16)
                        sp.dma_start(X[b][:, :, :], A["x"][n].rearrange("(t p) c -> p t c", p=P)).then_inc(x_in[b], 16)
                        sp.dma_start(CTX[b][:, :, :], A["ctx"][n].rearrange("(t p) c -> p t c", p=P))\
                            .then_inc(x_in[b], 16)
                        sp.dma_start(CTXT[b][CC:P, :], A["ctxT"][n]).then_inc(x_in[b], 16)

                    def stack(a, b, side, u):
                        if u == 0:
                            for m in range(2):
                                wait_emptied(sp, (side, a, b, m))
                        to, parts = {"q": (SQ[b], ("q_hi", "q_hi", "q_lo")),
                                     "k": (SK[b], ("k_hi", "k_lo", "k_hi"))}[side]
                        for n, part in enumerate(parts):
                            sp.dma_start(to[HD * n:HD * n + HD, UNIT * u:UNIT * u + UNIT, :].bitcast(fp32),
                                         halves[part][HD * u:HD * u + HD, :, :]).then_inc(stacked[b][u], 16)
                        if u == 0 and side == "q" and a != 1:
                            r = slice(3 * HD, 3 * HD + UNIT)
                            to = SK[b][r, :, :].bitcast(fp32).rearrange("p (v k) t -> p v (k t)", k=UNIT)
                            ones = choice.bitcast(fp32).rearrange("p k t -> p (k t)")
                            sp.dma_start(to, ones.unsqueeze(1).to_broadcast([UNIT, HEADS // UNIT, UNIT * T]))\
                                .then_inc(choice_in[b], 16)

                    def place_shifts(a, u):
                        b, h0, unit = u // 4, u % 4 * UNIT, head_number(a, 0) // UNIT + u
                        wait_emptied(sp, ("M", a, u))
                        rows = shift_rows[0:UNIT, u % 4, :].bitcast(fp32)
                        sp.dma_start(SQ[b][3 * HD:3 * HD + UNIT, h0:h0 + UNIT, :].bitcast(fp32),
                                     rows.unsqueeze(1).to_broadcast([UNIT, UNIT, T])).then_inc(shifts_in[unit % 4], 16)

                    def stacked_attention(a):
                        for u in range(HEADS // UNIT):
                            stack(a, 0, "k", u)
                            stack(a, 0, "q", u)
                        second = {u: [("k", u), ("q", u)] for u in range(HEADS // UNIT)}
                        for u in range(SHEADS // UNIT):
                            place_shifts(a, u)
                            for side, part in second.get(u, ()):
                                stack(a, 1, side, part)

                    def load_experts(f, scores):
                        scores()
                        for g in range(PARTS_OF_EXPERTS):
                            for n in (f"ffn{f}_w1", f"ffn{f}_w2"):
                                w = EXPERT_WEIGHTS[n][1] // PARTS_OF_EXPERTS
                                sp.dma_start(W[n][:, g * w:(g + 1) * w], A[n][:, g * w:(g + 1) * w])\
                                    .then_inc(experts_in[f][g], 16)

                    sp.wait_ge(masks_made, 3)
                    stacked_attention(0)
                    stacked_attention(1)
                    load_experts(0, lambda: sp.wait_ge(head_scores, 2 * SHEADS))
                    stacked_attention(3)
                    load_experts(1, lambda: sp.wait_ge(head_scores, 3 * SHEADS))
                    for b in range(PAIR):
                        sp.wait_ge(final_ready, b + 1)
                        sp.dma_start(out[it * PAIR + b].rearrange("(t p) c -> p t c", p=P), Z[b][:, :, :])\
                            .then_inc(out_stored, 16)
                    sp.wait_ge(out_stored, 16 * PAIR)

            numbers = sorted(s.num for s in per_pass)
            nc.sync.sem_clear(range(numbers[0], numbers[-1] + 1))
            nc.all_engine_barrier()


def arranged(x, ctx_512, **w):
    def heads_in(a):
        return a.transpose(1, 0, 2).reshape(a.shape[1], -1)

    def tiles(a):
        return a.reshape(-1, P, a.shape[-1]).transpose(1, 0, 2).reshape(P, -1)

    def padded(a):
        out = np.zeros((*a.shape[:-1], HEADS, 32), a.dtype)
        out[..., :HD0] = a.reshape(*a.shape[:-1], HEADS, HD0)
        return out.reshape(*a.shape[:-1], -1)

    def by_unit(a):
        return a.reshape(*a.shape[:-1], 4, 4, 32).swapaxes(-3, -2).reshape(a.shape)

    x0 = "L0_xattn_"
    A = {"x": x, "xT": x.transpose(0, 2, 1), "ctx": ctx_512, "ctxT": ctx_512.transpose(0, 2, 1),
         "qkv": w["L0_attn_W_qkv"].T, "wout": w["L0_attn_W_out"].T}
    for a in ("a1", "a2"):
        for k in ("wq", "wk", "wv") if a == "a1" else ("wq",):
            A[f"{a}_{k}"] = heads_in(w[f"{x0}{a}_{k}"])
            if k != "wv":
                A[f"{a}_{k}"] = by_unit(A[f"{a}_{k}"])
        A[a + "_li1"], A[a + "_li2"], A[a + "_li3"] = (tiles(w[x0 + a + "_li1_w"]), w[x0 + a + "_li2_w"],
                                                      tiles(w[x0 + a + "_li3_w"]))
    A["router"], A["ffn0_b2"] = w["L0_ffn_router_w"], w["L0_ffn_b2"]
    A["ffn0_w1"] = heads_in(w["L0_ffn_w1"])
    A["ffn0_w2"] = tiles(w["L0_ffn_w2"].reshape(-1, C))
    for k, n in (("wq", "W_Q"), ("wk", "W_K"), ("wv", "W_V")):
        A["l1_" + k] = w["L1_attn_" + n].reshape(-1, C).T
    A["l1_wo"] = tiles(w["L1_attn_W_O"].T)
    A["lx_wq"] = by_unit(padded(w["L1_xattn_Wq"]))
    for k in ("k", "v"):
        A["ctx_w" + k] = np.concatenate([heads_in(w[f"{x0}a2_w{k}"]), padded(w["L1_xattn_W" + k])])
    A["ctx_wk"] = by_unit(A["ctx_wk"])
    A["lx_wo"] = tiles(padded(w["L1_xattn_Wo"].T).T)
    A["router1"] = w["L1_ffn_Wr"]
    A["ffn1_w1"] = heads_in(w["L1_ffn_W1"])
    A["ffn1_w2"] = tiles(w["L1_ffn_W2"].reshape(-1, C))
    A["ffn1_b2"] = tiles(np.repeat(w["L1_ffn_b2"], SLOT, axis=0))
    rows = {"bo": w["L1_xattn_bo"], "router_b": w["L0_ffn_router_b"], "bv": padded(w["L1_xattn_bv"])}
    A["rows"] = np.concatenate([rows[n] if n in rows else w[x0 + n] for n in ROWS])
    columns = {"ffn0_b1": w["L0_ffn_b1"], "ffn1_b1": w["L1_ffn_b1"], "bq": by_unit(padded(w["L1_xattn_bq"])),
               "bk": by_unit(padded(w["L1_xattn_bk"]))}
    packed = np.zeros((P, NCOLS), x.dtype)
    for n, (at, width) in COLS.items():
        v = (columns[n] if n in columns else w[x0 + n]).reshape(width, -1)
        packed[:v.shape[1], at:at + width] = v.T
    A["cols"] = packed
    A["consts"] = shape_constants()
    return {n: np.ascontiguousarray(a) for n, a in A.items()}


def kernel(**inputs):
    import concourse.bacc as _bacc
    from concourse.bass_utils import run_bass_kernel_spmd as _run

    arrays = arranged(**{n: np.asarray(a) for n, a in inputs.items()})
    nc = _bacc.Bacc("TRN2", target_bir_lowering=False, num_devices=1)
    A = {n: nc.dram_tensor("in_" + n, a.shape, mybir.dt.from_np(a.dtype), kind="ExternalInput").ap()
         for n, a in arrays.items()}
    out = nc.dram_tensor("out", (BATCHES, T, C), fp32, kind="ExternalOutput").ap()
    decoder(nc, A, out)
    r = _run(nc, [{"in_" + n: a for n, a in arrays.items()}], core_ids=[0])
    return r.results[0]["out"]
```
